# Optimizing a Trainium2 kernel written in Bass

```python
import numpy as np
import jax
import jax.numpy as jnp

def _softmax(x, axis=-1):
    return jax.nn.softmax(x, axis=axis)

def _gelu(x):
    return jax.nn.gelu(x, approximate=True)

def _silu(x):
    return jax.nn.silu(x)

def _sigmoid(x):
    return jax.nn.sigmoid(x)

def _layernorm(x, axis=-1, eps=1e-05):
    m = jnp.mean(x, axis=axis, keepdims=True)
    v = jnp.var(x, axis=axis, keepdims=True)
    return (x - m) / jnp.sqrt(v + eps)

def _scatter_add(tgt, idx, src, axis=0):
    return tgt.at[idx].add(src)

def _segment_sum(src, seg, n):
    return jax.ops.segment_sum(src, seg, n)
kernel_name = 'mk_seq_postln_d2_jaxref_r4_9a4b2d'

def setup_inputs(seed: int=0):
    np.random.seed(seed)
    _w = jnp.asarray

    def _L0_attn_setup():
        import jax, jax.numpy as jnp
        import numpy as np
        from jax import lax
        D_MODEL = 256
        D_INNER = 2 * D_MODEL
        D_STATE = 16
        D_CONV = 4
        DT_RANK = (D_MODEL + 15) // 16
        B, L = (4, 512)
        EPS = 1e-06

        def _rmsnorm(h, w):
            var = jnp.mean(h.astype(jnp.float32) ** 2, axis=-1, keepdims=True)
            return (w * (h * lax.rsqrt(var + EPS))).astype(h.dtype)

        def _mamba(x, in_proj_w, conv_w, conv_b, x_proj_w, dt_proj_w, dt_proj_b, A_log, D_skip, out_proj_w):
            xz = jnp.einsum('bld,ed->ble', x, in_proj_w)
            u, z = jnp.split(xz, 2, axis=-1)
            u_t = jnp.transpose(u, (0, 2, 1))
            conv = lax.conv_general_dilated(u_t, conv_w[:, None, :], (1,), [(D_CONV - 1, 0)], dimension_numbers=('NCH', 'OIH', 'NCH'), feature_group_count=D_INNER)
            u = jax.nn.silu(jnp.transpose(conv + conv_b[None, :, None], (0, 2, 1)))
            dbc = jnp.einsum('bld,ed->ble', u, x_proj_w)
            dt, Bm, Cm = jnp.split(dbc, [DT_RANK, DT_RANK + D_STATE], axis=-1)
            dt = jax.nn.softplus(jnp.einsum('blr,dr->bld', dt, dt_proj_w) + dt_proj_b)
            A = -jnp.exp(A_log)

            def step(s, inp):
                d, u_i, b_i, c_i = inp
                s = s * jnp.exp(d[..., None] * A) + (d * u_i)[..., None] * b_i[:, None, :]
                y = jnp.einsum('bdn,bn->bd', s, c_i)
                return (s, y)
            s0 = jnp.zeros((u.shape[0], D_INNER, D_STATE), u.dtype)
            inputs = (jnp.moveaxis(dt, 1, 0), jnp.moveaxis(u, 1, 0), jnp.moveaxis(Bm, 1, 0), jnp.moveaxis(Cm, 1, 0))
            _, ys = lax.scan(step, s0, inputs)
            y = jnp.moveaxis(ys, 0, 1) + u * D_skip
            y = y * jax.nn.silu(z)
            return jnp.einsum('ble,de->bld', y, out_proj_w)

        def _mlp(x, fc1_w, fc1_b, fc2_w, fc2_b, fc3_w, fc3_b):
            h = jax.nn.relu(jnp.einsum('bld,hd->blh', x, fc1_w) + fc1_b)
            h = jax.nn.relu(jnp.einsum('blh,gh->blg', h, fc2_w) + fc2_b)
            return jnp.einsum('blg,dg->bld', h, fc3_w) + fc3_b
        key = jax.random.key(seed)
        ks = jax.random.split(key, 16)
        g = lambda k, shape, s=0.02: jax.random.normal(k, shape, jnp.float32) * s
        A_init = jnp.broadcast_to(jnp.arange(1, D_STATE + 1, dtype=jnp.float32), (D_INNER, D_STATE))
        return {'x': jax.random.normal(ks[0], (B, L, D_MODEL), jnp.float32), 'rms1_w': jnp.ones((D_MODEL,), jnp.float32), 'rms2_w': jnp.ones((D_MODEL,), jnp.float32), 'in_proj_w': g(ks[1], (2 * D_INNER, D_MODEL)), 'conv_w': g(ks[2], (D_INNER, D_CONV), 0.1), 'conv_b': jnp.zeros((D_INNER,), jnp.float32), 'x_proj_w': g(ks[3], (DT_RANK + 2 * D_STATE, D_INNER)), 'dt_proj_w': g(ks[4], (D_INNER, DT_RANK), 0.1), 'dt_proj_b': jnp.full((D_INNER,), -4.0, jnp.float32), 'A_log': jnp.log(A_init), 'D_skip': jnp.ones((D_INNER,), jnp.float32), 'out_proj_w': g(ks[5], (D_MODEL, D_INNER)), 'fc1_w': g(ks[6], (2 * D_MODEL, D_MODEL)), 'fc1_b': jnp.zeros((2 * D_MODEL,), jnp.float32), 'fc2_w': g(ks[7], (2 * D_MODEL, 2 * D_MODEL)), 'fc2_b': jnp.zeros((2 * D_MODEL,), jnp.float32), 'fc3_w': g(ks[8], (D_MODEL, 2 * D_MODEL)), 'fc3_b': jnp.zeros((D_MODEL,), jnp.float32)}
    _L0_attn_in = _L0_attn_setup()

    def _L0_ffn_setup():
        import jax, jax.numpy as jnp
        import numpy as np
        B, S, D = (2, 256, 256)
        E, K, F, FS = (8, 2, 128, 256)
        key = jax.random.key(seed)
        ks = jax.random.split(key, 9)
        s = lambda k, shape, fan: jax.random.normal(k, shape, jnp.float32) * fan ** (-0.5)
        return {'x': jax.random.normal(ks[0], (B, S, D), jnp.float32), 'Wr': s(ks[1], (D, E), D), 'Wg': s(ks[2], (E, D, F), D), 'Wu': s(ks[3], (E, D, F), D), 'Wd': s(ks[4], (E, F, D), F), 'Sg': s(ks[5], (D, FS), D), 'Su': s(ks[6], (D, FS), D), 'Sd': s(ks[7], (FS, D), FS), 'expert_bias': jnp.zeros((E,), jnp.float32)}
    _L0_ffn_in = _L0_ffn_setup()

    def _L1_attn_setup():
        import jax, jax.numpy as jnp
        import numpy as np
        D_MODEL = 256
        NHEAD = 16
        HEAD_DIM = D_MODEL // NHEAD
        WINDOW = 128
        BATCH = 2
        SEQ = 1024

        def _sliding_window_attention(q, k, v, window):
            B, H, S, D = q.shape
            W = window
            nc = S // W
            qc = q.reshape(B, H, nc, W, D)
            kb = k.reshape(B, H, nc, W, D)
            vb = v.reshape(B, H, nc, W, D)
            kprev = jnp.pad(kb, ((0, 0), (0, 0), (1, 0), (0, 0), (0, 0)))[:, :, :-1]
            vprev = jnp.pad(vb, ((0, 0), (0, 0), (1, 0), (0, 0), (0, 0)))[:, :, :-1]
            k2 = jnp.concatenate([kprev, kb], axis=3)
            v2 = jnp.concatenate([vprev, vb], axis=3)
            scores = jnp.einsum('bhcid,bhcjd->bhcij', qc, k2) / jnp.sqrt(jnp.asarray(D, dtype=q.dtype))
            i = jnp.arange(W)[:, None]
            j = jnp.arange(2 * W)[None, :]
            band = (j >= i + 1) & (j <= i + W)
            c = jnp.arange(nc)[:, None, None]
            valid = band[None] & ((c > 0) | (j[None] >= W))
            neg_inf = jnp.asarray(-jnp.inf, dtype=scores.dtype)
            scores = jnp.where(valid[None, None], scores, neg_inf)
            attn = jax.nn.softmax(scores, axis=-1)
            out = jnp.einsum('bhcij,bhcjd->bhcid', attn, v2)
            return out.reshape(B, H, S, D)
        key = jax.random.key(seed)
        kx, kq, kk, kv, ko = jax.random.split(key, 5)
        scale = 0.02
        return {'x': jax.random.normal(kx, (BATCH, SEQ, D_MODEL), dtype=jnp.float32), 'Wq': jax.random.normal(kq, (D_MODEL, D_MODEL), dtype=jnp.float32) * scale, 'Wk': jax.random.normal(kk, (D_MODEL, D_MODEL), dtype=jnp.float32) * scale, 'Wv': jax.random.normal(kv, (D_MODEL, D_MODEL), dtype=jnp.float32) * scale, 'Wo': jax.random.normal(ko, (D_MODEL, D_MODEL), dtype=jnp.float32) * scale}
    _L1_attn_in = _L1_attn_setup()

    def _L1_ffn_setup():
        import jax, jax.numpy as jnp
        import numpy as np
        DIM = 256
        HEADS = 8
        DH = 64
        HDH = HEADS * DH
        SEQ = 2048
        BATCH = 2
        WIN = 64
        N_ITERS = 50
        EPS = 1.0
        NQ = 256
        NKV = 512
        FETCH_K = 9.0 / 8.0

        def rmsnorm(x, g):
            n = jnp.maximum(jnp.sqrt(jnp.sum(x * x, axis=-1, keepdims=True)), 1e-12)
            return x / n * DIM ** 0.5 * g

        def layernorm(x, g, b):
            m = jnp.mean(x, axis=-1, keepdims=True)
            v = jnp.mean((x - m) ** 2, axis=-1, keepdims=True)
            return (x - m) / jnp.sqrt(v + 1e-05) * g + b

        def coor_descent(s, k_eff):
            logk = jnp.log(jnp.float32(k_eff))

            def body(carry, _):
                a, b = carry
                sb = (s + b) / EPS
                a = EPS * (logk - jax.nn.logsumexp(sb, axis=-1, keepdims=True))
                b = -jax.nn.relu(s + a)
                return ((a, b), None)
            init = (jnp.zeros_like(s[..., :1]), -s)
            (a, b), _ = jax.lax.scan(body, init, None, length=N_ITERS)
            return jnp.exp((s + a + b) / EPS)

        def route(x, routing_token, num_tokens, k_eff):
            s = jnp.einsum('bnd,rd->brn', x, routing_token)[:, 0]
            scores = coor_descent(s, k_eff)
            sel_scores, sel_idx = jax.lax.top_k(scores, num_tokens)
            sel_scores = sel_scores + jax.lax.stop_gradient(1.0 - sel_scores)
            return (sel_scores, sel_idx)

        def light_attn(x, ln_g, ln_b, w_qkv, w_out):
            b, n, _ = x.shape
            xn = layernorm(x, ln_g, ln_b)
            q, k, v = jnp.split(xn @ w_qkv, 3, axis=-1)

            def towin(t):
                return t.reshape(b, n // WIN, WIN, HEADS, DH).transpose(0, 3, 1, 2, 4)
            q, k, v = (towin(q), towin(k), towin(v))

            def around(t):
                pad = jnp.pad(t, ((0, 0), (0, 0), (1, 1), (0, 0), (0, 0)))
                return jnp.concatenate([pad[:, :, :-2], pad[:, :, 1:-1], pad[:, :, 2:]], axis=3)
            kk, vv = (around(k), around(v))
            nw = n // WIN
            wvalid = jnp.pad(jnp.ones((nw,), bool), (1, 1))
            kmask = jnp.concatenate([jnp.repeat(wvalid[:-2, None], WIN, 1), jnp.repeat(wvalid[1:-1, None], WIN, 1), jnp.repeat(wvalid[2:, None], WIN, 1)], axis=1)
            sim = jnp.einsum('bhnwd,bhnWd->bhnwW', q * DH ** (-0.5), kk)
            sim = jnp.where(kmask[None, None, :, None, :], sim, -jnp.finfo(sim.dtype).max)
            attn = jax.nn.softmax(sim, axis=-1)
            o = jnp.einsum('bhnwW,bhnWd->bhnwd', attn, vv)
            o = o.transpose(0, 2, 3, 1, 4).reshape(b, n, HDH)
            return o @ w_out

        def heavy_attn(xq, ctx, scores_kv, rms_g, w_q, w_kv, null_kv, w_out):
            b = xq.shape[0]
            xq = rmsnorm(xq, rms_g)
            ctx = rmsnorm(ctx, rms_g)
            q = (xq @ w_q).reshape(b, -1, HEADS, DH).transpose(0, 2, 1, 3)
            kv = jnp.einsum('bni,ihd->bhnd', ctx, w_kv)
            k, v = (kv[..., :DH], kv[..., DH:])
            v = v * scores_kv[:, None, :, None]
            nk = jnp.broadcast_to(null_kv[0][None, :, None, :], (b, HEADS, 1, DH))
            nv = jnp.broadcast_to(null_kv[1][None, :, None, :], (b, HEADS, 1, DH))
            k = jnp.concatenate([nk, k], axis=2)
            v = jnp.concatenate([nv, v], axis=2)
            sim = jnp.einsum('bhqd,bhkd->bhqk', q * DH ** (-0.5), k)
            attn = jax.nn.softmax(sim, axis=-1)
            o = jnp.einsum('bhqk,bhkd->bhqd', attn, v)
            o = o.transpose(0, 2, 1, 3).reshape(b, -1, HDH)
            return o @ w_out

        def forward(x, ln_g, ln_b, w_qkv_l, w_out_l, null_q, rt_q, rt_kv, rms_g, w_q_h, w_kv_h, null_kv, w_out_h):
            light = light_attn(x, ln_g, ln_b, w_qkv_l, w_out_l)
            sq, iq = route(x, rt_q, NQ, min(NQ * FETCH_K, SEQ))
            skv, ikv = route(x, rt_kv, NKV, min(NKV * FETCH_K, SEQ))
            batch_idx = jnp.arange(x.shape[0])[:, None]
            xq = x[batch_idx, iq]
            xkv = x[batch_idx, ikv]
            routed_out = heavy_attn(xq, xkv, skv, rms_g, w_q_h, w_kv_h, null_kv, w_out_h)
            routed_out = routed_out * sq[..., None]
            out = jnp.broadcast_to(null_q, x.shape)
            out = out.at[batch_idx, iq].set(routed_out)
            return light + out
        key = jax.random.key(seed)
        ks = jax.random.split(key, 10)
        p = lambda i, shape: jax.random.normal(ks[i], shape, jnp.float32) * 0.02
        return dict(x=jax.random.normal(ks[0], (BATCH, SEQ, DIM), jnp.float32), ln_g=jnp.ones((DIM,), jnp.float32), ln_b=jnp.zeros((DIM,), jnp.float32), w_qkv_l=p(1, (DIM, 3 * HDH)), w_out_l=p(2, (HDH, DIM)), null_q=jax.random.normal(ks[3], (DIM,), jnp.float32), rt_q=jax.random.normal(ks[4], (1, DIM), jnp.float32), rt_kv=jax.random.normal(ks[5], (1, DIM), jnp.float32), rms_g=jnp.ones((DIM,), jnp.float32), w_q_h=p(6, (DIM, HDH)), w_kv_h=p(7, (DIM, HEADS, 2 * DH)), null_kv=jax.random.normal(ks[8], (2, HEADS, DH), jnp.float32), w_out_h=p(9, (HDH, DIM)))
    _L1_ffn_in = _L1_ffn_setup()
    _d = {'L0_attn_x': _L0_attn_in['x'], 'L0_attn_rms1_w': _L0_attn_in['rms1_w'], 'L0_attn_rms2_w': _L0_attn_in['rms2_w'], 'L0_attn_in_proj_w': _L0_attn_in['in_proj_w'], 'L0_attn_conv_w': _L0_attn_in['conv_w'], 'L0_attn_conv_b': _L0_attn_in['conv_b'], 'L0_attn_x_proj_w': _L0_attn_in['x_proj_w'], 'L0_attn_dt_proj_w': _L0_attn_in['dt_proj_w'], 'L0_attn_dt_proj_b': _L0_attn_in['dt_proj_b'], 'L0_attn_A_log': _L0_attn_in['A_log'], 'L0_attn_D_skip': _L0_attn_in['D_skip'], 'L0_attn_out_proj_w': _L0_attn_in['out_proj_w'], 'L0_attn_fc1_w': _L0_attn_in['fc1_w'], 'L0_attn_fc1_b': _L0_attn_in['fc1_b'], 'L0_attn_fc2_w': _L0_attn_in['fc2_w'], 'L0_attn_fc2_b': _L0_attn_in['fc2_b'], 'L0_attn_fc3_w': _L0_attn_in['fc3_w'], 'L0_attn_fc3_b': _L0_attn_in['fc3_b'], 'L0_ffn_Wr': _L0_ffn_in['Wr'], 'L0_ffn_Wg': _L0_ffn_in['Wg'], 'L0_ffn_Wu': _L0_ffn_in['Wu'], 'L0_ffn_Wd': _L0_ffn_in['Wd'], 'L0_ffn_Sg': _L0_ffn_in['Sg'], 'L0_ffn_Su': _L0_ffn_in['Su'], 'L0_ffn_Sd': _L0_ffn_in['Sd'], 'L0_ffn_expert_bias': _L0_ffn_in['expert_bias'], 'L1_attn_Wq': _L1_attn_in['Wq'], 'L1_attn_Wk': _L1_attn_in['Wk'], 'L1_attn_Wv': _L1_attn_in['Wv'], 'L1_attn_Wo': _L1_attn_in['Wo'], 'L1_ffn_ln_g': _L1_ffn_in['ln_g'], 'L1_ffn_ln_b': _L1_ffn_in['ln_b'], 'L1_ffn_w_qkv_l': _L1_ffn_in['w_qkv_l'], 'L1_ffn_w_out_l': _L1_ffn_in['w_out_l'], 'L1_ffn_null_q': _L1_ffn_in['null_q'], 'L1_ffn_rt_q': _L1_ffn_in['rt_q'], 'L1_ffn_rt_kv': _L1_ffn_in['rt_kv'], 'L1_ffn_rms_g': _L1_ffn_in['rms_g'], 'L1_ffn_w_q_h': _L1_ffn_in['w_q_h'], 'L1_ffn_w_kv_h': _L1_ffn_in['w_kv_h'], 'L1_ffn_null_kv': _L1_ffn_in['null_kv'], 'L1_ffn_w_out_h': _L1_ffn_in['w_out_h']}
    _x0 = _d['L0_attn_x']
    _d['L0_attn_x'] = jax.random.normal(jax.random.fold_in(jax.random.key(seed), 1), (2, 2048, 256), dtype=_x0.dtype)
    del _x0
    return _d

def reference(L0_attn_x, L0_attn_rms1_w, L0_attn_rms2_w, L0_attn_in_proj_w, L0_attn_conv_w, L0_attn_conv_b, L0_attn_x_proj_w, L0_attn_dt_proj_w, L0_attn_dt_proj_b, L0_attn_A_log, L0_attn_D_skip, L0_attn_out_proj_w, L0_attn_fc1_w, L0_attn_fc1_b, L0_attn_fc2_w, L0_attn_fc2_b, L0_attn_fc3_w, L0_attn_fc3_b, L0_ffn_Wr, L0_ffn_Wg, L0_ffn_Wu, L0_ffn_Wd, L0_ffn_Sg, L0_ffn_Su, L0_ffn_Sd, L0_ffn_expert_bias, L1_attn_Wq, L1_attn_Wk, L1_attn_Wv, L1_attn_Wo, L1_ffn_ln_g, L1_ffn_ln_b, L1_ffn_w_qkv_l, L1_ffn_w_out_l, L1_ffn_null_q, L1_ffn_rt_q, L1_ffn_rt_kv, L1_ffn_rms_g, L1_ffn_w_q_h, L1_ffn_w_kv_h, L1_ffn_null_kv, L1_ffn_w_out_h):

    def _L0_attn_ref(x, rms1_w, rms2_w, in_proj_w, conv_w, conv_b, x_proj_w, dt_proj_w, dt_proj_b, A_log, D_skip, out_proj_w, fc1_w, fc1_b, fc2_w, fc2_b, fc3_w, fc3_b):
        import jax, jax.numpy as jnp
        import numpy as np
        from jax import lax
        D_MODEL = 256
        D_INNER = 2 * D_MODEL
        D_STATE = 16
        D_CONV = 4
        DT_RANK = (D_MODEL + 15) // 16
        B, L = (4, 512)
        EPS = 1e-06

        def _rmsnorm(h, w):
            var = jnp.mean(h.astype(jnp.float32) ** 2, axis=-1, keepdims=True)
            return (w * (h * lax.rsqrt(var + EPS))).astype(h.dtype)

        def _mamba(x, in_proj_w, conv_w, conv_b, x_proj_w, dt_proj_w, dt_proj_b, A_log, D_skip, out_proj_w):
            xz = jnp.einsum('bld,ed->ble', x, in_proj_w)
            u, z = jnp.split(xz, 2, axis=-1)
            u_t = jnp.transpose(u, (0, 2, 1))
            conv = lax.conv_general_dilated(u_t, conv_w[:, None, :], (1,), [(D_CONV - 1, 0)], dimension_numbers=('NCH', 'OIH', 'NCH'), feature_group_count=D_INNER)
            u = jax.nn.silu(jnp.transpose(conv + conv_b[None, :, None], (0, 2, 1)))
            dbc = jnp.einsum('bld,ed->ble', u, x_proj_w)
            dt, Bm, Cm = jnp.split(dbc, [DT_RANK, DT_RANK + D_STATE], axis=-1)
            dt = jax.nn.softplus(jnp.einsum('blr,dr->bld', dt, dt_proj_w) + dt_proj_b)
            A = -jnp.exp(A_log)

            def step(s, inp):
                d, u_i, b_i, c_i = inp
                s = s * jnp.exp(d[..., None] * A) + (d * u_i)[..., None] * b_i[:, None, :]
                y = jnp.einsum('bdn,bn->bd', s, c_i)
                return (s, y)
            s0 = jnp.zeros((u.shape[0], D_INNER, D_STATE), u.dtype)
            inputs = (jnp.moveaxis(dt, 1, 0), jnp.moveaxis(u, 1, 0), jnp.moveaxis(Bm, 1, 0), jnp.moveaxis(Cm, 1, 0))
            _, ys = lax.scan(step, s0, inputs)
            y = jnp.moveaxis(ys, 0, 1) + u * D_skip
            y = y * jax.nn.silu(z)
            return jnp.einsum('ble,de->bld', y, out_proj_w)

        def _mlp(x, fc1_w, fc1_b, fc2_w, fc2_b, fc3_w, fc3_b):
            h = jax.nn.relu(jnp.einsum('bld,hd->blh', x, fc1_w) + fc1_b)
            h = jax.nn.relu(jnp.einsum('blh,gh->blg', h, fc2_w) + fc2_b)
            return jnp.einsum('blg,dg->bld', h, fc3_w) + fc3_b
        x0 = _rmsnorm(x, rms1_w)
        x1 = _mamba(x0, in_proj_w, conv_w, conv_b, x_proj_w, dt_proj_w, dt_proj_b, A_log, D_skip, out_proj_w)
        x = x1 + x
        x2 = _rmsnorm(x, rms2_w)
        x3 = _mlp(x2, fc1_w, fc1_b, fc2_w, fc2_b, fc3_w, fc3_b)
        return x + x3

    def _L0_ffn_ref(x, Wr, Wg, Wu, Wd, Sg, Su, Sd, expert_bias):
        import jax, jax.numpy as jnp
        import numpy as np
        B, S, D = (2, 256, 256)
        E, K, F, FS = (8, 2, 128, 256)
        b, s, d = x.shape
        xf = x.reshape(-1, d)
        T = xf.shape[0]
        logits = xf @ Wr + expert_bias
        top_v, top_i = jax.lax.top_k(logits, K)
        probs = jax.nn.softmax(top_v, axis=-1)
        rw = jnp.zeros_like(logits).at[jnp.arange(T)[:, None], top_i].set(probs)
        gate = jnp.einsum('td,edf->tef', xf, Wg)
        up = jnp.einsum('td,edf->tef', xf, Wu)
        h = jax.nn.silu(gate) * up
        eo = jnp.einsum('tef,efd->ted', h, Wd)
        out = jnp.einsum('te,ted->td', rw, eo)
        out = out + jax.nn.silu(xf @ Sg) * (xf @ Su) @ Sd
        return out.reshape(b, s, d)

    def _L1_attn_ref(x, Wq, Wk, Wv, Wo):
        import jax, jax.numpy as jnp
        import numpy as np
        D_MODEL = 256
        NHEAD = 16
        HEAD_DIM = D_MODEL // NHEAD
        WINDOW = 128
        BATCH = 2
        SEQ = 1024

        def _sliding_window_attention(q, k, v, window):
            B, H, S, D = q.shape
            W = window
            nc = S // W
            qc = q.reshape(B, H, nc, W, D)
            kb = k.reshape(B, H, nc, W, D)
            vb = v.reshape(B, H, nc, W, D)
            kprev = jnp.pad(kb, ((0, 0), (0, 0), (1, 0), (0, 0), (0, 0)))[:, :, :-1]
            vprev = jnp.pad(vb, ((0, 0), (0, 0), (1, 0), (0, 0), (0, 0)))[:, :, :-1]
            k2 = jnp.concatenate([kprev, kb], axis=3)
            v2 = jnp.concatenate([vprev, vb], axis=3)
            scores = jnp.einsum('bhcid,bhcjd->bhcij', qc, k2) / jnp.sqrt(jnp.asarray(D, dtype=q.dtype))
            i = jnp.arange(W)[:, None]
            j = jnp.arange(2 * W)[None, :]
            band = (j >= i + 1) & (j <= i + W)
            c = jnp.arange(nc)[:, None, None]
            valid = band[None] & ((c > 0) | (j[None] >= W))
            neg_inf = jnp.asarray(-jnp.inf, dtype=scores.dtype)
            scores = jnp.where(valid[None, None], scores, neg_inf)
            attn = jax.nn.softmax(scores, axis=-1)
            out = jnp.einsum('bhcij,bhcjd->bhcid', attn, v2)
            return out.reshape(B, H, S, D)
        B, S, E = x.shape
        q = (x @ Wq.T).reshape(B, S, NHEAD, HEAD_DIM).transpose(0, 2, 1, 3)
        k = (x @ Wk.T).reshape(B, S, NHEAD, HEAD_DIM).transpose(0, 2, 1, 3)
        v = (x @ Wv.T).reshape(B, S, NHEAD, HEAD_DIM).transpose(0, 2, 1, 3)
        attn_out = _sliding_window_attention(q, k, v, WINDOW)
        attn_out = attn_out.transpose(0, 2, 1, 3).reshape(B, S, E)
        return attn_out @ Wo.T

    def _L1_ffn_ref(x, ln_g, ln_b, w_qkv_l, w_out_l, null_q, rt_q, rt_kv, rms_g, w_q_h, w_kv_h, null_kv, w_out_h):
        import jax, jax.numpy as jnp
        import numpy as np
        DIM = 256
        HEADS = 8
        DH = 64
        HDH = HEADS * DH
        SEQ = 2048
        BATCH = 2
        WIN = 64
        N_ITERS = 50
        EPS = 1.0
        NQ = 256
        NKV = 512
        FETCH_K = 9.0 / 8.0

        def rmsnorm(x, g):
            n = jnp.maximum(jnp.sqrt(jnp.sum(x * x, axis=-1, keepdims=True)), 1e-12)
            return x / n * DIM ** 0.5 * g

        def layernorm(x, g, b):
            m = jnp.mean(x, axis=-1, keepdims=True)
            v = jnp.mean((x - m) ** 2, axis=-1, keepdims=True)
            return (x - m) / jnp.sqrt(v + 1e-05) * g + b

        def coor_descent(s, k_eff):
            logk = jnp.log(jnp.float32(k_eff))

            def body(carry, _):
                a, b = carry
                sb = (s + b) / EPS
                a = EPS * (logk - jax.nn.logsumexp(sb, axis=-1, keepdims=True))
                b = -jax.nn.relu(s + a)
                return ((a, b), None)
            init = (jnp.zeros_like(s[..., :1]), -s)
            (a, b), _ = jax.lax.scan(body, init, None, length=N_ITERS)
            return jnp.exp((s + a + b) / EPS)

        def route(x, routing_token, num_tokens, k_eff):
            s = jnp.einsum('bnd,rd->brn', x, routing_token)[:, 0]
            scores = coor_descent(s, k_eff)
            sel_scores, sel_idx = jax.lax.top_k(scores, num_tokens)
            sel_scores = sel_scores + jax.lax.stop_gradient(1.0 - sel_scores)
            return (sel_scores, sel_idx)

        def light_attn(x, ln_g, ln_b, w_qkv, w_out):
            b, n, _ = x.shape
            xn = layernorm(x, ln_g, ln_b)
            q, k, v = jnp.split(xn @ w_qkv, 3, axis=-1)

            def towin(t):
                return t.reshape(b, n // WIN, WIN, HEADS, DH).transpose(0, 3, 1, 2, 4)
            q, k, v = (towin(q), towin(k), towin(v))

            def around(t):
                pad = jnp.pad(t, ((0, 0), (0, 0), (1, 1), (0, 0), (0, 0)))
                return jnp.concatenate([pad[:, :, :-2], pad[:, :, 1:-1], pad[:, :, 2:]], axis=3)
            kk, vv = (around(k), around(v))
            nw = n // WIN
            wvalid = jnp.pad(jnp.ones((nw,), bool), (1, 1))
            kmask = jnp.concatenate([jnp.repeat(wvalid[:-2, None], WIN, 1), jnp.repeat(wvalid[1:-1, None], WIN, 1), jnp.repeat(wvalid[2:, None], WIN, 1)], axis=1)
            sim = jnp.einsum('bhnwd,bhnWd->bhnwW', q * DH ** (-0.5), kk)
            sim = jnp.where(kmask[None, None, :, None, :], sim, -jnp.finfo(sim.dtype).max)
            attn = jax.nn.softmax(sim, axis=-1)
            o = jnp.einsum('bhnwW,bhnWd->bhnwd', attn, vv)
            o = o.transpose(0, 2, 3, 1, 4).reshape(b, n, HDH)
            return o @ w_out

        def heavy_attn(xq, ctx, scores_kv, rms_g, w_q, w_kv, null_kv, w_out):
            b = xq.shape[0]
            xq = rmsnorm(xq, rms_g)
            ctx = rmsnorm(ctx, rms_g)
            q = (xq @ w_q).reshape(b, -1, HEADS, DH).transpose(0, 2, 1, 3)
            kv = jnp.einsum('bni,ihd->bhnd', ctx, w_kv)
            k, v = (kv[..., :DH], kv[..., DH:])
            v = v * scores_kv[:, None, :, None]
            nk = jnp.broadcast_to(null_kv[0][None, :, None, :], (b, HEADS, 1, DH))
            nv = jnp.broadcast_to(null_kv[1][None, :, None, :], (b, HEADS, 1, DH))
            k = jnp.concatenate([nk, k], axis=2)
            v = jnp.concatenate([nv, v], axis=2)
            sim = jnp.einsum('bhqd,bhkd->bhqk', q * DH ** (-0.5), k)
            attn = jax.nn.softmax(sim, axis=-1)
            o = jnp.einsum('bhqk,bhkd->bhqd', attn, v)
            o = o.transpose(0, 2, 1, 3).reshape(b, -1, HDH)
            return o @ w_out

        def forward(x, ln_g, ln_b, w_qkv_l, w_out_l, null_q, rt_q, rt_kv, rms_g, w_q_h, w_kv_h, null_kv, w_out_h):
            light = light_attn(x, ln_g, ln_b, w_qkv_l, w_out_l)
            sq, iq = route(x, rt_q, NQ, min(NQ * FETCH_K, SEQ))
            skv, ikv = route(x, rt_kv, NKV, min(NKV * FETCH_K, SEQ))
            batch_idx = jnp.arange(x.shape[0])[:, None]
            xq = x[batch_idx, iq]
            xkv = x[batch_idx, ikv]
            routed_out = heavy_attn(xq, xkv, skv, rms_g, w_q_h, w_kv_h, null_kv, w_out_h)
            routed_out = routed_out * sq[..., None]
            out = jnp.broadcast_to(null_q, x.shape)
            out = out.at[batch_idx, iq].set(routed_out)
            return light + out
        return forward(x, ln_g, ln_b, w_qkv_l, w_out_l, null_q, rt_q, rt_kv, rms_g, w_q_h, w_kv_h, null_kv, w_out_h)
    x = L0_attn_x
    x = _layernorm(x + _L0_attn_ref(x, L0_attn_rms1_w, L0_attn_rms2_w, L0_attn_in_proj_w, L0_attn_conv_w, L0_attn_conv_b, L0_attn_x_proj_w, L0_attn_dt_proj_w, L0_attn_dt_proj_b, L0_attn_A_log, L0_attn_D_skip, L0_attn_out_proj_w, L0_attn_fc1_w, L0_attn_fc1_b, L0_attn_fc2_w, L0_attn_fc2_b, L0_attn_fc3_w, L0_attn_fc3_b), axis=-1)
    x = _layernorm(x + _L0_ffn_ref(x, L0_ffn_Wr, L0_ffn_Wg, L0_ffn_Wu, L0_ffn_Wd, L0_ffn_Sg, L0_ffn_Su, L0_ffn_Sd, L0_ffn_expert_bias), axis=-1)
    x = _layernorm(x + _L1_attn_ref(x, L1_attn_Wq, L1_attn_Wk, L1_attn_Wv, L1_attn_Wo), axis=-1)
    x = _layernorm(x + _L1_ffn_ref(x, L1_ffn_ln_g, L1_ffn_ln_b, L1_ffn_w_qkv_l, L1_ffn_w_out_l, L1_ffn_null_q, L1_ffn_rt_q, L1_ffn_rt_kv, L1_ffn_rms_g, L1_ffn_w_q_h, L1_ffn_w_kv_h, L1_ffn_null_kv, L1_ffn_w_out_h), axis=-1)
    return x

_drawn_inputs = setup_inputs


def setup_inputs(seed=0):
    import zlib

    import numpy as np

    out = dict(_drawn_inputs(seed))
    spreads = {'L0_attn_rms1_w': (1.0, 0.6),
     'L0_attn_rms2_w': (1.0, 0.6),
     'L0_attn_conv_b': (0.0, 0.321),
     'L0_attn_dt_proj_b': (-4.0, 0.6),
     'L0_attn_D_skip': (1.0, 0.6),
     'L0_attn_fc1_b': (0.0, 0.8),
     'L0_attn_fc2_b': (0.0, 0.442),
     'L0_attn_fc3_b': (0.0, 0.1),
     'L0_ffn_expert_bias': (0.0, 0.1),
     'L1_ffn_ln_g': (1.0, 0.6),
     'L1_ffn_ln_b': (0.0, 0.609),
     'L1_ffn_rms_g': (1.0, 0.6)}
    factors = {'L0_attn_in_proj_w': 3.814,
     'L0_attn_conv_w': 3.221,
     'L0_attn_x_proj_w': 8.0,
     'L0_attn_dt_proj_w': 8.0,
     'L0_attn_A_log': 8.0,
     'L0_attn_out_proj_w': 2.997,
     'L1_attn_Wq': 3.533,
     'L1_attn_Wk': 2.859,
     'L1_ffn_w_qkv_l': 3.695,
     'L1_ffn_w_out_l': 3.578,
     'L1_ffn_rt_kv': 8.0,
     'L1_ffn_w_q_h': 8.0,
     'L1_ffn_w_kv_h': 8.0,
     'L1_ffn_null_kv': 8.0,
     'L1_ffn_w_out_h': 8.0,
     'L0_attn_fc3_w': 2.723}
    for name, (base, spread) in spreads.items():
        noise = np.random.default_rng([zlib.crc32(name.encode()), seed]).standard_normal(out[name].shape)
        drawn = base * np.exp(spread * noise) if base else spread * noise
        out[name] = jnp.asarray(drawn.astype(out[name].dtype))
    for name, factor in factors.items():
        out[name] = (out[name] * factor).astype(out[name].dtype)
    return out
```

```python
import math
from contextlib import ExitStack

import concourse.bass as bass
from concourse import mybir

F32 = mybir.dt.float32
BF16 = mybir.dt.bfloat16
I32 = mybir.dt.int32
U32 = mybir.dt.uint32
ALU = mybir.AluOpType
ACT = mybir.ActivationFunctionType
AXX = mybir.AxisListType.X

P = 128
D = 256
DH = D // P
BATCH, SEQ = 2, 2048
TOK = BATCH * SEQ
TILES = TOK // P
GT = 4
GN = GT * P
GROUPS = TOK // GN
SGROUPS = SEQ // GN
LN_EPS = 1e-5
BIG = 1e30


class Steps:

    def __init__(self, eng, sem, per=0, i=0):
        self.eng, self.sem, self.base, self.per, self.n = eng, sem, i * per, per, 0

    def then(self, ins):
        self.n += 1
        ins.then_inc(self.sem, 1)
        return self.base + self.n

    def wait(self):
        self.eng.wait_ge(self.sem, self.base + self.n)

    def chain(self, ins):
        self.then(ins)
        self.wait()

    def close(self):
        assert self.n == self.per, (self.n, self.per)


class Alloc:

    def __init__(self, nc, ctx, tag):
        self.nc, self.ctx, self.tag, self.sems = nc, ctx, tag, []
        ctx.callback(self.clear)

    def clear(self):
        self.nc.clear_and_free_semaphores(self.sems)
        self.nc.all_engine_barrier()

    def sb(self, name, shape, dt=F32):
        return self.ctx.enter_context(self.nc.sbuf_tensor(f"{self.tag}_{name}", shape, dt))

    def ps(self, name, shape=(P, GN), dt=F32):
        return self.ctx.enter_context(self.nc.psum_tensor(f"{self.tag}_{name}", list(shape), dt))

    def sem(self, name):
        self.sems.append(self.nc.alloc_semaphore(name=f"{self.tag}_{name}"))
        return self.sems[-1]


def over(ap, n):
    return ap.unsqueeze(2).to_broadcast([ap.shape[0], ap.shape[1], n])


def each(ap, n):
    return ap.unsqueeze(1).to_broadcast([ap.shape[0], n, ap.shape[1]])


def statistics(st, v, row_of, stat, mv, rstd, n):
    for j in range(n):
        st.then(v.bn_stats(stat[:, j, :], row_of(j)))
    st.wait()
    st.then(v.memset(rstd[:, 0:n], 1.0))
    for j in range(n):
        st.then(v.bn_aggr(mv[:, j, :], stat[:, j, :]))
    st.wait()


def normalize(st, v, y, stat, mv, rstd, S, turn, i, X):
    statistics(st, v, lambda j: y[:, j, :], stat, mv, rstd, GT)
    v.tensor_scalar(mv[:, :, 1], mv[:, :, 1], LN_EPS, None, ALU.add).then_inc(S["var"], 1)
    st.eng.wait_ge(S["rstd_done"], turn)
    for j in range(GT):
        st.then(v.tensor_scalar(X[:, bass.ds(i * GT + j, 1), :].rearrange("p a d -> p (a d)"), y[:, j, :], mv[:, j, 0:1],
                                rstd[:, j:j + 1], ALU.subtract, ALU.mult))
    st.wait()


def load_phase(nc, x, X, K):
    with ExitStack() as ctx:
        A = Alloc(nc, ctx, "ld")
        x_in, made = A.sem("x_in"), A.sem("made")
        xv = x.rearrange("b (t p) d -> p (b t) d", p=P)
        block = ctx.enter_context(nc.Block())

        @block.sync
        def _(sp):
            for g in range(GROUPS):
                sp.dma_start(X[:, g * GT:(g + 1) * GT, :], xv[:, g * GT:(g + 1) * GT, :]).then_inc(x_in, 16)
            sp.wait_ge(x_in, 16 * GROUPS)

        @block.gpsimd
        def _(pool):
            st = Steps(pool, made)
            nc.gpsimd.memset(K["neghalf"][:, :], -0.5)
            st.then(nc.gpsimd.memset(K["ident"][:, :], 0.0))
            st.chain(nc.gpsimd.memset(K["sel"][:, :, :], 0.0))
            st.chain(nc.gpsimd.affine_select(out=K["ident"][:, :], in_=K["ident"][:, :], compare_op=ALU.not_equal,
                                            fill=1.0, base=0, pattern=[[-1, P]], channel_multiplier=1))
            for part in range(3):
                s = K["sel"][32 * part:32 * part + 32, :, :]
                st.chain(nc.gpsimd.affine_select(out=s, in_=s, compare_op=ALU.not_equal, fill=1.0, base=0,
                                                pattern=[[-1, 32], [0, P]], channel_multiplier=1))


def store_phase(nc, X, out):
    with ExitStack() as ctx:
        A = Alloc(nc, ctx, "st")
        stored = A.sem("stored")
        ov = out.rearrange("b (t p) d -> p (b t) d", p=P)
        block = ctx.enter_context(nc.Block())

        @block.sync
        def _(sp):
            for g in range(GROUPS):
                sp.dma_start(ov[:, g * GT:(g + 1) * GT, :], X[:, g * GT:(g + 1) * GT, :]).then_inc(stored, 16)
            sp.wait_ge(stored, 16 * GROUPS)


DI = 2 * D
MB = DI // P
NS = 16
CONV = 4
RANK = D // 16
HID = 2 * D
HB = HID // P
RMS_EPS = 1e-6
LOG1P = [1 / k for k in (13, 11, 9, 7, 5, 3, 1)]


def split3(st, v, src, rest, part, dst, rows):
    st.chain(v.tensor_copy(dst[0:rows, :], src))
    st.chain(v.tensor_tensor(out=rest, in0=src, in1=dst[0:rows, :], op=ALU.subtract))
    st.then(v.tensor_copy(dst[32:32 + rows, :], rest))
    st.chain(v.tensor_copy(part, rest))
    st.chain(v.tensor_tensor(out=rest, in0=rest, in1=part, op=ALU.subtract))
    return v.tensor_copy(dst[64:64 + rows, :], rest)


def mean_square(st, v, x_of, stat, mv, rstd, S):
    statistics(st, v, x_of, stat, mv, rstd, GT)
    st.chain(v.tensor_tensor(out=mv[:, :, 0], in0=mv[:, :, 0], in1=mv[:, :, 0], op=ALU.mult))
    st.chain(v.tensor_tensor(out=mv[:, :, 0], in0=mv[:, :, 0], in1=mv[:, :, 1], op=ALU.add))
    v.tensor_scalar(mv[:, :, 1], mv[:, :, 0], RMS_EPS, None, ALU.add).then_inc(S["var"], 1)


def mamba_phase(nc, X, K, I):
    with ExitStack() as ctx:
        A = Alloc(nc, ctx, "ma")
        w = lambda n: I["L0_attn_" + n]
        w_in = A.sb("w_in", [P, DH, 2 * DI])
        w_x, w_dt = A.sb("w_x", [P, MB, 48]), A.sb("w_dt", [48, DI])
        w_out = A.sb("w_out", [P, MB, D])
        w_fc1, w_fc2, w_fc3 = A.sb("w_fc1", [P, DH, HID]), A.sb("w_fc2", [P, HB, HID]), A.sb("w_fc3", [P, HB, D])
        rms1, rms2 = A.sb("rms1", [P, DH]), A.sb("rms2", [P, DH])
        conv_w, conv_b = A.sb("conv_w", [P, MB, CONV]), A.sb("conv_b", [P, MB])
        dt_b, skip = A.sb("dt_b", [P, MB]), A.sb("skip", [P, MB])
        a_log, a_neg = A.sb("a_log", [P, MB, NS]), A.sb("a_neg", [P, MB, NS])
        b_fc1, b_fc2, b_fc3 = A.sb("b_fc1", [P, HB]), A.sb("b_fc2", [P, HB]), A.sb("b_fc3", [P, D])
        xs, xT = A.sb("xs", [P, GT, D]), A.sb("xT", [P, DH, GN])
        x1, y = A.sb("x1", [P, GT, D]), A.sb("y", [P, GT, D])
        ubuf = A.sb("ubuf", [P, MB, CONV - 1 + GN])
        conv, u, gz = A.sb("conv", [P, MB, GN]), A.sb("u", [P, MB, GN]), A.sb("gz", [P, MB, GN])
        dbc, rest, part = A.sb("dbc", [48, GN]), A.sb("rest", [32, GN]), A.sb("part", [32, GN], BF16)
        bcp = A.sb("bcp", [96, GN], BF16)
        dt = A.sb("dt", [P, MB, GN])
        decay = [A.sb(f"decay{k}", [P, MB, GN]) for k in range(2)]
        drive = [A.sb(f"drive{k}", [P, MB, GN]) for k in range(2)]
        state = [A.sb(f"state{k}", [P, MB, GN]) for k in range(2)]
        read = [A.sb(f"read{k}", [P, MB, GN]) for k in range(2)]
        cs = [A.sb(f"cs{k}", [P, GN]) for k in range(2)]
        last = A.sb("last", [P, NS, MB])
        stat, mv, rstd = A.sb("stat", [P, GT, 6]), A.sb("mv", [P, GT, 2]), A.sb("rstd", [P, GT])
        ex, inv, z2, wdt = conv, decay[0], decay[1], conv
        zz, poly = drive[0], drive[1]
        h1, h2 = drive[0], drive[1]
        bank = [A.ps(f"bank{k}") for k in range(8)]
        acc = bank[0:4]
        spread_b, spread_c = bank[4:6], bank[6:8]
        S = {n: A.sem(n) for n in (
            "w_in", "dve", "act", "a_neg", "var", "rstd_done", "xs_full", "turned", "xT_full", "proj", "proj_out", "conv_done",
            "u_full", "dbc_done", "dbc_out", "bc_parts", "dt_raw", "dt_abs", "ex_done", "inv_done", "z2_done", "zz_done", "dt_done",
            "b_spread", "c_spread", "decay_done", "c_copied", "drive_done", "scan_done", "read_done", "read_used",
            "gated", "mixed", "x1_done", "fc1", "h1_done", "fc2", "h2_done", "fc3", "y_done", "sums", "reset", "halo")}
        block = ctx.enter_context(nc.Block())

        vec = lambda a, n: a.rearrange("(m p) -> p m", p=P)
        loads = [(w_in[:, :, :], w("in_proj_w").rearrange("(h p) e -> p h e", p=P)),
                 (w_x[:, :, :], w("x_proj_w").rearrange("(m p) e -> p m e", p=P)),
                 (w_dt[32:48, :], w("dt_proj_w")),
                 (w_out[:, :, :], w("out_proj_w").rearrange("(m p) e -> p m e", p=P)),
                 (w_fc1[:, :, :], w("fc1_w").rearrange("(h p) e -> p h e", p=P)),
                 (w_fc2[:, :, :], w("fc2_w").rearrange("(h p) e -> p h e", p=P)),
                 (w_fc3[:, :, :], w("fc3_w").rearrange("(h p) e -> p h e", p=P)),
                 (rms1[:, :], vec(w("rms1_w"), DH)), (rms2[:, :], vec(w("rms2_w"), DH)),
                 (conv_w[:, :, :], w("conv_w").rearrange("(m p) k -> p m k", p=P)), (conv_b[:, :], vec(w("conv_b"), MB)),
                 (dt_b[:, :], vec(w("dt_proj_b"), MB)), (skip[:, :], vec(w("D_skip"), MB)),
                 (a_log[:, :, :], w("A_log").rearrange("(m p) n -> p m n", p=P)),
                 (b_fc1[:, :], vec(w("fc1_b"), HB)), (b_fc2[:, :], vec(w("fc2_b"), HB)),
                 (b_fc3[:, :], w("fc3_b").unsqueeze(0).to_broadcast([P, D]))]
        LOADED = 16 * len(loads)

        @block.sync
        def _(sp):
            with nc.allow_non_contiguous_dma(reason="vectors onto partitions, once"):
                for dst, src in loads:
                    sp.dma_start(dst, src).then_inc(S["w_in"], 16)
            sp.wait_ge(S["w_in"], LOADED)

        @block.gpsimd
        def _(pool):
            g = nc.gpsimd
            pool.wait_ge(S["w_in"], LOADED)
            with pool.Fori(0, GROUPS) as i:
                pool.wait_ge(S["var"], 3 * i + 1)
                g.tensor_tensor(out=rstd[:, :], in0=mv[:, :, 1], in1=K["neghalf"][:, :], op=ALU.pow).then_inc(S["rstd_done"], 1)
                for n in range(NS):
                    pool.wait_ge(S["scan_done"], NS * i + n + 1)
                    pool.wait_ge(S["c_copied"], NS * i + n + 1)
                    if n >= 2:
                        pool.wait_ge(S["read_used"], NS * i + n - 1)
                    g.tensor_tensor(out=read[n % 2][:, :, :], in0=state[n % 2][:, :, :], in1=each(cs[n % 2][:, :], MB),
                                    op=ALU.mult).then_inc(S["read_done"], 1)
                pool.wait_ge(S["var"], 3 * i + 2)
                g.tensor_tensor(out=rstd[:, :], in0=mv[:, :, 1], in1=K["neghalf"][:, :], op=ALU.pow).then_inc(S["rstd_done"], 1)
                pool.wait_ge(S["x1_done"], 2 * (i + 1))
                g.tensor_tensor(out=y[:, :, :], in0=x1[:, :, :], in1=X[:, bass.ds(i * GT, GT), :], op=ALU.add)\
                 .then_inc(S["sums"], 1)
                pool.wait_ge(S["sums"], 2 * i + 1)
                g.tensor_tensor(out=y[:, :, :], in0=y[:, :, :], in1=each(b_fc3[:, :], GT), op=ALU.add).then_inc(S["sums"], 1)
                pool.wait_ge(S["var"], 3 * i + 3)
                g.tensor_tensor(out=rstd[:, :], in0=mv[:, :, 1], in1=K["neghalf"][:, :], op=ALU.pow).then_inc(S["rstd_done"], 1)

        @block.tensor
        def _(pe):
            t = nc.tensor
            pe.wait_ge(S["w_in"], LOADED)

            def turn(banks, n):
                pe.wait_ge(S["xs_full"], n)
                for hh in range(DH):
                    for j in range(GT):
                        m = t.transpose(banks[hh][:, j * P:(j + 1) * P], xs[:, j, hh * P:(hh + 1) * P], K["ident"][:, :])
                    m.then_inc(S["turned"], 1)

            with pe.Fori(0, GROUPS) as i:
                turn(bank[4:6], 2 * i + 1)
                pe.wait_ge(S["xT_full"], 2 * DH * i + DH)
                for m in range(2 * MB):
                    if m >= 2:
                        pe.wait_ge(S["proj_out"], 2 * MB * i + m - 1)
                    for hh in range(DH):
                        ins = t.matmul(bank[6 + m % 2][:, :], w_in[:, hh, m * P:(m + 1) * P], xT[:, hh, :],
                                       start=(hh == 0), stop=(hh == DH - 1))
                    ins.then_inc(S["proj"], 1)
                for m in range(MB):
                    pe.wait_ge(S["u_full"], MB * i + m + 1)
                    ins = t.matmul(bank[4][0:48, :], w_x[:, m, :], u[:, m, :], start=(m == 0), stop=(m == MB - 1))
                ins.then_inc(S["dbc_done"], 1)
                pe.wait_ge(S["dbc_out"], i + 1)
                for m in range(MB):
                    pe.wait_ge(S["dt_abs"], MB * i + m - 1) if m >= 2 else pe.wait_ge(S["proj_out"], 2 * MB * (i + 1))
                    t.matmul(bank[6 + m % 2][:, :], w_dt[32:48, m * P:(m + 1) * P], dbc[32:48, :], start=True, stop=True,
                             tile_position=(32, 0)).then_inc(S["dt_raw"], 1)

                def spread(n):
                    if n >= 2:
                        pe.wait_ge(S["drive_done"], NS * i + n - 1)
                    t.matmul(spread_b[n % 2][:, :], K["sel"][:, n, :], bcp[:, :], start=True, stop=True).then_inc(S["b_spread"], 1)
                    if n >= 2:
                        pe.wait_ge(S["c_copied"], NS * i + n - 1)
                    t.matmul(spread_c[n % 2][:, :], K["sel"][:, NS + n, :], bcp[:, :], start=True, stop=True).then_inc(S["c_spread"], 1)

                def sum_states(n):
                    pe.wait_ge(S["read_done"], NS * i + n + 1)
                    for m in range(MB):
                        ins = t.matmul(acc[m][:, :], K["ident"][:, :], read[n % 2][:, m, :], start=(n == 0), stop=(n == NS - 1))
                    ins.then_inc(S["read_used"], 1)

                pe.wait_ge(S["bc_parts"], i + 1)
                pe.wait_ge(S["dt_abs"], MB * (i + 1))
                for n in range(NS + 2):
                    if n < NS:
                        spread(n)
                    if n >= 2:
                        sum_states(n - 2)
                pe.wait_ge(S["gated"], i + 1)
                for j in range(GT):
                    for m in range(MB):
                        ins = t.matmul(bank[4 + j // 2][:, (j % 2) * D:(j % 2 + 1) * D], u[:, m, j * P:(j + 1) * P], w_out[:, m, :],
                                       start=(m == 0), stop=(m == MB - 1))
                    if j % 2:
                        ins.then_inc(S["mixed"], 1)
                turn(bank[0:2], 2 * i + 2)
                pe.wait_ge(S["xT_full"], 2 * DH * i + 2 * DH)
                for m in range(HB):
                    if m >= 2:
                        pe.wait_ge(S["h1_done"], HB * i + m - 1)
                    for hh in range(DH):
                        ins = t.matmul(bank[6 + m % 2][:, :], w_fc1[:, hh, m * P:(m + 1) * P], xT[:, hh, :],
                                       start=(hh == 0), stop=(hh == DH - 1))
                    ins.then_inc(S["fc1"], 1)
                pe.wait_ge(S["h1_done"], HB * (i + 1))
                for m in range(HB):
                    if m >= 2:
                        pe.wait_ge(S["h2_done"], HB * i + m - 1)
                    for k in range(HB):
                        ins = t.matmul(bank[6 + m % 2][:, :], w_fc2[:, k, m * P:(m + 1) * P], h1[:, k, :],
                                       start=(k == 0), stop=(k == HB - 1))
                    ins.then_inc(S["fc2"], 1)
                pe.wait_ge(S["h2_done"], HB * (i + 1))
                for j in range(GT):
                    for k in range(HB):
                        ins = t.matmul(bank[2 + j // 2][:, (j % 2) * D:(j % 2 + 1) * D], h2[:, k, j * P:(j + 1) * P], w_fc3[:, k, :],
                                       start=(k == 0), stop=(k == HB - 1))
                    if j % 2:
                        ins.then_inc(S["fc3"], 1)

        @block.scalar
        def _(act):
            a = nc.scalar
            act.wait_ge(S["w_in"], LOADED)
            a.activation(a_neg[:, :, :], a_log[:, :, :], ACT.Exp).then_inc(S["a_neg"], 1)

            def turned(banks, gain, n):
                for hh in range(DH):
                    act.wait_ge(S["turned"], n + hh + 1)
                    a.activation(xT[:, hh, :], banks[hh][:, :], ACT.Copy, scale=gain[:, hh:hh + 1]).then_inc(S["xT_full"], 1)

            with act.Fori(0, GROUPS) as i:
                turned(bank[4:6], rms1, 2 * DH * i)
                act.wait_ge(S["halo"], i)
                for m in range(2 * MB):
                    act.wait_ge(S["proj"], 2 * MB * i + m + 1)
                    if m < MB:
                        ins = a.activation(ubuf[:, m, CONV - 1:], bank[6 + m % 2][:, :], ACT.Copy)
                    else:
                        ins = a.activation(gz[:, m - MB, :], bank[6 + m % 2][:, :], ACT.Silu)
                    ins.then_inc(S["proj_out"], 1)
                for m in range(MB):
                    act.wait_ge(S["conv_done"], MB * i + m + 1)
                    a.activation(u[:, m, :], conv[:, m, :], ACT.Silu).then_inc(S["u_full"], 1)
                act.wait_ge(S["u_full"], MB * (i + 1))
                for m in range(MB):
                    act.wait_ge(S["dt_raw"], MB * i + m + 1)
                    a.activation(dt[:, m, :], bank[6 + m % 2][:, :], ACT.Relu, bias=dt_b[:, m:m + 1]).then_inc(S["act"], 1)
                    a.activation(ex[:, m, :], bank[6 + m % 2][:, :], ACT.Abs, bias=dt_b[:, m:m + 1]).then_inc(S["dt_abs"], 1)
                act.wait_ge(S["dt_abs"], MB * (i + 1))
                a.activation(ex[:, :, :], ex[:, :, :], ACT.Exp, scale=-1.0).then_inc(S["ex_done"], 1)
                act.wait_ge(S["ex_done"], i + 1)
                a.activation(inv[:, :, :], ex[:, :, :], ACT.Ln, scale=0.5, bias=1.0).then_inc(S["act"], 1)
                act.wait_ge(S["act"], (MB + 1) * (i + 1))
                a.activation(inv[:, :, :], inv[:, :, :], ACT.Exp, scale=-1.0).then_inc(S["inv_done"], 1)
                act.wait_ge(S["z2_done"], i + 1)
                a.activation(zz[:, :, :], z2[:, :, :], ACT.Square, scale=0.5).then_inc(S["zz_done"], 1)
                act.wait_ge(S["dt_done"], i + 1)
                for n in range(NS):
                    if n >= 2:
                        act.wait_ge(S["scan_done"], NS * i + n - 1)
                    for m in range(MB):
                        ins = a.activation(decay[n % 2][:, m, :], dt[:, m, :], ACT.Exp, scale=a_neg[:, m, n:n + 1])
                    ins.then_inc(S["decay_done"], 1)
                    act.wait_ge(S["c_spread"], NS * i + n + 1)
                    if n >= 2:
                        act.wait_ge(S["read_done"], NS * i + n - 1)
                    a.activation(cs[n % 2][:, :], spread_c[n % 2][:, :], ACT.Copy).then_inc(S["c_copied"], 1)
                turned(bank[0:2], rms2, 2 * DH * i + DH)
                for m in range(HB):
                    act.wait_ge(S["fc1"], HB * i + m + 1)
                    a.activation(h1[:, m, :], bank[6 + m % 2][:, :], ACT.Relu, bias=b_fc1[:, m:m + 1]).then_inc(S["h1_done"], 1)
                for m in range(HB):
                    act.wait_ge(S["fc2"], HB * i + m + 1)
                    a.activation(h2[:, m, :], bank[6 + m % 2][:, :], ACT.Relu, bias=b_fc2[:, m:m + 1]).then_inc(S["h2_done"], 1)

        @block.vector
        def _(dve):
            v = nc.vector
            dve.wait_ge(S["a_neg"], 1)
            v.tensor_scalar(a_neg[:, :, :], a_neg[:, :, :], -1.0, None, ALU.mult).then_inc(S["a_neg"], 1)
            with dve.Fori(0, BATCH) as b:
                v.memset(last[:, :, :], 0.0).then_inc(S["reset"], 1)
                v.memset(ubuf[:, :, 0:CONV - 1], 0.0).then_inc(S["reset"], 1)
                with dve.Fori(0, SGROUPS) as s:
                    i = b * SGROUPS + s
                    st = Steps(dve, S["dve"], 80, i)
                    xj = lambda j: X[:, bass.ds(i * GT + j, 1), :].rearrange("p a d -> p (a d)")
                    mean_square(st, v, xj, stat, mv, rstd, S)
                    dve.wait_ge(S["rstd_done"], 3 * i + 1)
                    for j in range(GT):
                        ins = v.tensor_scalar(xs[:, j, :], xj(j), rstd[:, j:j + 1], None, ALU.mult)
                    ins.then_inc(S["xs_full"], 1)
                    dve.wait_ge(S["reset"], 2 * (b + 1))
                    for m in range(MB):
                        dve.wait_ge(S["proj_out"], 2 * MB * i + m + 1)
                        st.chain(v.tensor_scalar(conv[:, m, :], ubuf[:, m, CONV - 1:], conv_w[:, m, CONV - 1:CONV], conv_b[:, m:m + 1],
                                                 ALU.mult, ALU.add))
                        for k in range(CONV - 1):
                            ins = v.scalar_tensor_tensor(out=conv[:, m, :], in0=ubuf[:, m, k:k + GN], scalar=conv_w[:, m, k:k + 1],
                                                         in1=conv[:, m, :], op0=ALU.mult, op1=ALU.add)
                            if k < CONV - 2:
                                st.chain(ins)
                        ins.then_inc(S["conv_done"], 1)
                    dve.wait_ge(S["conv_done"], MB * (i + 1))
                    v.tensor_copy(ubuf[:, :, 0:CONV - 1], ubuf[:, :, GN:GN + CONV - 1]).then_inc(S["halo"], 1)
                    dve.wait_ge(S["dbc_done"], i + 1)
                    v.tensor_copy(dbc[:, :], bank[4][0:48, :]).then_inc(S["dbc_out"], 1)
                    dve.wait_ge(S["dbc_out"], i + 1)
                    split3(st, v, dbc[0:32, :], rest[:, :], part[:, :], bcp, 32).then_inc(S["bc_parts"], 1)
                    flat = lambda a: a[:, :, :].rearrange("p m t -> p (m t)")
                    dve.wait_ge(S["inv_done"], i + 1)
                    v.tensor_tensor(out=flat(z2), in0=flat(ex), in1=flat(inv), op=ALU.mult).then_inc(S["z2_done"], 1)
                    dve.wait_ge(S["zz_done"], i + 1)
                    st.chain(v.tensor_scalar(flat(poly), flat(zz), LOG1P[0], LOG1P[1], ALU.mult, ALU.add))
                    st.chain(v.tensor_tensor(out=flat(poly), in0=flat(poly), in1=flat(zz), op=ALU.mult))
                    for c, by in zip(LOG1P[2:], [zz] * (len(LOG1P) - 3) + [z2]):
                        st.chain(v.scalar_tensor_tensor(out=flat(poly), in0=flat(poly), scalar=c, in1=flat(by),
                                                        op0=ALU.add, op1=ALU.mult))
                    v.tensor_tensor(out=flat(dt), in0=flat(dt), in1=flat(poly), op=ALU.add).then_inc(S["dt_done"], 1)
                    dve.wait_ge(S["dt_done"], i + 1)
                    st.chain(v.tensor_tensor(out=wdt[:, :, :], in0=dt[:, :, :], in1=u[:, :, :], op=ALU.mult))

                    def drives(n):
                        dve.wait_ge(S["b_spread"], NS * i + n + 1)
                        if n >= 2:
                            dve.wait_ge(S["scan_done"], NS * i + n - 1)
                        v.tensor_tensor(out=drive[n % 2][:, :, :], in0=wdt[:, :, :], in1=each(spread_b[n % 2][:, :], MB),
                                        op=ALU.mult).then_inc(S["drive_done"], 1)

                    def scans(n):
                        dve.wait_ge(S["decay_done"], NS * i + n + 1)
                        dve.wait_ge(S["drive_done"], NS * i + n + 1)
                        if n >= 2:
                            dve.wait_ge(S["read_done"], NS * i + n - 1)
                        st.wait()
                        for m in range(MB):
                            ins = v.tensor_tensor_scan(state[n % 2][:, m, :], decay[n % 2][:, m, :], drive[n % 2][:, m, :],
                                                       last[:, n, m:m + 1], ALU.mult, ALU.add)
                        ins.then_inc(S["scan_done"], 1)

                    def keeps(n):
                        dve.wait_ge(S["scan_done"], NS * i + n + 1)
                        st.then(v.tensor_copy(last[:, n, :], state[n % 2][:, :, GN - 1]))

                    drives(0)
                    for n in range(NS):
                        if n + 1 < NS:
                            drives(n + 1)
                        if n >= 1:
                            keeps(n - 1)
                        scans(n)
                    keeps(NS - 1)
                    dve.wait_ge(S["read_used"], NS * (i + 1))
                    for m in range(MB):
                        st.then(v.scalar_tensor_tensor(out=u[:, m, :], in0=u[:, m, :], scalar=skip[:, m:m + 1], in1=acc[m][:, :],
                                                       op0=ALU.mult, op1=ALU.add))
                    st.wait()
                    v.tensor_tensor(out=u[:, :, :], in0=u[:, :, :], in1=gz[:, :, :], op=ALU.mult).then_inc(S["gated"], 1)
                    for k in range(2):
                        dve.wait_ge(S["mixed"], 2 * i + k + 1)
                        v.tensor_tensor(out=x1[:, 2 * k:2 * k + 2, :], in0=bank[4 + k][:, :].rearrange("p (j d) -> p j d", d=D),
                                        in1=X[:, bass.ds(i * GT + 2 * k, 2), :], op=ALU.add).then_inc(S["x1_done"], 1)
                    dve.wait_ge(S["x1_done"], 2 * (i + 1))
                    mean_square(st, v, lambda j: x1[:, j, :], stat, mv, rstd, S)
                    dve.wait_ge(S["rstd_done"], 3 * i + 2)
                    for j in range(GT):
                        ins = v.tensor_scalar(xs[:, j, :], x1[:, j, :], rstd[:, j:j + 1], None, ALU.mult)
                    ins.then_inc(S["xs_full"], 1)
                    dve.wait_ge(S["sums"], 2 * (i + 1))
                    for k in range(2):
                        dve.wait_ge(S["fc3"], 2 * i + k + 1)
                        v.tensor_tensor(out=y[:, 2 * k:2 * k + 2, :], in0=bank[2 + k][:, :].rearrange("p (j d) -> p j d", d=D),
                                        in1=y[:, 2 * k:2 * k + 2, :], op=ALU.add).then_inc(S["y_done"], 1)
                    dve.wait_ge(S["y_done"], 2 * (i + 1))
                    normalize(st, v, y, stat, mv, rstd, S, 3 * i + 3, i, X)
                    st.close()


E = 8
FE = 128
FS = 256
UNITS = E + FS // P


def moe_phase(nc, X, K, Wr, Wg, Wu, Wd, Sg, Su, Sd, expert_bias):
    with ExitStack() as ctx:
        A = Alloc(nc, ctx, "moe")
        wr, wg, wu = A.sb("wr", [P, DH, E]), A.sb("wg", [P, DH, UNITS * P]), A.sb("wu", [P, DH, UNITS * P])
        wd, ebias = A.sb("wd", [P, UNITS, D]), A.sb("ebias", [P, E])
        xg, xT = A.sb("xg", [P, GT, D]), A.sb("xT", [P, DH, GN])
        silu, prod, h = A.sb("silu", [P, 2, GN]), A.sb("prod", [P, 2, GN]), A.sb("h", [P, UNITS, GN])
        logit, eq, key, first, second = (A.sb(n, [P, GT, E]) for n in ("logit", "eq", "key", "first", "second"))
        rank = A.sb("rank", [P, GT, E])
        m1, m2, km, th, p1, p2 = (A.sb(n, [P, GT]) for n in ("m1", "m2", "km", "th", "p1", "p2"))
        rw = A.sb("rw", [P, GT, E])
        rwT, rwp = A.sb("rwT", [E, GN]), A.sb("rwp", [96, GN], BF16)
        rest, part = A.sb("rest", [E, GN]), A.sb("part", [E, GN], BF16)
        y, stat, mv, rstd = A.sb("y", [P, GT, D]), A.sb("stat", [P, GT, 6]), A.sb("mv", [P, GT, 2]), A.sb("rstd", [P, GT])
        turn = [A.ps(f"turn{n}") for n in range(DH)]
        gate, up = [A.ps(f"gate{n}") for n in range(2)], [A.ps(f"up{n}") for n in range(2)]
        lg, spread = A.ps("lg"), A.ps("spread")
        sems = ("w_in", "ready", "xg_full", "turned", "xT_full", "logits", "dve", "gap", "halves", "weights",
                "rwT_turned", "gated", "upped", "silued", "spreaded", "h_done", "out_done", "var", "rstd_done", "y_done", "tanh")
        S = {n: A.sem(n) for n in sems}
        W_DMAS = 10
        order = list(range(E, UNITS)) + list(range(E))
        block = ctx.enter_context(nc.Block())

        @block.sync
        def _(sp):
            loads = [(wr[:, :, :], Wr.rearrange("(h p) e -> p h e", p=P)),
                     (wd[:, 0:E, :], Wd.rearrange("e f d -> f e d")),
                     (wd[:, E:UNITS, :], Sd.rearrange("(u f) d -> f u d", f=P)),
                     (ebias[:, :], expert_bias.unsqueeze(0).to_broadcast([P, E]))]
            for dst, routed, shared in ((wg, Wg, Sg), (wu, Wu, Su)):
                loads.append((dst[:, :, E * P:], shared.rearrange("(h p) f -> p h f", p=P)))
                for hh in range(DH):
                    loads.append((dst[:, hh, 0:E * P].rearrange("p (e f) -> p e f", e=E),
                                  routed[:, hh * P:(hh + 1) * P, :].rearrange("e p f -> p e f")))
            assert len(loads) == W_DMAS
            for dst, src in loads:
                sp.dma_start(dst, src).then_inc(S["w_in"], 16)
            sp.wait_ge(S["w_in"], 16 * W_DMAS)

        @block.gpsimd
        def _(pool):
            nc.gpsimd.iota(rank[:, :, :], pattern=[[0, GT], [-1, E]], base=E, channel_multiplier=0,
                           allow_small_or_imprecise_dtypes=True).then_inc(S["ready"], 1)
            nc.gpsimd.memset(rwp[:, :], 0.0).then_inc(S["ready"], 1)
            with pool.Fori(0, GROUPS) as i:
                pool.wait_ge(S["y_done"], 2 * i)
                nc.gpsimd.tensor_copy(xg[:, :, :], X[:, bass.ds(i * GT, GT), :]).then_inc(S["xg_full"], 1)
                pool.wait_ge(S["var"], i + 1)
                nc.gpsimd.tensor_tensor(out=rstd[:, :], in0=mv[:, :, 1], in1=K["neghalf"][:, 0:GT],
                                        op=ALU.pow).then_inc(S["rstd_done"], 1)

        @block.tensor
        def _(pe):
            pe.wait_ge(S["w_in"], 16 * W_DMAS)
            with pe.Fori(0, GROUPS) as i:
                pe.wait_ge(S["xg_full"], i + 1)
                pe.wait_ge(S["y_done"], 2 * i)
                for hh in range(DH):
                    for j in range(GT):
                        t = nc.tensor.transpose(turn[hh][:, j * P:(j + 1) * P], xg[:, j, hh * P:(hh + 1) * P], K["ident"][:, :])
                    t.then_inc(S["turned"], 1)
                pe.wait_ge(S["xT_full"], DH * (i + 1))
                for j in range(GT):
                    for hh in range(DH):
                        m = nc.tensor.matmul(lg[:, j * E:(j + 1) * E], xT[:, hh, j * P:(j + 1) * P], wr[:, hh, :],
                                             start=(hh == 0), stop=(hh == DH - 1))
                m.then_inc(S["logits"], 1)
                for n, u in enumerate(order):
                    if n >= 2:
                        pe.wait_ge(S["silued"], UNITS * i + n - 1)
                    for hh in range(DH):
                        m = nc.tensor.matmul(gate[n % 2][:, :], wg[:, hh, u * P:(u + 1) * P], xT[:, hh, :],
                                             start=(hh == 0), stop=(hh == DH - 1))
                    m.then_inc(S["gated"], 1)
                    if n >= 2:
                        pe.wait_ge(S["upped"], UNITS * i + n - 1)
                    for hh in range(DH):
                        m = nc.tensor.matmul(up[n % 2][:, :], wu[:, hh, u * P:(u + 1) * P], xT[:, hh, :],
                                             start=(hh == 0), stop=(hh == DH - 1))
                    m.then_inc(S["gated"], 1)
                    if n == 1:
                        pe.wait_ge(S["weights"], i + 1)
                        for j in range(GT):
                            t = nc.tensor.transpose(spread[0:E, j * P:(j + 1) * P], rw[:, j, :], K["ident"][:, :])
                        t.then_inc(S["rwT_turned"], 1)
                        pe.wait_ge(S["halves"], i + 1)
                    if n >= 2:
                        if n >= 3:
                            pe.wait_ge(S["h_done"], E * i + n - 2)
                        nc.tensor.matmul(spread[:, :], K["sel"][0:96, u, :], rwp[:, :], start=True,
                                         stop=True).then_inc(S["spreaded"], 1)
                pe.wait_ge(S["h_done"], E * (i + 1))
                for j in range(GT):
                    for u in range(UNITS):
                        m = nc.tensor.matmul(turn[j // 2][:, (j % 2) * D:(j % 2 + 1) * D], h[:, u, j * P:(j + 1) * P],
                                             wd[:, u, :], start=(u == 0), stop=(u == UNITS - 1))
                    if j % 2:
                        m.then_inc(S["out_done"], 1)

        @block.scalar
        def _(act):
            with act.Fori(0, GROUPS) as i:
                for hh in range(DH):
                    act.wait_ge(S["turned"], DH * i + hh + 1)
                    nc.scalar.activation(xT[:, hh, :], turn[hh][:, :], ACT.Copy).then_inc(S["xT_full"], 1)
                for n in range(UNITS):
                    act.wait_ge(S["gated"], 2 * UNITS * i + 2 * n + 1)
                    if n >= 2:
                        act.wait_ge(S["upped"], UNITS * i + n - 1)
                    nc.scalar.activation(silu[:, n % 2, :], gate[n % 2][:, :], ACT.Silu).then_inc(S["silued"], 1)
                    if n == 0:
                        act.wait_ge(S["gap"], i + 1)
                        nc.scalar.activation(th[:, :], km[:, :], ACT.Tanh, scale=0.5).then_inc(S["tanh"], 1)

        @block.vector
        def _(dve):
            v = nc.vector
            dve.wait_ge(S["ready"], 2)
            dve.wait_ge(S["w_in"], 16 * W_DMAS)
            with dve.Fori(0, GROUPS) as i:
                st = Steps(dve, S["dve"], 35, i)

                def best(one_hot, m):
                    st.chain(v.tensor_reduce(m[:, :], logit[:, :, :], AXX, ALU.max))
                    st.chain(v.tensor_tensor(out=eq[:, :, :], in0=logit[:, :, :], in1=over(m[:, :], E), op=ALU.is_equal))
                    st.chain(v.tensor_tensor(out=key[:, :, :], in0=eq[:, :, :], in1=rank[:, :, :], op=ALU.mult))
                    st.chain(v.tensor_reduce(km[:, :], key[:, :, :], AXX, ALU.max))
                    st.chain(v.tensor_tensor(out=one_hot[:, :, :], in0=key[:, :, :], in1=over(km[:, :], E), op=ALU.is_equal))

                dve.wait_ge(S["logits"], i + 1)
                st.chain(v.tensor_tensor(out=logit[:, :, :], in0=lg[:, 0:GT * E].rearrange("p (j e) -> p j e", e=E),
                                         in1=each(ebias[:, :], GT), op=ALU.add))
                best(first, m1)
                st.chain(v.scalar_tensor_tensor(out=logit[:, :, :], in0=first[:, :, :], scalar=-3e38, in1=logit[:, :, :],
                                                op0=ALU.mult, op1=ALU.add))
                best(second, m2)
                v.tensor_tensor(out=km[:, :], in0=m1[:, :], in1=m2[:, :], op=ALU.subtract).then_inc(S["gap"], 1)
                dve.wait_ge(S["tanh"], i + 1)
                st.then(v.tensor_scalar(p1[:, :], th[:, :], 0.5, 0.5, ALU.mult, ALU.add))
                st.chain(v.tensor_scalar(p2[:, :], th[:, :], -0.5, 0.5, ALU.mult, ALU.add))
                st.then(v.tensor_tensor(out=first[:, :, :], in0=first[:, :, :], in1=over(p1[:, :], E), op=ALU.mult))
                st.chain(v.tensor_tensor(out=second[:, :, :], in0=second[:, :, :], in1=over(p2[:, :], E), op=ALU.mult))
                v.tensor_tensor(out=rw[:, :, :], in0=first[:, :, :], in1=second[:, :, :], op=ALU.add).then_inc(S["weights"], 1)

                def unit(n):
                    u = order[n]
                    dve.wait_ge(S["silued"], UNITS * i + n + 1)
                    dve.wait_ge(S["gated"], 2 * UNITS * i + 2 * n + 2)
                    dst = h[:, u, :] if u >= E else prod[:, n % 2, :]
                    t = v.tensor_tensor(out=dst, in0=silu[:, n % 2, :], in1=up[n % 2][:, :], op=ALU.mult)
                    t.then_inc(S["upped"], 1)
                    if u < E:
                        dve.wait_ge(S["spreaded"], E * i + u + 1)
                        dve.wait_ge(S["upped"], UNITS * i + n + 1)
                        v.tensor_tensor(out=h[:, u, :], in0=prod[:, n % 2, :], in1=spread[:, :], op=ALU.mult)\
                         .then_inc(S["h_done"], 1)

                unit(0)
                unit(1)
                dve.wait_ge(S["rwT_turned"], i + 1)
                st.chain(v.tensor_copy(rwT[:, :], spread[0:E, :]))
                split3(st, v, rwT[:, :], rest[:, :], part[:, :], rwp, E).then_inc(S["halves"], 1)
                for n in range(2, UNITS):
                    unit(n)
                for b in range(2):
                    dve.wait_ge(S["out_done"], 2 * i + b + 1)
                    v.tensor_tensor(out=y[:, 2 * b:2 * b + 2, :], in0=turn[b][:, :].rearrange("p (j d) -> p j d", d=D),
                                    in1=xg[:, 2 * b:2 * b + 2, :], op=ALU.add).then_inc(S["y_done"], 1)
                dve.wait_ge(S["y_done"], 2 * (i + 1))
                normalize(st, v, y, stat, mv, rstd, S, i + 1, i, X)
                st.close()




HW = 512
HT = HW // P
CHUNKS = SEQ // P
KEYS = 2 * P
VT = CHUNKS + 1


def banded_phase(nc, X, K, tag, W, heads, scale, shift, valid, norm=None, add=None):
    rows = HW // heads
    per = P // rows
    pairs = heads // 2
    block_of = lambda p, a: p // per * 2 + a
    head = lambda p, a: block_of(p, a) * per + p % per
    halo = P - shift
    with ExitStack() as ctx:
        A = Alloc(nc, ctx, tag)
        wq, wk, wv = (A.sb(n, [P, DH, HW]) for n in ("wq", "wk", "wv"))
        wo = A.sb("wo", [P, HT, D])
        gain, bias = A.sb("gain", [P, DH]), A.sb("bias", [P, DH])
        xs = A.sb("xs", [P, GT, D])
        xT = A.sb("xT", [P, DH, halo + GN + halo])
        QT, KT = A.sb("QT", [P, HT, SEQ]), A.sb("KT", [P, HT, P + SEQ])
        V = A.sb("V", [P, VT, HW])
        band, edge = A.sb("band", [P, KEYS], BF16), A.sb("edge", [P, P + SEQ], BF16)
        identb, expand = A.sb("identb", [P, P], BF16), A.sb("expand", [heads, HT, P])
        qs = [A.sb(f"qs{k}", [P, HT, P]) for k in range(2)]
        ks = [A.sb(f"ks{k}", [P, HT, KEYS]) for k in range(2)]
        vs = [A.sb(f"vs{k}", [P, 2, HW]) for k in range(2)]
        mask = [A.sb(f"mask{k}", [P, KEYS], BF16) for k in range(2)]
        prob = [A.sb(f"prob{k}", [P, 2, KEYS]) for k in range(3)]
        probT = [A.sb(f"probT{k}", [P, 4, P]) for k in range(2)]
        nmax, sums, inv = A.sb("nmax", [P, heads]), A.sb("sums", [P, heads]), A.sb("inv", [P, heads])
        invT, invs = A.sb("invT", [heads, P]), A.sb("invs", [P, HT, P])
        mixed = A.sb("mixed", [P, HT, P])
        stat, mv, rstd = A.sb("stat", [P, GT, 6]), A.sb("mv", [P, GT, 2]), A.sb("rstd", [P, GT])
        y = A.sb("y", [P, D])
        if add:
            pick, picked = [A.sb(f"pick{k}", [P, 1], U32) for k in range(2)], [A.sb(f"picked{k}", [P, D]) for k in range(2)]
        bank = [A.ps(f"bank{k}") for k in range(8)]
        score, turned, outT, small = bank[0:3], bank[3:5], bank[5:7], bank[7]
        S = {n: A.sem(n) for n in (
            "w_in", "made", "zeroed", "xs_full", "turned", "xT_full", "proj", "proj_out", "v_done", "v_out", "halo", "var", "rstd_done", "dve",
            "q_copied", "k_copied", "masked", "scored", "maxed", "exped", "prob_turned", "probT_full", "outT_done", "inv_done",
            "inv_turned", "invT_full", "spread", "invs_full", "mixed_full", "out_done", "y_done", "x_done", "picks", "picked0", "picked1", "chunk_pv", "started")}
        block = ctx.enter_context(nc.Block())
        vec = lambda a: a.rearrange("(h p) -> p h", p=P)
        loads = [(dst[:, :, :], src.rearrange("(h p) e -> p h e", p=P))
                 for dst, src in ((wq, W["q"]), (wk, W["k"]), (wv, W["v"]), (wo, W["o"]))]
        if norm:
            loads += [(gain[:, :], vec(norm[0])), (bias[:, :], vec(norm[1]))]
        LOADED = 16 * len(loads)
        VTILES = CHUNKS + (1 if halo else 0)
        PRE = SGROUPS if norm else 0
        NORMS = PRE + CHUNKS
        made_steps = []

        @block.sync
        def _(sp):
            with nc.allow_non_contiguous_dma(reason="vectors onto partitions, once"):
                for dst, src in loads:
                    sp.dma_start(dst, src).then_inc(S["w_in"], 16)
            sp.wait_ge(S["w_in"], LOADED)

        @block.gpsimd
        def _(pool):
            g = nc.gpsimd
            made = Steps(pool, S["made"])
            made.chain(g.memset(identb[:, :], 0.0))
            made.chain(g.affine_select(out=identb[:, :], in_=identb[:, :], compare_op=ALU.not_equal, fill=1.0, base=0,
                                       pattern=[[-1, P]], channel_multiplier=1))
            made.chain(g.memset(expand[:, :, :], 1.0))
            flat = expand[:, :, :].rearrange("h m p -> h (m p)")
            made.chain(g.affine_select(out=flat, in_=flat, compare_op=ALU.is_ge, fill=0.0, base=0,
                                       pattern=[[1, HW]], channel_multiplier=-rows))
            made.chain(g.affine_select(out=flat, in_=flat, compare_op=ALU.is_ge, fill=0.0, base=rows - 1,
                                       pattern=[[-1, HW]], channel_multiplier=rows))
            made.chain(g.memset(band[:, :], 0.0))
            valid(g, made, band)
            made.chain(g.memset(edge[:, :], 0.0))
            made.chain(g.memset(edge[:, 0:shift], -BIG))
            made.chain(g.memset(KT[:, :, 0:shift], 0.0))
            if halo:
                made.chain(g.memset(edge[:, shift + SEQ:], -BIG))
                made.chain(g.memset(KT[:, :, shift + SEQ:], 0.0))
                made.chain(g.memset(xT[:, :, halo + GN:], 0.0))
            else:
                made.chain(g.memset(V[:, 0, :], 0.0))
            g.memset(qs[0][:, :, :], 0.0).then_inc(S["chunk_pv"], 1)
            pool.wait_ge(S["chunk_pv"], 1)
            made_steps.append(made.n)
            pool.wait_ge(S["w_in"], LOADED)
            with pool.Fori(0, BATCH) as b:
                if norm:
                    with pool.Fori(0, SGROUPS) as s:
                        pool.wait_ge(S["var"], b * NORMS + s + 1)
                        g.tensor_tensor(out=rstd[:, :], in0=mv[:, :, 1], in1=K["neghalf"][:, :], op=ALU.pow).then_inc(S["rstd_done"], 1)
                with pool.Fori(0, CHUNKS // 2) as c2:
                    if add:
                        for k in range(2):
                            c = b * CHUNKS + c2 * 2 + k
                            pool.wait_ge(S["x_done"], c)
                            g.tensor_copy(pick[k][:, :], add[1][:, bass.ds(c, 1)]).then_inc(S["picks"], 1)
                    for k in range(2):
                        cc = c2 * 2 + k
                        c = b * CHUNKS + c2 * 2 + k
                        pool.wait_ge(S["proj_out"], 2 * HT * SGROUPS * (b + 1))
                        pool.wait_ge(S["v_out"], VTILES * (b + 1))
                        pool.wait_ge(S["chunk_pv"], c)
                        g.tensor_copy(qs[k][:, :, :], QT[:, :, bass.ds(cc * P, P)]).then_inc(S["q_copied"], 1)
                        g.tensor_copy(vs[k][:, :, :], V[:, bass.ds(cc, 2), :]).then_inc(S["q_copied"], 1)
                        if add:
                            pool.wait_ge(S["picks"], c + 1)
                        g.tensor_tensor(out=mask[k][:, :], in0=band[:, :], in1=edge[:, bass.ds(cc * P, KEYS)],
                                        op=ALU.add).then_inc(S["masked"], 1)
                        if add:
                            g.indirect_dma_start(out=picked[k][:, :], out_offset=None, in_=add[0],
                                                 in_offset=bass.IndirectOffsetOnAxis(ap=pick[k][:, 0:1], axis=0)).then_inc(S[f"picked{k}"], 16)
                    for k in range(2):
                        pool.wait_ge(S["var"], b * NORMS + PRE + c2 * 2 + k + 1)
                        g.tensor_tensor(out=rstd[:, 0:1], in0=mv[:, 0, 1:2], in1=K["neghalf"][:, 0:1], op=ALU.pow).then_inc(S["rstd_done"], 1)

        @block.tensor
        def _(pe):
            t = nc.tensor
            pe.wait_ge(S["w_in"], LOADED)
            pe.wait_ge(S["made"], made_steps[0])

            def values(n, j, first):
                pe.wait_ge(S["v_out"], n - 1) if not first else None
                for hh in range(DH):
                    ins = t.matmul(bank[4 + j % 2][:, :], xT[:, hh, j * P:(j + 1) * P], wv[:, hh, :],
                                   start=(hh == 0), stop=(hh == DH - 1))
                ins.then_inc(S["v_done"], 1)

            with pe.Fori(0, BATCH) as b:
                with pe.Fori(0, SGROUPS) as s:
                    i = b * SGROUPS + s
                    pe.wait_ge(S["xs_full"], i + 1)
                    for hh in range(DH):
                        for j in range(GT):
                            ins = t.transpose(bank[hh][:, j * P:(j + 1) * P], xs[:, j, hh * P:(hh + 1) * P], K["ident"][:, :])
                        ins.then_inc(S["turned"], 1)
                    pe.wait_ge(S["xT_full"], DH * (i + 1))
                    for m in range(2 * HT):
                        w = wq if m < HT else wk
                        pe.wait_ge(S["proj_out"], 2 * HT * i + max(m - 1, 0))
                        for hh in range(DH):
                            ins = t.matmul(bank[2 + m % 2][:, :], w[:, hh, (m % HT) * P:(m % HT + 1) * P], xT[:, hh, halo:halo + GN],
                                           start=(hh == 0), stop=(hh == DH - 1))
                        ins.then_inc(S["proj"], 1)
                    for j in range(GT):
                        values(b * VTILES + s * GT + j, j, j < 2)
                if halo:
                    values(b * VTILES + CHUNKS, GT, False)
                with pe.Fori(0, CHUNKS // 2) as c2:
                    def scores(k, p):
                        c = b * CHUNKS + c2 * 2 + k
                        if p >= 3:
                            pe.wait_ge(S["exped"], c * pairs + p - 2)
                        t.matmul(score[p % 3][:, :], identb[:, :], mask[k][:, :].unsqueeze(1).to_broadcast([P, 2, KEYS]),
                                 start=True, stop=False)
                        for a in range(2):
                            m, base = block_of(p, a), p % per * rows
                            ins = t.matmul(score[p % 3][:, a * KEYS:(a + 1) * KEYS], qs[k][base:base + rows, m, :],
                                           ks[k][base:base + rows, m, :], start=False, stop=(a == 1), tile_position=(base, 0))
                        ins.then_inc(S["scored"], 1)

                    def turns(k, p):
                        c = b * CHUNKS + c2 * 2 + k
                        pe.wait_ge(S["exped"], c * pairs + p + 1)
                        if p >= 2:
                            pe.wait_ge(S["probT_full"], c * pairs + p - 1)
                        for a in range(2):
                            for kt in range(2):
                                ins = t.transpose(turned[p % 2][:, (2 * a + kt) * P:(2 * a + kt + 1) * P],
                                                  prob[p % 3][:, a, kt * P:(kt + 1) * P], K["ident"][:, :])
                        ins.then_inc(S["prob_turned"], 1)

                    def mixes(k, p):
                        c = b * CHUNKS + c2 * 2 + k
                        pe.wait_ge(S["probT_full"], c * pairs + p + 1)
                        for a in range(2):
                            h, m, base = head(p, a), block_of(p, a), p % per * rows
                            for kt in range(2):
                                ins = t.matmul(outT[k][base:base + rows, m * P:(m + 1) * P], vs[k][:, kt, h * rows:(h + 1) * rows],
                                               probT[p % 2][:, 2 * a + kt, :], start=(kt == 0), stop=(kt == 1), tile_position=(0, base))
                        ins.then_inc(S["outT_done"], 1)
                        if p == pairs - 1:
                            t.matmul(small[:, 0:2], K["ident"][:, :], K["ident"][:, 0:2], start=True, stop=True)\
                             .then_inc(S["chunk_pv"], 1)

                    def finish(k):
                        c = b * CHUNKS + c2 * 2 + k
                        pe.wait_ge(S["inv_done"], c + 1)
                        pe.wait_ge(S["y_done"], c)
                        t.transpose(small[0:heads, 0:P], inv[:, :], K["ident"][:, :]).then_inc(S["inv_turned"], 1)
                        pe.wait_ge(S["invT_full"], c + 1)
                        for m in range(HT):
                            ins = t.matmul(small[:, m * P:(m + 1) * P], expand[:, m, :], invT[:, :], start=True, stop=True)
                        ins.then_inc(S["spread"], 1)
                        pe.wait_ge(S["mixed_full"], c + 1)
                        for m in range(HT):
                            ins = t.matmul(small[:, 0:D], mixed[:, m, :], wo[:, m, :], start=(m == 0), stop=(m == HT - 1))
                        ins.then_inc(S["out_done"], 1)

                    for k in range(2):
                        c = b * CHUNKS + c2 * 2 + k
                        pe.wait_ge(S["q_copied"], 2 * (c + 1))
                        pe.wait_ge(S["k_copied"], c + 1)
                        pe.wait_ge(S["masked"], c + 1)
                        scores(k, 0)
                        scores(k, 1)
                        if k == 1:
                            finish(0)
                        for p in range(pairs):
                            if p + 2 < pairs:
                                scores(k, p + 2)
                            turns(k, p)
                            if p >= 1:
                                mixes(k, p - 1)
                        mixes(k, pairs - 1)
                    finish(1)

        @block.scalar
        def _(act):
            a_ = nc.scalar
            act.wait_ge(S["w_in"], LOADED)
            act.wait_ge(S["made"], made_steps[0])
            with act.Fori(0, BATCH) as b:
                with act.Fori(0, SGROUPS) as s:
                    i = b * SGROUPS + s
                    if halo:
                        act.wait_ge(S["halo"], i + b + 1)
                    for hh in range(DH):
                        act.wait_ge(S["turned"], DH * i + hh + 1)
                        dst = xT[:, hh, halo:halo + GN]
                        if norm:
                            ins = a_.activation(dst, bank[hh][:, :], ACT.Identity, scale=gain[:, hh:hh + 1], bias=bias[:, hh:hh + 1])
                        else:
                            ins = a_.activation(dst, bank[hh][:, :], ACT.Copy)
                        ins.then_inc(S["xT_full"], 1)
                    for m in range(2 * HT):
                        act.wait_ge(S["proj"], 2 * HT * i + m + 1)
                        if m < HT:
                            ins = a_.activation(QT[:, m, bass.ds(s * GN, GN)], bank[2 + m % 2][:, :], ACT.Copy, scale=scale)
                        else:
                            ins = a_.activation(KT[:, m - HT, bass.ds(s * GN + shift, GN)], bank[2 + m % 2][:, :], ACT.Copy)
                        ins.then_inc(S["proj_out"], 1)
                act.wait_ge(S["proj_out"], 2 * HT * SGROUPS * (b + 1))
                with act.Fori(0, CHUNKS // 2) as c2:
                    def finish(k):
                        c = b * CHUNKS + c2 * 2 + k
                        act.wait_ge(S["inv_turned"], c + 1)
                        a_.activation(invT[:, :], small[0:heads, 0:P], ACT.Copy).then_inc(S["invT_full"], 1)
                        act.wait_ge(S["spread"], c + 1)
                        a_.activation(invs[:, :, :], small[:, :].rearrange("p (m q) -> p m q", q=P), ACT.Copy).then_inc(S["invs_full"], 1)

                    for k in range(2):
                        c = b * CHUNKS + c2 * 2 + k
                        act.wait_ge(S["chunk_pv"], c)
                        a_.activation(ks[k][:, :, :], KT[:, :, bass.ds((c2 * 2 + k) * P, KEYS)], ACT.Copy).then_inc(S["k_copied"], 1)
                        for p in range(pairs):
                            act.wait_ge(S["maxed"], c * pairs + p + 1)
                            if p >= 3:
                                act.wait_ge(S["prob_turned"], c * pairs + p - 2)
                            if p == 0:
                                act.wait_ge(S["inv_done"], c)
                            for a in range(2):
                                h = head(p, a)
                                ins = a_.activation(prob[p % 3][:, a, :], score[p % 3][:, a * KEYS:(a + 1) * KEYS], ACT.Exp,
                                                    bias=nmax[:, h:h + 1], accum_out=sums[:, h:h + 1])
                            ins.then_inc(S["exped"], 1)
                            if k == 1 and p == 1:
                                finish(0)
                    finish(1)

        @block.vector
        def _(dve):
            v = nc.vector
            dve.wait_ge(S["made"], made_steps[0])
            v.memset(y[:, :], 0.0).then_inc(S["x_done"], 1)
            with dve.Fori(0, BATCH) as b:
                if halo:
                    v.memset(xT[:, :, 0:halo], 0.0).then_inc(S["halo"], 1)
                with dve.Fori(0, SGROUPS) as s:
                    i = b * SGROUPS + s
                    st = Steps(dve, S["dve"], (1 + 2 * GT) if norm else 0, i)
                    dve.wait_ge(S["turned"], DH * i)
                    if norm:
                        xj = lambda j: X[:, bass.ds(i * GT + j, 1), :].rearrange("p a d -> p (a d)")
                        statistics(st, v, xj, stat, mv, rstd, GT)
                        v.tensor_scalar(mv[:, :, 1], mv[:, :, 1], LN_EPS, None, ALU.add).then_inc(S["var"], 1)
                        dve.wait_ge(S["rstd_done"], b * NORMS + s + 1)
                        for j in range(GT):
                            ins = v.tensor_scalar(xs[:, j, :], xj(j), mv[:, j, 0:1], rstd[:, j:j + 1], ALU.subtract, ALU.mult)
                    else:
                        ins = v.tensor_copy(xs[:, :, :], X[:, bass.ds(i * GT, GT), :])
                    ins.then_inc(S["xs_full"], 1)
                    for j in range(GT):
                        dve.wait_ge(S["v_done"], b * VTILES + s * GT + j + 1)
                        v.tensor_copy(V[:, bass.ds(s * GT + j + (0 if halo else 1), 1), :].rearrange("p a d -> p (a d)"),
                                      bank[4 + j % 2][:, :]).then_inc(S["v_out"], 1)
                    if halo:
                        v.tensor_copy(xT[:, :, 0:halo], xT[:, :, GN:GN + halo]).then_inc(S["halo"], 1)
                    st.close()
                if halo:
                    dve.wait_ge(S["v_done"], VTILES * (b + 1))
                    v.tensor_copy(V[:, CHUNKS, :], bank[4 + GT % 2][:, :]).then_inc(S["v_out"], 1)
                with dve.Fori(0, CHUNKS // 2) as c2:
                    st = Steps(dve, S["started"], 2 * (4 if add else 3), b * (CHUNKS // 2) + c2)

                    def maxes(k, p):
                        c = b * CHUNKS + c2 * 2 + k
                        dve.wait_ge(S["scored"], c * pairs + p + 1)
                        v.tensor_reduce(nmax[:, head(p, 0):head(p, 1) + 1:per], score[p % 3][:, :].rearrange("p (a j) -> p a j", j=KEYS), AXX, ALU.max,
                                        negate=True).then_inc(S["maxed"], 1)

                    def copies(k, p):
                        c = b * CHUNKS + c2 * 2 + k
                        dve.wait_ge(S["prob_turned"], c * pairs + p + 1)
                        if p >= 2:
                            dve.wait_ge(S["outT_done"], c * pairs + p - 1)
                        v.tensor_copy(probT[p % 2][:, :, :], turned[p % 2][:, :].rearrange("p (n q) -> p n q", q=P))\
                         .then_inc(S["probT_full"], 1)

                    def finish(k):
                        c = b * CHUNKS + c2 * 2 + k
                        xc = X[:, bass.ds(c, 1), :].rearrange("p a d -> p (a d)")
                        dve.wait_ge(S["exped"], (c + 1) * pairs - 1 + 1)
                        v.reciprocal(inv[:, :], sums[:, :]).then_inc(S["inv_done"], 1)
                        dve.wait_ge(S["invs_full"], c + 1)
                        dve.wait_ge(S["outT_done"], (c + 1) * pairs)
                        v.tensor_tensor(out=mixed[:, :, :], in0=outT[k][:, :].rearrange("p (m q) -> p m q", q=P), in1=invs[:, :, :],
                                        op=ALU.mult).then_inc(S["mixed_full"], 1)
                        dve.wait_ge(S["out_done"], c + 1)
                        ins = v.tensor_tensor(out=y[:, :], in0=small[:, 0:D], in1=xc, op=ALU.add)
                        ins.then_inc(S["y_done"], 1)
                        dve.wait_ge(S["y_done"], c + 1)
                        if add:
                            dve.wait_ge(S[f"picked{k}"], 16 * (b * (CHUNKS // 2) + c2 + 1))
                            st.chain(v.tensor_tensor(out=y[:, :], in0=y[:, :], in1=picked[k][:, :], op=ALU.add))
                        statistics(st, v, lambda j: y[:, :], stat, mv, rstd, 1)
                        v.tensor_scalar(mv[:, 0, 1:2], mv[:, 0, 1:2], LN_EPS, None, ALU.add).then_inc(S["var"], 1)
                        dve.wait_ge(S["rstd_done"], b * NORMS + PRE + c2 * 2 + k + 1)
                        v.tensor_scalar(xc, y[:, :], mv[:, 0, 0:1], rstd[:, 0:1], ALU.subtract, ALU.mult).then_inc(S["x_done"], 1)

                    for k in range(2):
                        maxes(k, 0)
                        maxes(k, 1)
                        if k == 1:
                            finish(0)
                        for p in range(pairs):
                            if p + 2 < pairs:
                                maxes(k, p + 2)
                            copies(k, p)
                    finish(1)
                    st.close()


def sliding_phase(nc, X, K, I):
    def valid(g, made, band):
        made.chain(g.affine_select(out=band[:, :], in_=band[:, :], compare_op=ALU.is_ge, fill=-BIG, base=-1,
                                   pattern=[[1, KEYS]], channel_multiplier=-1))
        made.chain(g.affine_select(out=band[:, :], in_=band[:, :], compare_op=ALU.is_ge, fill=-BIG, base=P,
                                   pattern=[[-1, KEYS]], channel_multiplier=1))

    W = {n: I["L1_attn_W" + n] for n in "qkvo"}
    banded_phase(nc, X, K, "sw", W, heads=16, scale=0.25, shift=P, valid=valid)


LH, DHD = 8, 64
NQ, NKV = 256, 512
QT_, KVT = NQ // P, NKV // P
K_EFF = [min(n * 9 / 8, SEQ) for n in (NQ, NKV)]
ITERS = 50
BT = SEQ // P
PROBLEMS = 2 * BATCH
ROUTES = ((0, QT_), (1, QT_), (2, KVT), (3, KVT))
RANKED = BATCH * (QT_ + KVT)
SLOT = lambda q, blk: q % BATCH * (QT_ + KVT) + (QT_ if q >= BATCH else 0) + blk
KEY_SCALE, KEY_LOW = 2.0 ** -38, 2.0 ** -63
KEY_HIGH = 2.0 ** -31 * (1 - 2.0 ** -24)
DIGITS = 14


def route_block(nc, X, K, I, R):
    T = BT
    with ExitStack() as ctx:
        A = Alloc(nc, ctx, "ro")
        rt, prod = A.sb("rt", [P, 2, D]), A.sb("prod", [P, GT, D])
        s, d, ex = A.sb("s", [P, PROBLEMS, T]), A.sb("d", [P, PROBLEMS, T]), A.sb("ex", [P, PROBLEMS, T])
        part, na, m, mk, lnt = (A.sb(n, [P, PROBLEMS]) for n in ("part", "na", "m", "mk", "lnt"))
        top, diag = A.sb("top", [PROBLEMS, 1]), A.sb("diag", [PROBLEMS, PROBLEMS])
        logk, first = A.sb("logk", [P, PROBLEMS]), A.sb("first", [P, PROBLEMS])
        ones, before = A.sb("ones", [P, P]), A.sb("before", [P, P])
        kneg = A.sb("kneg", [P, PROBLEMS, 4])
        base = A.sb("base", [P, PROBLEMS, T])
        go_on = A.sb("go_on", [P, PROBLEMS, T])
        iota, ptok = A.sb("iota", [P, NKV]), A.sb("ptok", [P, 1])
        score, key = A.sb("score", [P, PROBLEMS, T]), A.sb("key", [P, PROBLEMS, T])
        digit = A.sb("digit", [P, 4], U32)
        cand, kept, cut = A.sb("cand", [P, PROBLEMS, 4]), A.sb("kept", [P, PROBLEMS, 4]), A.sb("cut", [P, PROBLEMS])
        less = A.sb("less", [P, PROBLEMS * 4, T])
        lt, eq, sel, incl, rank = (A.sb(n, [P, PROBLEMS, T]) for n in ("lt", "eq", "sel", "incl", "rank"))
        count = A.sb("count", [P, PROBLEMS * 4])
        vals = A.sb("vals", [P, PROBLEMS, T, 5], BF16)
        zeros = A.sb("zeros", [P, P], BF16)
        hot = [A.sb(f"hot{k}", [P, NKV], BF16) for k in range(2)]
        rows = A.sb("rows", [P, RANKED], U32)
        small, totals, tri, tot = (A.ps(n) for n in ("small", "totals", "tri", "tot"))
        acc = [A.ps(f"acc{k}") for k in range(KVT)]
        S = {n: A.sem(n) for n in ("loaded", "spilled", "made", "dve", "maxed", "max_turned", "max_diag", "max_spread", "shifted", "exped",
                                   "summed", "totalled", "logged", "low", "scored", "counted", "tallied", "flagged", "placed", "ties",
                                   "chosen", "vals_full", "hot_full", "hot_used", "listed", "rows_full", "gathered")}
        xd = R["xd"]
        block = ctx.enter_context(nc.Block())

        @block.sync
        def _(sp):
            for r, n in enumerate(("rt_q", "rt_kv")):
                sp.dma_start(rt[:, r, :], I["L1_ffn_" + n].to_broadcast([P, D])).then_inc(S["loaded"], 16)
            sp.dma_start(xd.rearrange("(t p) d -> p t d", p=P), X[:, :, :]).then_inc(S["spilled"], 16)
            sp.dma_start(R["out"][BATCH * NQ:, :], I["L1_ffn_null_q"].unsqueeze(0)).then_inc(S["spilled"], 16)
            sp.wait_ge(S["loaded"], 32)
            sp.wait_ge(S["spilled"], 32)

        made_steps = []

        @block.gpsimd
        def _(pool):
            g = nc.gpsimd
            made = Steps(pool, S["made"])
            made.then(g.memset(ones[:, :], 1.0))
            made.then(g.memset(zeros[:, :], 0.0))
            made.chain(g.memset(before[:, :], 1.0))
            made.chain(g.affine_select(out=before[:, :], in_=before[:, :], compare_op=ALU.is_gt, fill=0.0, base=0,
                                       pattern=[[1, P]], channel_multiplier=-1))
            for r in range(2):
                half = slice(r * BATCH, (r + 1) * BATCH)
                made.then(g.memset(kneg[:, half, :], -(NQ, NKV)[r] / P))
                made.then(g.memset(logk[:, half], math.log(K_EFF[r])))
                made.then(g.memset(first[:, half], math.log(SEQ / K_EFF[r])))
            for b in range(BATCH):
                made.then(g.memset(base[:, b, :], float(b * NQ - BATCH * NQ)))
            made.chain(g.memset(go_on[:, :, :], 1.0))
            made.chain(g.memset(go_on[:, :, 0:1], 0.0))
            for c in range(4):
                made.then(g.memset(digit[:, c:c + 1], c << 2 * (DIGITS - 1)))
            made.chain(g.iota(iota[:, :], pattern=[[1, NKV]], base=0, channel_multiplier=0, allow_small_or_imprecise_dtypes=True))
            made.chain(g.iota(ptok[:, :], pattern=[[0, 1]], base=0, channel_multiplier=1, allow_small_or_imprecise_dtypes=True))
            for q in range(PROBLEMS):
                made.chain(g.tensor_copy(vals[:, q, :, 3], ptok[:, :].to_broadcast([P, T])))
                made.chain(g.iota(vals[:, q, :, 4], pattern=[[P, T]], base=q % BATCH * SEQ, channel_multiplier=0,
                                  allow_small_or_imprecise_dtypes=True))
            made_steps.append(made.n)
            pool.wait_ge(S["spilled"], 32)
            for q, blocks in ROUTES:
                for blk in range(blocks):
                    n = SLOT(q, blk)
                    pool.wait_ge(S["rows_full"], PROBLEMS)
                    g.indirect_dma_start(out=R["x"][:, n, :], out_offset=None, in_=xd,
                                         in_offset=bass.IndirectOffsetOnAxis(ap=rows[:, n:n + 1], axis=0)).then_inc(S["gathered"], 16)
            pool.wait_ge(S["gathered"], 16 * RANKED)

        @block.tensor
        def _(pe):
            t = nc.tensor
            pe.wait_ge(S["made"], made_steps[0])
            pe.wait_ge(S["maxed"], 1)
            t.transpose(small[0:PROBLEMS, 0:P], part[:, :], K["ident"][:, :]).then_inc(S["max_turned"], 1)
            pe.wait_ge(S["max_diag"], 1)
            t.matmul(small[:, 0:PROBLEMS], ones[0:PROBLEMS, :], diag[:, :], start=True, stop=True).then_inc(S["max_spread"], 1)
            with pe.Fori(0, ITERS - 1) as i:
                pe.wait_ge(S["summed"], i + 1)
                t.matmul(totals[:, 0:PROBLEMS], ones[:, :], part[:, :], start=True, stop=True).then_inc(S["totalled"], 1)
            flat = lambda a: a[:, :, :].rearrange("p q t -> p (q t)")
            with pe.Fori(0, DIGITS) as i:
                pe.wait_ge(S["counted"], i + 1)
                t.matmul(small[:, 0:4 * PROBLEMS], ones[:, :], count[:, :], start=True, stop=False)
                t.matmul(small[:, 0:4 * PROBLEMS], ones[:, :], flat(kneg), start=False, stop=True).then_inc(S["tallied"], 1)
            pe.wait_ge(S["flagged"], 1)
            t.matmul(small[:, 0:PROBLEMS], ones[:, :], part[:, :], start=True, stop=False)
            t.matmul(small[:, 0:PROBLEMS], ones[:, :], kneg[:, :, 0], start=False, stop=True)
            for k, flags in ((1, eq), (2, sel)):
                pe.wait_ge(S["flagged"], k)
                t.matmul(tri[:, 0:PROBLEMS * T], before[:, :], flat(flags), start=True, stop=True)
                t.matmul(tot[:, 0:PROBLEMS * T], ones[:, :], flat(flags), start=True, stop=True).then_inc(S["placed"], 1)
            pe.wait_ge(S["vals_full"], 1)
            for q, blocks in ROUTES:
                for blk in range(blocks):
                    t.matmul(acc[blk][:, 8 * q:8 * q + 5], zeros[:, :], vals[:, q, 0, :], start=True, stop=False)
                if q == 0:
                    ins = t.matmul(acc[KVT - 1][:, 0:5], zeros[:, :], vals[:, 0, 0, :], start=True, stop=True)
                    ins.then_inc(S["hot_used"], 1)
                with pe.Fori(0, T // 2) as t2:
                    for k in range(2):
                        pe.wait_ge(S["hot_full"], q * T + t2 * 2 + k + 1)
                        for blk in range(blocks):
                            ins = t.matmul(acc[blk][:, 8 * q:8 * q + 5], hot[k][:, blk * P:(blk + 1) * P],
                                           vals[:, q, bass.ds(t2 * 2 + k, 1), :].rearrange("p a c -> p (a c)"), start=False, stop=False)
                        ins.then_inc(S["hot_used"], 1)
                for blk in range(blocks):
                    ins = t.matmul(acc[blk][:, 8 * q:8 * q + 5], zeros[:, :], vals[:, q, 0, :], start=False, stop=True)
                ins.then_inc(S["listed"], 1)

        @block.scalar
        def _(act):
            a_ = nc.scalar
            with act.Fori(0, ITERS - 1) as i:
                act.wait_ge(S["shifted"], i + 1)
                a_.activation(ex[:, :, :], d[:, :, :], ACT.Exp).then_inc(S["exped"], 1)
                act.wait_ge(S["totalled"], i + 1)
                a_.activation(lnt[:, :], totals[:, 0:PROBLEMS], ACT.Ln).then_inc(S["logged"], 1)
            act.wait_ge(S["low"], 1)
            a_.activation(score[:, :, :], d[:, :, :], ACT.Exp).then_inc(S["scored"], 1)

        @block.vector
        def _(dve):
            v = nc.vector
            tt = v.tensor_tensor
            wide = lambda a: over(a[:, :], T)
            flat = lambda a: a[:, :, :].rearrange("p q t -> p (q t)")
            dve.wait_ge(S["loaded"], 32)
            tiles = s[:, :, :].rearrange("p (r b) t -> p r (b t)", r=2)
            with dve.Fori(0, GROUPS) as i:
                st = Steps(dve, S["dve"], 4, i)
                for r in range(2):
                    st.chain(tt(out=prod[:, :, :], in0=X[:, bass.ds(i * GT, GT), :], in1=each(rt[:, r, :], GT), op=ALU.mult))
                    st.chain(v.tensor_reduce(tiles[:, r, bass.ds(i * GT, GT)], prod[:, :, :], AXX, ALU.add))
                st.close()
            dve.wait_ge(S["made"], made_steps[0])
            v.tensor_reduce(part[:, :], s[:, :, :], AXX, ALU.max).then_inc(S["maxed"], 1)
            dve.wait_ge(S["max_turned"], 1)
            st = Steps(dve, S["dve"], 0, 0)
            st.base = 4 * GROUPS
            st.chain(v.tensor_reduce(top[:, :], small[0:PROBLEMS, 0:P], AXX, ALU.max))
            v.tensor_scalar(diag[:, :], K["ident"][0:PROBLEMS, 0:PROBLEMS], top[:, 0:1], None, ALU.mult).then_inc(S["max_diag"], 1)
            dve.wait_ge(S["max_spread"], 1)
            st.then(tt(out=s[:, :, :], in0=s[:, :, :], in1=over(small[:, 0:PROBLEMS], T), op=ALU.subtract))
            st.chain(tt(out=na[:, :], in0=first[:, :], in1=small[:, 0:PROBLEMS], op=ALU.subtract))
            start = st.base + st.n
            with dve.Fori(0, ITERS - 1) as i:
                st = Steps(dve, S["dve"], 4, i)
                st.base = start + i * 4
                st.then(tt(out=d[:, :, :], in0=s[:, :, :], in1=wide(na), op=ALU.min))
                st.chain(v.tensor_scalar(m[:, :], na[:, :], 0.0, None, ALU.min))
                tt(out=d[:, :, :], in0=d[:, :, :], in1=wide(m), op=ALU.subtract).then_inc(S["shifted"], 1)
                st.then(tt(out=mk[:, :], in0=m[:, :], in1=logk[:, :], op=ALU.subtract))
                dve.wait_ge(S["exped"], i + 1)
                v.tensor_reduce(part[:, :], ex[:, :, :], AXX, ALU.add).then_inc(S["summed"], 1)
                st.wait()
                dve.wait_ge(S["logged"], i + 1)
                st.chain(tt(out=na[:, :], in0=lnt[:, :], in1=mk[:, :], op=ALU.add))
                st.close()
            st = Steps(dve, S["dve"])
            st.base = start + 4 * (ITERS - 1)
            st.chain(tt(out=s[:, :, :], in0=s[:, :, :], in1=wide(na), op=ALU.subtract))
            v.tensor_scalar(d[:, :, :], s[:, :, :], 0.0, None, ALU.min).then_inc(S["low"], 1)
            st.chain(v.tensor_scalar(key[:, :, :], s[:, :, :], -KEY_SCALE, KEY_LOW, ALU.mult, ALU.max))
            st.chain(v.tensor_scalar(key[:, :, :], key[:, :, :], KEY_HIGH, None, ALU.min))
            st.chain(v.memset(cut[:, :], KEY_LOW))
            start = st.base + st.n
            with dve.Fori(0, DIGITS) as i:
                st = Steps(dve, S["dve"], 5)
                st.base = start + i * 5
                st.chain(tt(out=cand[:, :, :].bitcast(U32), in0=over(cut[:, :].bitcast(U32), 4), in1=each(digit[:, :], PROBLEMS),
                            op=ALU.bitwise_or))
                for c in range(4):
                    ins = tt(out=less[:, c * PROBLEMS:(c + 1) * PROBLEMS, :], in0=key[:, :, :], in1=over(cand[:, :, c], T), op=ALU.is_lt)
                st.chain(ins)
                v.tensor_reduce(count[:, :].rearrange("p (q c) -> p c q", c=4), less[:, :, :].rearrange("p (c q) t -> p c q t", c=4),
                                AXX, ALU.add).then_inc(S["counted"], 1)
                st.then(v.tensor_scalar(digit[:, :], digit[:, :], 2, None, ALU.logical_shift_right))
                dve.wait_ge(S["tallied"], i + 1)
                st.chain(v.scalar_tensor_tensor(out=kept[:, :, :], in0=small[:, 0:4 * PROBLEMS].rearrange("p (q c) -> p q c", c=4),
                                                scalar=0.0, in1=cand[:, :, :], op0=ALU.is_lt, op1=ALU.mult))
                st.chain(v.tensor_reduce(cut[:, :], kept[:, :, :], AXX, ALU.max))
                st.close()
            st = Steps(dve, S["dve"])
            st.base = start + 5 * DIGITS
            st.chain(tt(out=lt[:, :, :], in0=key[:, :, :], in1=wide(cut), op=ALU.is_lt))
            st.chain(v.tensor_reduce(part[:, :], lt[:, :, :], AXX, ALU.add))
            tt(out=eq[:, :, :], in0=key[:, :, :], in1=wide(cut), op=ALU.is_equal).then_inc(S["flagged"], 1)

            def places():
                st.chain(v.tensor_tensor_scan(flat(incl), flat(go_on), tot[:, 0:PROBLEMS * T], 0.0, ALU.mult, ALU.add))
                st.chain(tt(out=flat(rank), in0=flat(incl), in1=tot[:, 0:PROBLEMS * T], op=ALU.subtract))
                st.chain(tt(out=flat(rank), in0=flat(rank), in1=tri[:, 0:PROBLEMS * T], op=ALU.add))

            dve.wait_ge(S["placed"], 1)
            places()
            st.chain(tt(out=rank[:, :, :], in0=rank[:, :, :], in1=over(small[:, 0:PROBLEMS], T), op=ALU.add))
            st.chain(v.scalar_tensor_tensor(out=sel[:, :, :], in0=rank[:, :, :], scalar=0.0, in1=eq[:, :, :], op0=ALU.is_lt, op1=ALU.mult))
            tt(out=sel[:, :, :], in0=sel[:, :, :], in1=lt[:, :, :], op=ALU.add).then_inc(S["flagged"], 1)
            dve.wait_ge(S["scored"], 1)
            st.chain(v.tensor_scalar(d[:, :, :], score[:, :, :], -1.0, 1.0, ALU.mult, ALU.add))
            st.chain(tt(out=d[:, :, :], in0=d[:, :, :], in1=score[:, :, :], op=ALU.add))
            for k in range(3):
                ins = v.tensor_copy(vals[:, :, :, k], d[:, :, :])
                if k < 2:
                    st.chain(ins)
                    st.chain(tt(out=d[:, :, :], in0=d[:, :, :], in1=vals[:, :, :, k], op=ALU.subtract))
            ins.then_inc(S["vals_full"], 1)
            dve.wait_ge(S["flagged"], 2)
            dve.wait_ge(S["placed"], 2)
            places()
            nq = slice(0, BATCH)
            st.chain(tt(out=incl[:, nq, :], in0=rank[:, nq, :], in1=base[:, nq, :], op=ALU.add))
            st.chain(tt(out=incl[:, nq, :], in0=incl[:, nq, :], in1=sel[:, nq, :], op=ALU.mult))
            st.then(v.tensor_scalar(R["pick"][:, :], incl[:, nq, :].rearrange("p b t -> p (b t)"), float(BATCH * NQ), None, ALU.add))
            st.chain(v.scalar_tensor_tensor(out=rank[:, :, :], in0=rank[:, :, :], scalar=1.0, in1=sel[:, :, :], op0=ALU.add, op1=ALU.mult))
            st.chain(v.tensor_scalar(rank[:, :, :], rank[:, :, :], -1.0, None, ALU.add))
            for q, blocks in ROUTES:
                with dve.Fori(0, T // 2) as t2:
                    for k in range(2):
                        n = q * T + t2 * 2 + k
                        dve.wait_ge(S["hot_used"], n)
                        v.tensor_scalar(hot[k][:, 0:blocks * P], iota[:, 0:blocks * P], rank[:, q, bass.ds(t2 * 2 + k, 1)], None,
                                        ALU.is_equal).then_inc(S["hot_full"], 1)
            dve.wait_ge(S["listed"], PROBLEMS)
            for q, blocks in ROUTES:
                for blk in range(blocks):
                    n = SLOT(q, blk)
                    st.then(v.tensor_reduce(R["score"][:, n:n + 1], acc[blk][:, 8 * q:8 * q + 3], AXX, ALU.add))
                    with nc.allow_low_precision(reason="whole numbers"):
                        ins = v.tensor_reduce(rows[:, n:n + 1], acc[blk][:, 8 * q + 3:8 * q + 5], AXX, ALU.add)
                ins.then_inc(S["rows_full"], 1)


def heavy_block(nc, X, K, I, R):
    w = lambda n: I["L1_ffn_" + n]
    RT = QT_ + KVT
    with ExitStack() as ctx:
        A = Alloc(nc, ctx, "he")
        wq, wk, wv = (A.sb(n, [P, DH, HW]) for n in ("wq", "wk", "wv"))
        wo, gain = A.sb("wo", [P, HT, D]), A.sb("gain", [P, DH])
        nkey, nval = A.sb("nkey", [P, HT, 2]), A.sb("nval", [LH, HW])
        expand = A.sb("expand", [LH, HT, P])
        stat, mv, rstd = A.sb("stat", [P, RT, 6]), A.sb("mv", [P, RT, 2]), A.sb("rstd", [P, RT])
        half = A.sb("half", [P, RT])
        xs = A.sb("xs", [P, RT, D])
        qT, kvT = A.sb("qT", [P, DH, NQ]), A.sb("kvT", [P, DH, NKV])
        Q, KK, V = A.sb("Q", [P, HT, NQ]), A.sb("K", [P, HT, NKV]), A.sb("V", [P, KVT, HW])
        prob = [A.sb(f"prob{k}", [P, NKV]) for k in range(3)]
        probT = [A.sb(f"probT{k}", [P, KVT, P]) for k in range(2)]
        nsim, nmax, sums, nprob, inv = (A.sb(n, [P, LH]) for n in ("nsim", "nmax", "sums", "nprob", "inv"))
        nprobT, invT = A.sb("nprobT", [LH, P]), A.sb("invT", [LH, P])
        invs, mixed = A.sb("invs", [P, HT, P]), A.sb("mixed", [P, HT, P])
        y = [A.sb(f"y{k}", [P, D]) for k in range(QT_)]
        bank = [A.ps(f"bank{k}") for k in range(8)]
        score, turned, outT, nullT, small = bank[0:3], bank[3:5], bank[5], bank[6], bank[7]
        S = {n: A.sem(n) for n in (
            "w_in", "zeroed", "made", "dve", "var", "rstd_done", "xs_full", "turned", "xT_full", "q_done", "q_out", "k_done", "k_out", "v_done",
            "v_out", "null_scored", "null_out", "scored", "maxed", "exped", "prob_turned", "probT_full", "outT_done", "null_shift",
            "null_exped", "inv_done", "nprob_turned", "nprobT_full", "inv_turned", "invT_full", "null_mixed", "invs_used", "spread", "invs_full",
            "mixed_full", "out_done", "y_full", "stored")}
        block = ctx.enter_context(nc.Block())
        w_kv = w("w_kv_h").rearrange("(h p) e c -> p h e c", p=P)
        heads_of = lambda a: a[:, :, :].rearrange("p h (e c) -> p h e c", c=DHD)
        loads = [(wq[:, :, :], w("w_q_h").rearrange("(h p) e -> p h e", p=P))]
        loads += [(heads_of(wk)[:, hh], w_kv[:, hh, :, 0:DHD]) for hh in range(DH)]
        loads += [(heads_of(wv)[:, hh], w_kv[:, hh, :, DHD:]) for hh in range(DH)]
        loads += [(wo[:, :, :], w("w_out_h").rearrange("(h p) e -> p h e", p=P)),
                  (gain[:, :], w("rms_g").rearrange("(h p) -> p h", p=P))]
        loads += [(nkey[DHD * a:DHD * (a + 1), :, a], w("null_kv")[0].rearrange("(m a) d -> a d m", a=2)[a]) for a in range(2)]
        loads += [(nval[h:h + 1, h * DHD:(h + 1) * DHD], w("null_kv")[1, h:h + 1, :]) for h in range(LH)]
        LOADED = 16 * len(loads)
        made_steps = []

        @block.sync
        def _(sp):
            sp.wait_ge(S["zeroed"], 2)
            with nc.allow_non_contiguous_dma(reason="vectors onto partitions, once"):
                for dst, src in loads:
                    sp.dma_start(dst, src).then_inc(S["w_in"], 16)
            sp.wait_ge(S["w_in"], LOADED)
            with sp.Fori(0, BATCH) as b:
                for k in range(QT_):
                    sp.wait_ge(S["y_full"], b * QT_ + k + 1)
                    sp.dma_start(R["out"][bass.ds(b * NQ + k * P, P), :], y[k][:, :]).then_inc(S["stored"], 16)
            sp.wait_ge(S["stored"], 16 * BATCH * QT_)

        @block.gpsimd
        def _(pool):
            g = nc.gpsimd
            g.memset(nkey[:, :, :], 0.0).then_inc(S["zeroed"], 1)
            g.memset(nval[:, :], 0.0).then_inc(S["zeroed"], 1)
            made = Steps(pool, S["made"])
            made.chain(g.memset(half[:, :], -0.5))
            made.chain(g.memset(expand[:, :, :], 1.0))
            flat = expand[:, :, :].rearrange("h m p -> h (m p)")
            made.chain(g.affine_select(out=flat, in_=flat, compare_op=ALU.is_ge, fill=0.0, base=0,
                                       pattern=[[1, HW]], channel_multiplier=-DHD))
            made.chain(g.affine_select(out=flat, in_=flat, compare_op=ALU.is_ge, fill=0.0, base=DHD - 1,
                                       pattern=[[-1, HW]], channel_multiplier=DHD))
            made_steps.append(made.n)
            with pool.Fori(0, BATCH) as b:
                pool.wait_ge(S["var"], b + 1)
                g.tensor_tensor(out=rstd[:, :], in0=mv[:, :, 1], in1=half[:, :], op=ALU.pow).then_inc(S["rstd_done"], 1)

        @block.tensor
        def _(pe):
            t = nc.tensor
            pe.wait_ge(S["w_in"], LOADED)
            pe.wait_ge(S["made"], made_steps[0])
            with pe.Fori(0, BATCH) as b:
                pe.wait_ge(S["xs_full"], b + 1)
                for hh in range(DH):
                    for j in range(QT_):
                        t.transpose(bank[2][:, hh * NQ + j * P:hh * NQ + (j + 1) * P], xs[:, j, hh * P:(hh + 1) * P], K["ident"][:, :])
                    for j in range(KVT):
                        ins = t.transpose(bank[hh][:, j * P:(j + 1) * P], xs[:, QT_ + j, hh * P:(hh + 1) * P], K["ident"][:, :])
                    ins.then_inc(S["turned"], 1)
                pe.wait_ge(S["xT_full"], 2 * DH * (b + 1))
                for m in range(HT):
                    for hh in range(DH):
                        ins = t.matmul(bank[3 + m // 2][:, m % 2 * NQ:(m % 2 + 1) * NQ], wq[:, hh, m * P:(m + 1) * P], qT[:, hh, :],
                                       start=(hh == 0), stop=(hh == DH - 1))
                    if m % 2:
                        ins.then_inc(S["q_done"], 1)
                for m in range(HT):
                    if m >= 2:
                        pe.wait_ge(S["k_out"], HT * b + m - 1)
                    for hh in range(DH):
                        ins = t.matmul(bank[5 + m % 2][:, :], wk[:, hh, m * P:(m + 1) * P], kvT[:, hh, :], start=(hh == 0), stop=(hh == DH - 1))
                    ins.then_inc(S["k_done"], 1)
                for j in range(KVT):
                    if j >= 2:
                        pe.wait_ge(S["v_out"], KVT * b + j - 1)
                    for hh in range(DH):
                        ins = t.matmul(bank[j % 2][:, :], kvT[:, hh, j * P:(j + 1) * P], wv[:, hh, :], start=(hh == 0), stop=(hh == DH - 1))
                    ins.then_inc(S["v_done"], 1)
                pe.wait_ge(S["q_out"], QT_ * (b + 1))
                pe.wait_ge(S["k_out"], HT * (b + 1))
                pe.wait_ge(S["v_out"], KVT * (b + 1))
                for k in range(QT_):
                    c = b * QT_ + k
                    tokens = slice(k * P, (k + 1) * P)

                    def scores(h):
                        if h >= 3:
                            pe.wait_ge(S["exped"], c * LH + h - 2)
                        m, base = h // 2, h % 2 * DHD
                        t.matmul(score[h % 3][:, :], Q[base:base + DHD, m, tokens], KK[base:base + DHD, m, :], start=True, stop=True,
                                 tile_position=(base, 0)).then_inc(S["scored"], 1)

                    def turns(h):
                        pe.wait_ge(S["exped"], c * LH + h + 1)
                        if h >= 2:
                            pe.wait_ge(S["probT_full"], c * LH + h - 1)
                        for kt in range(KVT):
                            ins = t.transpose(turned[h % 2][:, kt * P:(kt + 1) * P], prob[h % 3][:, kt * P:(kt + 1) * P], K["ident"][:, :])
                        ins.then_inc(S["prob_turned"], 1)

                    def mixes(h):
                        pe.wait_ge(S["probT_full"], c * LH + h + 1)
                        m, base = h // 2, h % 2 * DHD
                        for kt in range(KVT):
                            ins = t.matmul(outT[base:base + DHD, m * P:(m + 1) * P], V[:, kt, h * DHD:(h + 1) * DHD], probT[h % 2][:, kt, :],
                                           start=(kt == 0), stop=(kt == KVT - 1), tile_position=(0, base))
                        ins.then_inc(S["outT_done"], 1)

                    if k:
                        pe.wait_ge(S["mixed_full"], c)
                        pe.wait_ge(S["y_full"], c)
                    for m in range(HT):
                        ins = t.matmul(small[:, 2 * m:2 * m + 2], Q[:, m, tokens], nkey[:, m, :], start=True, stop=True)
                    ins.then_inc(S["null_scored"], 1)
                    scores(0)
                    scores(1)
                    for h in range(LH):
                        if h + 2 < LH:
                            scores(h + 2)
                        turns(h)
                        if h >= 1:
                            mixes(h - 1)
                    mixes(LH - 1)
                    pe.wait_ge(S["null_exped"], c + 1)
                    t.transpose(small[0:LH, 0:P], nprob[:, :], K["ident"][:, :]).then_inc(S["nprob_turned"], 1)
                    pe.wait_ge(S["nprobT_full"], c + 1)
                    for m in range(HT):
                        ins = t.matmul(nullT[:, m * P:(m + 1) * P], nval[:, m * P:(m + 1) * P], nprobT[:, :], start=True, stop=True)
                    ins.then_inc(S["null_mixed"], 1)
                    pe.wait_ge(S["inv_done"], c + 1)
                    t.transpose(small[0:LH, 0:P], inv[:, :], K["ident"][:, :]).then_inc(S["inv_turned"], 1)
                    pe.wait_ge(S["invT_full"], c + 1)
                    for m in range(HT):
                        ins = t.matmul(small[:, m * P:(m + 1) * P], expand[:, m, :], invT[:, :], start=True, stop=True)
                    ins.then_inc(S["spread"], 1)
                    pe.wait_ge(S["mixed_full"], c + 1)
                    for m in range(HT):
                        ins = t.matmul(small[:, 0:D], mixed[:, m, :], wo[:, m, :], start=(m == 0), stop=(m == HT - 1))
                    ins.then_inc(S["out_done"], 1)

        @block.scalar
        def _(act):
            a_ = nc.scalar
            act.wait_ge(S["w_in"], LOADED)
            with act.Fori(0, BATCH) as b:
                for hh in range(DH):
                    act.wait_ge(S["turned"], DH * b + hh + 1)
                    a_.activation(kvT[:, hh, :], bank[hh][:, :], ACT.Copy, scale=gain[:, hh:hh + 1]).then_inc(S["xT_full"], 1)
                for hh in range(DH):
                    a_.activation(qT[:, hh, :], bank[2][:, hh * NQ:(hh + 1) * NQ], ACT.Copy, scale=gain[:, hh:hh + 1]).then_inc(S["xT_full"], 1)
                for n in range(2):
                    act.wait_ge(S["q_done"], 2 * b + n + 1)
                    a_.activation(Q[:, 2 * n:2 * n + 2, :], bank[3 + n][:, :].rearrange("p (m q) -> p m q", m=2), ACT.Copy,
                                  scale=DHD ** -0.5).then_inc(S["q_out"], 1)
                for m in range(HT):
                    act.wait_ge(S["k_done"], HT * b + m + 1)
                    a_.activation(KK[:, m, :], bank[5 + m % 2][:, :], ACT.Copy).then_inc(S["k_out"], 1)
                for k in range(QT_):
                    c = b * QT_ + k
                    for h in range(LH):
                        act.wait_ge(S["maxed"], c * LH + h + 1)
                        if h >= 3:
                            act.wait_ge(S["prob_turned"], c * LH + h - 2)
                        a_.activation(prob[h % 3][:, :], score[h % 3][:, :], ACT.Exp, bias=nmax[:, h:h + 1],
                                      accum_out=sums[:, h:h + 1]).then_inc(S["exped"], 1)
                    act.wait_ge(S["null_shift"], c + 1)
                    a_.activation(nprob[:, :], nprob[:, :], ACT.Exp).then_inc(S["null_exped"], 1)
                    act.wait_ge(S["nprob_turned"], c + 1)
                    a_.activation(nprobT[:, :], small[0:LH, 0:P], ACT.Copy).then_inc(S["nprobT_full"], 1)
                    act.wait_ge(S["inv_turned"], c + 1)
                    a_.activation(invT[:, :], small[0:LH, 0:P], ACT.Copy).then_inc(S["invT_full"], 1)
                    act.wait_ge(S["spread"], c + 1)
                    a_.activation(invs[:, :, :], small[:, :].rearrange("p (m q) -> p m q", q=P), ACT.Copy).then_inc(S["invs_full"], 1)

        @block.vector
        def _(dve):
            v = nc.vector
            with dve.Fori(0, BATCH) as b:
                st = Steps(dve, S["dve"], 2 * RT + 3 + QT_ * (LH + 2), b)
                row = lambda j: R["x"][:, bass.ds(b * RT + j, 1), :].rearrange("p a d -> p (a d)")
                statistics(st, v, row, stat, mv, rstd, RT)
                st.chain(v.tensor_tensor(out=mv[:, :, 0], in0=mv[:, :, 0], in1=mv[:, :, 0], op=ALU.mult))
                st.chain(v.tensor_tensor(out=mv[:, :, 0], in0=mv[:, :, 0], in1=mv[:, :, 1], op=ALU.add))
                v.tensor_scalar(mv[:, :, 1], mv[:, :, 0], 1e-24 / D, None, ALU.max).then_inc(S["var"], 1)
                dve.wait_ge(S["rstd_done"], b + 1)
                for j in range(RT):
                    ins = v.tensor_scalar(xs[:, j, :], row(j), rstd[:, j:j + 1], None, ALU.mult)
                ins.then_inc(S["xs_full"], 1)
                for j in range(KVT):
                    dve.wait_ge(S["v_done"], KVT * b + j + 1)
                    v.tensor_scalar(V[:, j, :], bank[j % 2][:, :], R["score"][:, bass.ds(b * RT + QT_ + j, 1)], None,
                                    ALU.mult).then_inc(S["v_out"], 1)
                for k in range(QT_):
                    c = b * QT_ + k
                    dve.wait_ge(S["null_scored"], c + 1)
                    v.tensor_scalar(nsim[:, :], small[:, 0:LH], -1.0, None, ALU.mult).then_inc(S["null_out"], 1)

                    def maxes(h):
                        dve.wait_ge(S["scored"], c * LH + h + 1)
                        st.chain(v.tensor_reduce(nmax[:, h:h + 1], score[h % 3][:, :], AXX, ALU.max, negate=True))
                        if h == 0:
                            dve.wait_ge(S["null_out"], c + 1)
                        v.tensor_tensor(out=nmax[:, h:h + 1], in0=nmax[:, h:h + 1], in1=nsim[:, h:h + 1], op=ALU.min).then_inc(S["maxed"], 1)

                    maxes(0)
                    maxes(1)
                    for h in range(LH):
                        if h + 2 < LH:
                            maxes(h + 2)
                        dve.wait_ge(S["prob_turned"], c * LH + h + 1)
                        if h >= 2:
                            dve.wait_ge(S["outT_done"], c * LH + h - 1)
                        v.tensor_copy(probT[h % 2][:, :, :], turned[h % 2][:, :].rearrange("p (n q) -> p n q", q=P)).then_inc(S["probT_full"], 1)
                    dve.wait_ge(S["maxed"], (c + 1) * LH)
                    v.tensor_tensor(out=nprob[:, :], in0=nmax[:, :], in1=nsim[:, :], op=ALU.subtract).then_inc(S["null_shift"], 1)
                    dve.wait_ge(S["null_exped"], c + 1)
                    st.chain(v.tensor_tensor(out=sums[:, :], in0=sums[:, :], in1=nprob[:, :], op=ALU.add))
                    v.reciprocal(inv[:, :], sums[:, :]).then_inc(S["inv_done"], 1)
                    dve.wait_ge(S["outT_done"], (c + 1) * LH)
                    dve.wait_ge(S["invs_full"], c + 1)
                    both = lambda a: a[:, :].rearrange("p (m q) -> p m q", q=P)
                    st.chain(v.tensor_tensor(out=mixed[:, :, :], in0=both(outT), in1=invs[:, :, :], op=ALU.mult))
                    dve.wait_ge(S["null_mixed"], c + 1)
                    v.tensor_tensor(out=invs[:, :, :], in0=both(nullT), in1=invs[:, :, :], op=ALU.mult).then_inc(S["invs_used"], 1)
                    dve.wait_ge(S["invs_used"], c + 1)
                    v.tensor_tensor(out=mixed[:, :, :], in0=mixed[:, :, :], in1=invs[:, :, :], op=ALU.add).then_inc(S["mixed_full"], 1)
                    dve.wait_ge(S["stored"], 16 * QT_ * b)
                    dve.wait_ge(S["out_done"], c + 1)
                    v.tensor_scalar(y[k][:, :], small[:, 0:D], R["score"][:, bass.ds(b * RT + k, 1)], None, ALU.mult).then_inc(S["y_full"], 1)
                st.close()


def routed_phase(nc, X, K, I):
    w = lambda n: I["L1_ffn_" + n]

    def valid(g, made, band):
        half = P // 2
        made.chain(g.memset(band[0:half, KEYS - half:], -BIG))
        made.chain(g.memset(band[half:P, 0:half], -BIG))

    with ExitStack() as ctx:
        R = {"xd": nc.dram_tensor("x_rows", (TOK, D), F32).ap(), "out": nc.dram_tensor("heavy_rows", (BATCH * NQ + 1, D), F32).ap(),
             "pick": ctx.enter_context(nc.sbuf_tensor("pick", [P, TILES], U32))}
        with ExitStack() as inner:
            R["x"] = inner.enter_context(nc.sbuf_tensor("routed_x", [P, RANKED, D], F32))
            R["score"] = inner.enter_context(nc.sbuf_tensor("routed_score", [P, RANKED], F32))
            route_block(nc, X, K, I, R)
            heavy_block(nc, X, K, I, R)
        qkv = w("w_qkv_l")
        W = {"q": qkv[:, 0:HW], "k": qkv[:, HW:2 * HW], "v": qkv[:, 2 * HW:], "o": w("w_out_l")}
        banded_phase(nc, X, K, "li", W, heads=LH, scale=DHD ** -0.5, shift=P // 2, valid=valid, norm=(w("ln_g"), w("ln_b")),
                     add=(R["out"], R["pick"]))


def lay_out(inputs, np):
    a = {k: np.asarray(v) for k, v in inputs.items()}
    for name in ("L0_attn_in_proj_w", "L0_attn_x_proj_w", "L0_attn_dt_proj_w", "L0_attn_out_proj_w", "L0_attn_fc1_w",
                 "L0_attn_fc2_w", "L0_attn_fc3_w"):
        a[name] = a[name].T
    a["L0_attn_x_proj_w"] = np.concatenate([a["L0_attn_x_proj_w"][:, RANK:], a["L0_attn_x_proj_w"][:, :RANK]], axis=1)
    for name in ("L1_attn_Wq", "L1_attn_Wk", "L1_attn_Wv"):
        heads = a[name].T.reshape(D, 16, 16)
        a[name] = np.concatenate([heads, np.zeros_like(heads)], axis=2).reshape(D, HW)
    heads = a["L1_attn_Wo"].T.reshape(16, 16, D)
    a["L1_attn_Wo"] = np.concatenate([heads, np.zeros_like(heads)], axis=1).reshape(HW, D)
    return a


def program(nc, A, out):
    with ExitStack() as ctx:
        X = ctx.enter_context(nc.sbuf_tensor("X", [P, TILES, D], F32))
        K = {"ident": ctx.enter_context(nc.sbuf_tensor("ident", [P, P], F32)),
             "neghalf": ctx.enter_context(nc.sbuf_tensor("neghalf", [P, GT], F32))}
        with nc.sbuf_tensor("sel", [96, 32, P], BF16) as K["sel"]:
            load_phase(nc, A["L0_attn_x"], X, K)
            if "A" in PHASES:
                mamba_phase(nc, X, K, A)
            if "B" in PHASES:
                moe_phase(nc, X, K, *(A["L0_ffn_" + n] for n in ("Wr", "Wg", "Wu", "Wd", "Sg", "Su", "Sd", "expert_bias")))
        if "C" in PHASES:
            sliding_phase(nc, X, K, A)
        if "D" in PHASES:
            routed_phase(nc, X, K, A)
        store_phase(nc, X, out)


PHASES = "ABCD"


def kernel(**inputs):
    import numpy as _np
    import concourse.bacc as _bacc
    from concourse import mybir as _mybir
    from concourse.bass_utils import run_bass_kernel_spmd as _run

    nc = _bacc.Bacc("TRN2", target_bir_lowering=False, num_devices=1)
    arrays, args = {}, {}
    for name, a in lay_out(inputs, _np).items():
        arrays[f"in_{name}_dram"] = _np.ascontiguousarray(a)
        args[name] = nc.dram_tensor(f"in_{name}_dram", a.shape, _mybir.dt.from_np(a.dtype), kind="ExternalInput").ap()
    out = nc.dram_tensor("out_0_dram", (BATCH, SEQ, D), F32, kind="ExternalOutput").ap()
    program(nc, args, out)
    r = _run(nc, [arrays], core_ids=[0])
    return r.results[0]["out_0_dram"]
```

```python
import math
from contextlib import ExitStack

import concourse.bass as bass
from concourse import mybir

F32 = mybir.dt.float32
BF16 = mybir.dt.bfloat16
F32R = mybir.dt.float32r
I32 = mybir.dt.int32
U32 = mybir.dt.uint32
ALU = mybir.AluOpType
ACT = mybir.ActivationFunctionType
AXX = mybir.AxisListType.X

P = 128
D = 256
DH = D // P
BATCH, SEQ = 2, 2048
TOK = BATCH * SEQ
TILES = TOK // P
GT = 4
GN = GT * P
GROUPS = TOK // GN
SGROUPS = SEQ // GN
LN_EPS = 1e-5
BIG = 1e30


class Steps:

    def __init__(self, eng, sem, per=0, i=0):
        self.eng, self.sem, self.base, self.per, self.n = eng, sem, i * per, per, 0

    def then(self, ins):
        self.n += 1
        ins.then_inc(self.sem, 1)
        return self.base + self.n

    def wait(self):
        self.eng.wait_ge(self.sem, self.base + self.n)

    def chain(self, ins):
        self.then(ins)
        self.wait()

    def close(self):
        assert self.n == self.per, (self.n, self.per)


class Alloc:

    def __init__(self, nc, ctx, tag):
        self.nc, self.ctx, self.tag, self.sems = nc, ctx, tag, []
        ctx.callback(self.clear)

    def clear(self):
        self.nc.clear_and_free_semaphores(self.sems)
        self.nc.all_engine_barrier()

    def sb(self, name, shape, dt=F32):
        return self.ctx.enter_context(self.nc.sbuf_tensor(f"{self.tag}_{name}", shape, dt))

    def ps(self, name, shape=(P, GN), dt=F32):
        return self.ctx.enter_context(self.nc.psum_tensor(f"{self.tag}_{name}", list(shape), dt))

    def sem(self, name):
        self.sems.append(self.nc.alloc_semaphore(name=f"{self.tag}_{name}"))
        return self.sems[-1]


def over(ap, n):
    return ap.unsqueeze(2).to_broadcast([ap.shape[0], ap.shape[1], n])


def each(ap, n):
    return ap.unsqueeze(1).to_broadcast([ap.shape[0], n, ap.shape[1]])


HIGH_BITS = 0xFFFFF000


def high(v, out, src):
    return v.tensor_scalar(out.bitcast(U32), src.bitcast(U32), HIGH_BITS, None, ALU.bitwise_and)


def low(eng, out, src, high_):
    return eng.tensor_tensor(out=out, in0=src, in1=high_, op=ALU.subtract)


def passes(a, b):
    return ((a[0], b[0]), (a[0], b[1]), (a[1], b[0]))


def statistics(st, v, row_of, stat, mv, rstd, n):
    for j in range(n):
        st.then(v.bn_stats(stat[:, j, :], row_of(j)))
    st.wait()
    st.then(v.memset(rstd[:, 0:n], 1.0))
    for j in range(n):
        st.then(v.bn_aggr(mv[:, j, :], stat[:, j, :]))
    st.wait()


def normalize(st, v, y, stat, mv, rstd, S, turn, i, X):
    statistics(st, v, lambda j: y[:, j, :], stat, mv, rstd, GT)
    v.tensor_scalar(mv[:, :, 1], mv[:, :, 1], LN_EPS, None, ALU.add).then_inc(S["var"], 1)
    st.eng.wait_ge(S["rstd_done"], turn)
    for j in range(GT):
        st.then(v.tensor_scalar(X[:, bass.ds(i * GT + j, 1), :].rearrange("p a d -> p (a d)"), y[:, j, :], mv[:, j, 0:1],
                                rstd[:, j:j + 1], ALU.subtract, ALU.mult))
    st.wait()


def load_rows(sp, x, X, groups):
    tiles = slice(groups.start * GT, groups.stop * GT)
    return sp.dma_start(X[:, tiles, :], x.rearrange("b (t p) d -> p (b t) d", p=P)[:, tiles, :])


def constants_phase(nc, K):
    with ExitStack() as ctx:
        A = Alloc(nc, ctx, "co")
        made = A.sem("made")
        block = ctx.enter_context(nc.Block())

        @block.gpsimd
        def _(pool):
            st = Steps(pool, made)
            nc.gpsimd.memset(K["neghalf"][:, :], -0.5)
            st.then(nc.gpsimd.memset(K["ident"][:, :], 0.0))
            st.chain(nc.gpsimd.memset(K["sel"][:, :], 0.0))
            st.chain(nc.gpsimd.affine_select(out=K["ident"][:, :], in_=K["ident"][:, :], compare_op=ALU.not_equal,
                                            fill=1.0, base=0, pattern=[[-1, P]], channel_multiplier=1))
            for part in range(3):
                s = K["sel"][32 * part:32 * part + 32, :]
                st.chain(nc.gpsimd.affine_select(out=s, in_=s, compare_op=ALU.not_equal, fill=1.0, base=0,
                                                pattern=[[-1, 32]], channel_multiplier=1))




DI = 2 * D
MB = DI // P
NS = 16
CONV = 4
RANK = D // 16
HID = 2 * D
HB = HID // P
RMS_EPS = 1e-6


def split3(st, v, src, rest, part, dst, rows):
    st.chain(v.tensor_copy(dst[0:rows, :], src))
    st.chain(v.tensor_tensor(out=rest, in0=src, in1=dst[0:rows, :], op=ALU.subtract))
    st.then(v.tensor_copy(dst[32:32 + rows, :], rest))
    st.chain(v.tensor_copy(part, rest))
    st.chain(v.tensor_tensor(out=rest, in0=rest, in1=part, op=ALU.subtract))
    return v.tensor_copy(dst[64:64 + rows, :], rest)


def mean_square(st, v, x_of, stat, mv, rstd):
    statistics(st, v, x_of, stat, mv, rstd, GT)
    st.chain(v.tensor_tensor(out=mv[:, :, 0], in0=mv[:, :, 0], in1=mv[:, :, 0], op=ALU.mult))
    st.chain(v.tensor_tensor(out=mv[:, :, 0], in0=mv[:, :, 0], in1=mv[:, :, 1], op=ALU.add))
    return v.tensor_scalar(mv[:, :, 1], mv[:, :, 0], RMS_EPS, None, ALU.add)


def mamba_phase(nc, X, K, I):
    with ExitStack() as ctx:
        A = Alloc(nc, ctx, "ma")
        w = lambda n: I["L0_attn_" + n]
        w_in = A.sb("w_in", [P, DH, 2 * DI])
        w_x, w_dt = A.sb("w_x", [P, MB, 48]), A.sb("w_dt", [48, DI])
        w_out = A.sb("w_out", [P, MB, D])
        w_fc1, w_fc2, w_fc3 = A.sb("w_fc1", [P, DH, HID]), A.sb("w_fc2", [P, HB, HID]), A.sb("w_fc3", [P, HB, D])
        rms1, rms2 = A.sb("rms1", [P, DH]), A.sb("rms2", [P, DH])
        conv_w, conv_b = A.sb("conv_w", [P, MB, CONV]), A.sb("conv_b", [P, MB])
        dt_b, skip = A.sb("dt_b", [P, MB]), A.sb("skip", [P, MB])
        a_neg = A.sb("a_neg", [P, MB, NS])
        b_fc1, b_fc2 = A.sb("b_fc1", [P, HB]), A.sb("b_fc2", [P, HB])
        b_fc3, one_row = w_dt[0:1, 0:D], w_dt[0:1, D:D + P]
        diag_skip = A.sb("diag_skip", [P, MB, P])
        goes_on = A.sb("goes_on", [P, GROUPS + 1])
        ln_one = A.sb("ln_one", [P, 1])
        xs, xT = A.sb("xs", [P, GT, D]), A.sb("xT", [P, DH, GN])
        ubuf = A.sb("ubuf", [P, MB, CONV - 1 + GN])
        u, gz = A.sb("u", [P, MB, GN]), A.sb("gz", [P, MB, GN])
        dt, wdt = A.sb("dt", [P, MB, GN]), A.sb("wdt", [P, MB, GN])
        bcp = A.sb("bcp", [96, GN], BF16)
        ramp = A.sb("ramp", [P, MB, GN])
        h1, h2 = A.sb("h1", [P, HB, GN]), A.sb("h2", [P, HB, GN])
        decay = [A.sb(f"decay{k}", [P, MB, GN]) for k in range(3)]
        state = [A.sb(f"state{k}", [P, MB, GN]) for k in range(3)]
        read = [A.sb(f"read{k}", [P, MB, GN]) for k in range(2)]
        cs = [A.sb(f"cs{k}", [P, GN]) for k in range(2)]
        last = A.sb("last", [P, NS, MB])
        norms = [(A.sb(f"stat{k}", [P, GT, 6]), A.sb(f"mv{k}", [P, GT, 2]), A.sb(f"rstd{k}", [P, GT])) for k in range(3)]
        dbc, bcp_next = xs[0:48, 0:2, :].rearrange("p j d -> p (j d)"), xs[0:96, 2, :].bitcast(BF16)
        ex, ln = h1, h2
        rest, part = ex[0:32, 0, :], ex[0:32, 1, 0:GN // 2].bitcast(BF16)
        conv = ramp
        acc = A.ps("acc", (P, MB * GN))
        accs = lambda m: acc[:, m * GN:(m + 1) * GN]
        spread_b, spread_c = A.ps("spread_b"), A.ps("spread_c")
        bank = [A.ps(f"bank{k}") for k in range(2)]
        S = {n: A.sem(n) for n in (
            "x_first", "x_rest", "w_in", "a_exp", "ln_one", "a_neg", "made", "diags", "front", "scan", "tail",
            "var1", "rstd1_done", "xs1_full", "turned1", "xT1_full", "halo", "u_proj", "u_out", "conv_done", "u_full", "dbc_done", "dbc_out",
            "bc_parts", "dt_raw", "ramp_out", "dt_abs", "ex_done", "w_done", "rest_done", "log_done",
            "dt_done", "wdt_done", "bc_ready", "b_spread", "c_spread", "decay_done", "c_copied", "drive_done", "scan_done", "read_done", "joined", "read_used",
            "gated", "mixed", "x1_full", "x1_added", "z_proj", "z_out", "var2", "rstd2_done", "xs2_full", "turned2", "xT2_full",
            "fc1", "h1_done", "fc2", "h2_done", "fc3", "y_out", "var3", "rstd3_done", "x_done")}
        block = ctx.enter_context(nc.Block())

        vec = lambda a, n: a.rearrange("(m p) -> p m", p=P)
        loads = [(w_in[:, :, :], w("in_proj_w").rearrange("(h p) e -> p h e", p=P)),
                 (w_x[:, :, :], w("x_proj_w").rearrange("(m p) e -> p m e", p=P)),
                 (w_dt[32:48, :], w("dt_proj_w")),
                 (w_out[:, :, :], w("out_proj_w").rearrange("(m p) e -> p m e", p=P)),
                 (w_fc1[:, :, :], w("fc1_w").rearrange("(h p) e -> p h e", p=P)),
                 (w_fc2[:, :, :], w("fc2_w").rearrange("(h p) e -> p h e", p=P)),
                 (w_fc3[:, :, :], w("fc3_w").rearrange("(h p) e -> p h e", p=P)),
                 (rms1[:, :], vec(w("rms1_w"), DH)), (rms2[:, :], vec(w("rms2_w"), DH)),
                 (conv_w[:, :, :], w("conv_w").rearrange("(m p) k -> p m k", p=P)), (conv_b[:, :], vec(w("conv_b"), MB)),
                 (dt_b[:, :], vec(w("dt_proj_b"), MB)), (skip[:, :], vec(w("D_skip"), MB)),
                 (a_neg[:, :, :], w("A_log").rearrange("(m p) n -> p m n", p=P)),
                 (b_fc1[:, :], vec(w("fc1_b"), HB)), (b_fc2[:, :], vec(w("fc2_b"), HB)),
                 (b_fc3, w("fc3_b").unsqueeze(0))]
        LOADED = 16 * len(loads)
        FIRST, LAST = 0, GROUPS - 1
        JOINED = [n for n in range(NS) if n % 3 == 2]
        SUMS = [n for n in range(NS) if n + 1 not in JOINED]
        BUF = [n % 3 for n in range(NS - 1)] + [1]
        last_use = lambda n: max(m for m in range(n) if BUF[m] == BUF[n]) + 1 if n >= 3 else \
            max(m for m in range(NS) if BUF[m] == BUF[n]) + 1 - NS
        xg = lambda i, j: X[:, bass.ds(i * GT + j, 1), :].rearrange("p a d -> p (a d)")

        @block.sync
        def _(sp):
            with nc.allow_non_contiguous_dma(reason="vectors onto partitions, once"):
                load_rows(sp, I["L0_attn_x"], X, range(1)).then_inc(S["x_first"], 16)
                for dst, src in loads:
                    sp.dma_start(dst, src).then_inc(S["w_in"], 16)
                load_rows(sp, I["L0_attn_x"], X, range(1, GROUPS)).then_inc(S["x_rest"], 16)
            sp.wait_ge(S["w_in"], LOADED)
            sp.wait_ge(S["x_first"], 16)
            sp.wait_ge(S["x_rest"], 16)

        @block.gpsimd
        def _(pool):
            g = nc.gpsimd
            made = Steps(pool, S["made"])
            made.then(g.memset(one_row, 1.0))
            made.then(g.memset(last[:, :, :], 0.0))
            made.then(g.memset(ubuf[:, :, GN:], 0.0))
            made.chain(g.memset(goes_on[:, :], 1.0))
            for b in range(BATCH):
                made.chain(g.memset(goes_on[:, b * SGROUPS:b * SGROUPS + 1], 0.0))

            def powers(k, name, i):
                pool.wait_ge(S["var" + name], i + 1)
                g.tensor_tensor(out=norms[k][2][:, :], in0=norms[k][1][:, :, 1], in1=K["neghalf"][:, :], op=ALU.pow)\
                 .then_inc(S[f"rstd{name}_done"], 1)

            def body(i, tail, front):
                for n in range(NS):
                    pool.wait_ge(S["scan_done"], NS * i + n + 1)
                    pool.wait_ge(S["c_copied"], NS * i + n + 1)
                    if n - 2 in SUMS:
                        pool.wait_ge(S["read_used"], len(SUMS) * i + SUMS.index(n - 2) + 1)
                    elif n >= 2:
                        pool.wait_ge(S["joined"], len(JOINED) * i + JOINED.index(n - 1) + 1)
                    elif tail:
                        pool.wait_ge(S["read_used"], len(SUMS) * i - 1 + n)
                    g.tensor_tensor(out=read[n % 2][:, :, :], in0=state[BUF[n]][:, :, :], in1=each(cs[n % 2][:, :], MB),
                                    op=ALU.mult).then_inc(S["read_done"], 1)
                    if n in JOINED:
                        pool.wait_ge(S["read_done"], NS * i + n + 1)
                        g.tensor_tensor(out=read[n % 2][:, :, :], in0=read[n % 2][:, :, :], in1=read[(n - 1) % 2][:, :, :],
                                        op=ALU.add).then_inc(S["joined"], 1)
                    if tail and n == 3:
                        adds(i - 1)
                        powers(1, "2", i - 1)
                    if front and n == 5:
                        powers(0, "1", i + 1)
                    if tail and n == 13:
                        powers(2, "3", i - 1)

            def adds(i):
                pool.wait_ge(S["x1_full"], 2 * (i + 1))
                xi = X[:, bass.ds(i * GT, GT), :]
                g.tensor_tensor(out=xi, in0=xi, in1=xs[:, :, :], op=ALU.add).then_inc(S["x1_added"], 1)

            powers(0, "1", 0)
            body(FIRST, False, True)
            with pool.Fori(1, LAST) as i:
                body(i, True, True)
            body(LAST, True, False)
            adds(LAST)
            powers(1, "2", LAST)
            powers(2, "3", LAST)

        @block.tensor
        def _(pe):
            t = nc.tensor
            pe.wait_ge(S["w_in"], LOADED)
            pe.wait_ge(S["made"], 4 + BATCH)

            def turn(name, i):
                pe.wait_ge(S[f"xs{name}_full"], i + 1)
                for hh in range(DH):
                    for j in range(GT):
                        m = t.transpose(bank[hh][:, j * P:(j + 1) * P], xs[:, j, hh * P:(hh + 1) * P], K["ident"][:, :])
                    m.then_inc(S["turned" + name], 1)

            def project(f, ms):
                pe.wait_ge(S["xT1_full"], DH * (f + 1))
                for m in ms:
                    if m >= 2:
                        pe.wait_ge(S["u_out"], MB * f + m - 1)
                    for hh in range(DH):
                        ins = t.matmul(bank[m % 2][:, :], w_in[:, hh, m * P:(m + 1) * P], xT[:, hh, :],
                                       start=(hh == 0), stop=(hh == DH - 1))
                    ins.then_inc(S["u_proj"], 1)

            def project_rows(f, tail=False):
                if tail:
                    pe.wait_ge(S["h2_done"], HB * (f - 1))
                pe.wait_ge(S["u_full"], MB * (f + 1))
                for m in range(MB):
                    ins = t.matmul(bank[0][0:48, :], w_x[:, m, :], u[:, m, :], start=(m == 0), stop=(m == MB - 1))
                ins.then_inc(S["dbc_done"], 1)

            def project_steps(f, tail=False):
                pe.wait_ge(S["dbc_out"], f + 1)
                if tail:
                    pe.wait_ge(S["y_out"], 2 * (f - 1))
                for m in range(MB):
                    if m >= 2:
                        pe.wait_ge(S["dt_abs"], MB * f + m - 1)
                    t.matmul(bank[(m + 1) % 2][:, :], w_dt[32:48, m * P:(m + 1) * P], dbc[32:48, :], start=True, stop=True,
                             tile_position=(32, 0)).then_inc(S["dt_raw"], 1)

            steps_done = lambda i: GROUPS if isinstance(i, int) and i == LAST else i + 2

            def mix(i, k):
                if k == 0:
                    pe.wait_ge(S["dt_abs"], MB * steps_done(i))
                for j in range(2 * k, 2 * k + 2):
                    out = bank[k][:, (j % 2) * D:(j % 2 + 1) * D]
                    for m in range(MB):
                        t.matmul(out, gz[:, m, j * P:(j + 1) * P], w_out[:, m, :], start=(m == 0), stop=False)
                    ins = t.matmul(out, K["ident"][:, :], xg(i, j), start=False, stop=True)
                ins.then_inc(S["mixed"], 1)

            def gates(i, tail, ms):
                if 0 not in ms:
                    pass
                elif tail:
                    pe.wait_ge(S["x1_full"], 2 * i)
                else:
                    pe.wait_ge(S["dt_abs"], MB * (i + 1))
                for m in ms:
                    if m >= 2:
                        pe.wait_ge(S["z_out"], MB * i + m - 1)
                    for hh in range(DH):
                        ins = t.matmul(bank[m % 2][:, :], w_in[:, hh, DI + m * P:DI + (m + 1) * P], xT[:, hh, :],
                                       start=(hh == 0), stop=(hh == DH - 1))
                    ins.then_inc(S["z_proj"], 1)

            def hidden1(i, ms):
                pe.wait_ge(S["xT2_full"], DH * (i + 1))
                for m in ms:
                    if m >= 2:
                        pe.wait_ge(S["h1_done"], HB * i + m - 1)
                    for hh in range(DH):
                        ins = t.matmul(bank[m % 2][:, :], w_fc1[:, hh, m * P:(m + 1) * P], xT[:, hh, :],
                                       start=(hh == 0), stop=(hh == DH - 1))
                    ins.then_inc(S["fc1"], 1)

            def hidden2(i, m, front):
                pe.wait_ge(S["h1_done"], HB * (i + 1))
                if m < 2 and front:
                    pe.wait_ge(S["u_out"], MB * (i + 3))
                elif m >= 2:
                    pe.wait_ge(S["h2_done"], HB * i + m - 1)
                for k in range(HB):
                    ins = t.matmul(bank[m % 2][:, :], w_fc2[:, k, m * P:(m + 1) * P], h1[:, k, :],
                                   start=(k == 0), stop=(k == HB - 1))
                ins.then_inc(S["fc2"], 1)

            def outputs(i, half, front=False):
                if half == 0 and front:
                    pe.wait_ge(S["dbc_out"], i + 3)
                if half:
                    pe.wait_ge(S["h2_done"], HB * (i + 1))
                    pe.wait_ge(S["x1_added"], i + 1)
                for j in range(2 * half, 2 * half + 2):
                    out = bank[j // 2][:, (j % 2) * D:(j % 2 + 1) * D]
                    for k in range(HB):
                        t.matmul(out, h2[:, k, j * P:(j + 1) * P], w_fc3[:, k, :], start=(k == 0), stop=False)
                    t.matmul(out, one_row, b_fc3, start=False, stop=False)
                    ins = t.matmul(out, K["ident"][:, :], xg(i, j), start=False, stop=True)
                    if j % 2:
                        ins.then_inc(S["fc3"], 1)

            def sum_states(i, n):
                if n in JOINED:
                    pe.wait_ge(S["joined"], len(JOINED) * i + JOINED.index(n) + 1)
                else:
                    pe.wait_ge(S["read_done"], NS * i + n + 1)
                for m in range(MB):
                    ins = t.matmul(accs(m), K["ident"][:, :], read[n % 2][:, m, :], start=False, stop=(n == NS - 1))
                ins.then_inc(S["read_used"], 1)

            def body(i, tail, front):
                def spread(n, rows, bank_, free, name):
                    pe.wait_ge(S[free], NS * i + n)
                    t.matmul(bank_[:, :], K["sel"][:, rows + n:rows + n + 1].to_broadcast([96, P]), bcp[:, :], start=True, stop=True)\
                     .then_inc(S[name], 1)

                pe.wait_ge(S["bc_ready"], i + 1)
                spread(0, 0, spread_b, "drive_done", "b_spread")
                spread(0, NS, spread_c, "c_copied", "c_spread")
                if tail:
                    sum_states(i - 1, NS - 2)
                spread(1, 0, spread_b, "drive_done", "b_spread")
                if tail:
                    sum_states(i - 1, NS - 1)

                def starts_sums():
                    pe.wait_ge(S["gated"], i) if tail else pe.wait_ge(S["diags"], MB)
                    for m in range(MB):
                        t.matmul(accs(m), diag_skip[:, m, :], u[:, m, :], start=True, stop=False)

                gaps = {n: ([], []) for n in range(NS)}
                gaps[1][0].append(starts_sums)
                gaps[3][0].append(lambda: gates(i, tail, range(2)))
                gaps[3][1].append(lambda: gates(i, tail, range(2, MB)))
                if tail:
                    gaps[1][1].append(lambda: mix(i - 1, 0))
                    gaps[2][1].append(lambda: mix(i - 1, 1))
                    gaps[5][0].append(lambda: turn("2", i - 1))
                    gaps[6][0].append(lambda: hidden1(i - 1, range(2)))
                    gaps[6][1].append(lambda: hidden1(i - 1, range(2, HB)))
                    for m in range(HB):
                        gaps[9 + m // 2][m % 2].append(lambda m=m: hidden2(i - 1, m, front))
                    gaps[11][0].append(lambda: outputs(i - 1, 1))
                    gaps[12][0].append(lambda: outputs(i - 1, 0, front))
                if front:
                    gaps[7][0].append(lambda: turn_next())
                    gaps[8][0].append(lambda: project(i + 1, range(2)))
                    gaps[8][1].append(lambda: project(i + 1, range(2, MB)))
                    gaps[11][1].append(lambda: project_rows(i + 1, tail))
                    gaps[13][0].append(lambda: project_steps(i + 1, tail))

                def turn_next():
                    pe.wait_ge(S["h1_done"], HB * i) if tail else pe.wait_ge(S["z_out"], MB * (i + 1))
                    turn("1", i + 1)

                for n in range(NS):
                    if n - 2 in SUMS:
                        sum_states(i, n - 2)
                    if n + 1 < NS:
                        spread(n + 1, NS, spread_c, "c_copied", "c_spread")
                    for step in gaps[n][0]:
                        step()
                    if n + 2 < NS:
                        spread(n + 2, 0, spread_b, "drive_done", "b_spread")
                    for step in gaps[n][1]:
                        step()

            turn("1", 0)
            project(0, range(MB))
            project_rows(0)
            project_steps(0)
            body(FIRST, False, True)
            with pe.Fori(1, LAST) as i:
                body(i, True, True)
            body(LAST, True, False)
            sum_states(LAST, NS - 2)
            sum_states(LAST, NS - 1)
            pe.wait_ge(S["gated"], GROUPS)
            mix(LAST, 0)
            mix(LAST, 1)
            pe.wait_ge(S["x1_full"], 2 * GROUPS)
            turn("2", LAST)
            hidden1(LAST, range(HB))
            for m in range(HB):
                hidden2(LAST, m, False)
            for k in (1, 0):
                outputs(LAST, k)

        @block.scalar
        def _(act):
            a = nc.scalar
            LN_SET = "natural_log_exp_and_others"
            a.preload_act_table_set(LN_SET)
            act.wait_ge(S["w_in"], LOADED)
            a.activation(a_neg[:, :, :], a_neg[:, :, :], ACT.Exp).then_inc(S["a_exp"], 1)
            act.wait_ge(S["made"], 4 + BATCH)
            a.activation(ln_one[:, :], goes_on[:, 1:2], ACT.Ln).then_inc(S["ln_one"], 1)

            def turned(name, gain, i):
                for hh in range(DH):
                    act.wait_ge(S["turned" + name], DH * i + hh + 1)
                    a.activation(xT[:, hh, :], bank[hh][:, :], ACT.Copy, scale=gain[:, hh:hh + 1]).then_inc(S[f"xT{name}_full"], 1)

            def projected(f):
                act.wait_ge(S["halo"], f + 1)
                for m in range(MB):
                    act.wait_ge(S["u_proj"], MB * f + m + 1)
                    a.activation(ubuf[:, m, CONV - 1:], bank[m % 2][:, :], ACT.Copy).then_inc(S["u_out"], 1)

            def convolved(f):
                a.preload_act_table_set("silu_and_others")
                for m in range(MB):
                    act.wait_ge(S["conv_done"], MB * f + m + 1)
                    a.activation(u[:, m, :], conv[:, m, :], ACT.Silu).then_inc(S["u_full"], 1)
                a.preload_act_table_set(LN_SET)

            def steps_raw(f):
                act.wait_ge(S["bc_parts"], f + 1)
                act.wait_ge(S["u_full"], MB * (f + 1))
                for m in range(MB):
                    act.wait_ge(S["dt_raw"], MB * f + m + 1)
                    a.activation(ramp[:, m, :], bank[(m + 1) % 2][:, :], ACT.Relu, bias=dt_b[:, m:m + 1]).then_inc(S["ramp_out"], 1)
                    a.activation(ex[:, m, :], bank[(m + 1) % 2][:, :], ACT.Abs, bias=dt_b[:, m:m + 1]).then_inc(S["dt_abs"], 1)

            def steps_exp(f):
                act.wait_ge(S["dt_abs"], MB * (f + 1))
                a.activation(ex[:, :, :], ex[:, :, :], ACT.Exp, scale=-1.0).then_inc(S["ex_done"], 1)

            def steps_one(f):
                act.wait_ge(S["ex_done"], f + 1)
                a.activation(ln[:, :, :], ex[:, :, :], ACT.Identity, bias=1.0).then_inc(S["w_done"], 1)

            def steps_log(f):
                act.wait_ge(S["rest_done"], f + 1)
                a.activation(ln[:, :, :], ln[:, :, :], ACT.Ln).then_inc(S["log_done"], 1)

            def mixed(i, k):
                    act.wait_ge(S["mixed"], 2 * i + k + 1)
                    a.activation(xs[:, 2 * k:2 * k + 2, :], bank[k][:, :].rearrange("p (j d) -> p j d", d=D), ACT.Copy).then_inc(S["x1_full"], 1)

            def outputs(i, k):
                act.wait_ge(S["fc3"], 2 * i + 2 - k)
                a.activation(X[:, bass.ds(i * GT + 2 * k, 2), :], bank[k][:, :].rearrange("p (j d) -> p j d", d=D), ACT.Copy)\
                 .then_inc(S["y_out"], 1)

            def rows_out(f):
                act.wait_ge(S["dbc_done"], f + 1)
                a.activation(dbc, bank[0][0:48, :], ACT.Copy).then_inc(S["dbc_out"], 1)

            def gates(i):
                a.preload_act_table_set("silu_and_others")
                for m in range(MB):
                    act.wait_ge(S["z_proj"], MB * i + m + 1)
                    a.activation(gz[:, m, :], bank[m % 2][:, :], ACT.Silu).then_inc(S["z_out"], 1)
                a.preload_act_table_set(LN_SET)

            def hidden(i, done, h, h_done, bias, ms=range(HB)):
                for m in ms:
                    act.wait_ge(S[done], HB * i + m + 1)
                    a.activation(h[:, m, :], bank[m % 2][:, :], ACT.Relu, bias=bias[:, m:m + 1]).then_inc(S[h_done], 1)

            def body(i, tail, front):
                def decays(n):
                    if n >= 3 or tail:
                        act.wait_ge(S["scan_done"], NS * i + last_use(n))
                    for m in range(MB):
                        ins = a.activation(decay[BUF[n]][:, m, :], dt[:, m, :], ACT.Exp, scale=a_neg[:, m, n:n + 1])
                    ins.then_inc(S["decay_done"], 1)

                def copies(n):
                    act.wait_ge(S["c_spread"], NS * i + n + 1)
                    if n >= 2 or tail:
                        act.wait_ge(S["read_done"], NS * i + n - 1)
                    a.activation(cs[n % 2][:, :], spread_c[:, :], ACT.Copy).then_inc(S["c_copied"], 1)

                copies(0)
                act.wait_ge(S["dt_done"], i + 1)
                decays(0)
                decays(1)
                for n in range(NS):
                    if n:
                        copies(n)
                    if n + 2 < NS:
                        decays(n + 2)
                    if tail and n in (1, 2):
                        mixed(i - 1, n - 1)
                    if n == 3:
                        gates(i)
                    if tail and n == 5:
                        turned("2", rms2, i - 1)
                    if tail and n == 6:
                        hidden(i - 1, "fc1", h1, "h1_done", b_fc1)
                    if front and n == 7:
                        turned("1", rms1, i + 1)
                    if front and n == 8:
                        projected(i + 1)
                    if tail and n == 9:
                        hidden(i - 1, "fc2", h2, "h2_done", b_fc2, range(2))
                    if tail and n == 10:
                        hidden(i - 1, "fc2", h2, "h2_done", b_fc2, range(2, HB))
                    if front and n == 11:
                        convolved(i + 1)
                    if tail and n == 11:
                        outputs(i - 1, 1)
                    if front and n == 11:
                        rows_out(i + 1)
                    if tail and n == 12:
                        outputs(i - 1, 0)
                    if front and n == 13:
                        steps_raw(i + 1)
                        steps_exp(i + 1)
                        steps_one(i + 1)
                    if front and n == 14:
                        steps_log(i + 1)

            turned("1", rms1, 0)
            projected(0)
            convolved(0)
            rows_out(0)
            steps_raw(0)
            steps_exp(0)
            steps_one(0)
            steps_log(0)
            act.wait_ge(S["a_neg"], 1)
            body(FIRST, False, True)
            with act.Fori(1, LAST) as i:
                body(i, True, True)
            body(LAST, True, False)
            mixed(LAST, 0)
            mixed(LAST, 1)
            turned("2", rms2, LAST)
            hidden(LAST, "fc1", h1, "h1_done", b_fc1)
            hidden(LAST, "fc2", h2, "h2_done", b_fc2)
            for k in (1, 0):
                outputs(LAST, k)

        @block.vector
        def _(dve):
            v = nc.vector
            flat = lambda a: a[:, :, :].rearrange("p m t -> p (m t)")
            FRONT, SCAN, TAIL = 16 + MB * (CONV - 1), NS + 1, 20

            def norm(st, k, name, i, x_of):
                stat, mv, rstd = norms[k]
                mean_square(st, v, x_of, stat, mv, rstd).then_inc(S["var" + name], 1)

            def scaled(k, name, i, x_of):
                dve.wait_ge(S[f"rstd{name}_done"], i + 1)
                if name == "2":
                    dve.wait_ge(S["x1_added"], i + 1)
                for j in range(GT):
                    ins = v.tensor_scalar(xs[:, j, :], x_of(j), norms[k][2][:, j:j + 1], None, ALU.mult)
                ins.then_inc(S[f"xs{name}_full"], 1)

            def carry(f):
                dve.wait_ge(S["conv_done"], MB * f)
                v.tensor_scalar(ubuf[:, :, 0:CONV - 1], ubuf[:, :, GN:GN + CONV - 1], goes_on[:, bass.ds(f, 1)], None,
                                ALU.mult).then_inc(S["halo"], 1)

            def convolve(st, f, ms):
                for m in ms:
                    dve.wait_ge(S["u_out"], MB * f + m + 1)
                    st.then(v.tensor_scalar(conv[:, m, :], ubuf[:, m, CONV - 1:], conv_w[:, m, CONV - 1:CONV], conv_b[:, m:m + 1],
                                            ALU.mult, ALU.add))
                for k in range(CONV - 1):
                    st.wait()
                    for m in ms:
                        ins = v.scalar_tensor_tensor(out=conv[:, m, :], in0=ubuf[:, m, k:k + GN], scalar=conv_w[:, m, k:k + 1],
                                                     in1=conv[:, m, :], op0=ALU.mult, op1=ALU.add)
                        st.then(ins) if k < CONV - 2 else ins.then_inc(S["conv_done"], 1)

            def parts(st, f):
                dve.wait_ge(S["dbc_out"], f + 1)
                dve.wait_ge(S["bc_ready"], f)
                split3(st, v, dbc[0:32, :], rest, part, bcp_next, 32).then_inc(S["bc_parts"], 1)

            def rests(f):
                dve.wait_ge(S["w_done"], f + 1)
                v.scalar_tensor_tensor(out=flat(ex), in0=flat(ln), scalar=1.0, in1=flat(ex), op0=ALU.subtract, op1=ALU.subtract)\
                 .then_inc(S["rest_done"], 1)

            def starts(st, i):
                dve.wait_ge(S["bc_parts"], i + 1)
                dve.wait_ge(S["b_spread"], NS * i)
                dve.wait_ge(S["c_spread"], NS * i)
                v.tensor_copy(bcp[:, :], bcp_next).then_inc(S["bc_ready"], 1)
                dve.wait_ge(S["log_done"], i + 1)
                dve.wait_ge(S["rest_done"], i + 1)
                st.chain(v.scalar_tensor_tensor(out=flat(ln), in0=flat(ln), scalar=ln_one[:, 0:1], in1=flat(ex),
                                                op0=ALU.subtract, op1=ALU.subtract))
                dve.wait_ge(S["decay_done"], NS * i)
                v.tensor_tensor(out=flat(dt), in0=flat(ramp), in1=flat(ln), op=ALU.add).then_inc(S["dt_done"], 1)
                dve.wait_ge(S["dt_done"], i + 1)
                v.tensor_tensor(out=flat(wdt), in0=flat(dt), in1=flat(u), op=ALU.mult).then_inc(S["wdt_done"], 1)
                dve.wait_ge(S["wdt_done"], i + 1)

            def gate(i):
                dve.wait_ge(S["read_used"], len(SUMS) * (i + 1))
                v.tensor_tensor(out=flat(gz), in0=acc[:, :], in1=flat(gz), op=ALU.mult).then_inc(S["gated"], 1)

            def variances(st, i):
                stat, mv, rstd = norms[2]
                dve.wait_ge(S["y_out"], 2 * (i + 1))
                statistics(st, v, lambda j: xg(i, j), stat, mv, rstd, GT)
                v.tensor_scalar(mv[:, :, 1], mv[:, :, 1], LN_EPS, None, ALU.add).then_inc(S["var3"], 1)

            def finished(i):
                stat, mv, rstd = norms[2]
                dve.wait_ge(S["rstd3_done"], i + 1)
                for j in range(GT):
                    ins = v.tensor_scalar(xg(i, j), xg(i, j), mv[:, j, 0:1], rstd[:, j:j + 1], ALU.subtract, ALU.mult)
                ins.then_inc(S["x_done"], 1)

            def body(i, tail, front):
                st = Steps(dve, S["scan"], SCAN, i)
                ts = Steps(dve, S["tail"], TAIL, i - 1) if tail else None
                fs = Steps(dve, S["front"], FRONT, i + 1) if front else None
                starts(st, i)

                def drives(n):
                    dve.wait_ge(S["b_spread"], NS * i + n + 1)
                    if n >= 3 or tail:
                        dve.wait_ge(S["read_done"], NS * i + last_use(n))
                    v.tensor_tensor(out=state[BUF[n]][:, :, :], in0=wdt[:, :, :], in1=each(spread_b[:, :], MB),
                                    op=ALU.mult).then_inc(S["drive_done"], 1)

                def scans(n):
                    dve.wait_ge(S["decay_done"], NS * i + n + 1)
                    dve.wait_ge(S["drive_done"], NS * i + n + 1)
                    st.wait()
                    for m in range(MB):
                        ins = v.tensor_tensor_scan(state[BUF[n]][:, m, :], decay[BUF[n]][:, m, :], state[BUF[n]][:, m, :],
                                                   last[:, n, m:m + 1], ALU.mult, ALU.add)
                    ins.then_inc(S["scan_done"], 1)

                def keeps(n):
                    dve.wait_ge(S["scan_done"], NS * i + n + 1)
                    st.then(v.tensor_scalar(last[:, n, :], state[BUF[n]][:, :, GN - 1], goes_on[:, bass.ds(i + 1, 1)], None, ALU.mult))

                drives(0)
                for n in range(NS):
                    scans(n)
                    if tail and n == 0:
                        gate(i - 1)
                    if n + 1 < NS:
                        drives(n + 1)
                    keeps(n)
                    if front and n == 1:
                        carry(i + 1)
                    if tail and n == 3:
                        dve.wait_ge(S["x1_full"], 2 * i)
                        norm(ts, 1, "2", i - 1, lambda j: xs[:, j, :])
                    if tail and n == 4:
                        scaled(1, "2", i - 1, lambda j: xs[:, j, :])
                    if front and n == 5:
                        if not tail:
                            dve.wait_ge(S["x_rest"], 16)
                        norm(fs, 0, "1", i + 1, lambda j: xg(i + 1, j))
                    if front and n == 6:
                        dve.wait_ge(S["turned2"], DH * i) if tail else None
                        scaled(0, "1", i + 1, lambda j: xg(i + 1, j))
                    if front and n == 8:
                        convolve(fs, i + 1, range(2))
                    if front and n == 9:
                        convolve(fs, i + 1, range(2, MB))
                    if front and n == 12:
                        parts(fs, i + 1)
                    if tail and n == 13:
                        variances(ts, i - 1)
                    if front and n == 14:
                        rests(i + 1)
                    if tail and n == 14:
                        finished(i - 1)
                for s in (st, ts, fs):
                    if s:
                        s.close()

            fs = Steps(dve, S["front"], FRONT, 0)
            dve.wait_ge(S["x_first"], 16)
            norm(fs, 0, "1", 0, lambda j: xg(0, j))
            scaled(0, "1", 0, lambda j: xg(0, j))
            dve.wait_ge(S["a_exp"], 1)
            dve.wait_ge(S["ln_one"], 1)
            v.tensor_scalar(a_neg[:, :, :], a_neg[:, :, :], -1.0, None, ALU.mult).then_inc(S["a_neg"], 1)
            dve.wait_ge(S["made"], 4 + BATCH)
            for m in range(MB):
                v.tensor_scalar(diag_skip[:, m, :], K["ident"][:, :], skip[:, m:m + 1], None, ALU.mult).then_inc(S["diags"], 1)
            carry(0)
            convolve(fs, 0, range(2))
            convolve(fs, 0, range(2, MB))
            parts(fs, 0)
            rests(0)
            fs.close()
            body(FIRST, False, True)
            with dve.Fori(1, LAST) as i:
                body(i, True, True)
            body(LAST, True, False)
            ts = Steps(dve, S["tail"], TAIL, LAST)
            gate(LAST)
            dve.wait_ge(S["x1_full"], 2 * GROUPS)
            norm(ts, 1, "2", LAST, lambda j: xs[:, j, :])
            scaled(1, "2", LAST, lambda j: xs[:, j, :])
            variances(ts, LAST)
            finished(LAST)
            ts.close()


E = 8
FE = 128
FS = 256
UNITS = E + FS // P


def moe_phase(nc, X, K, Wr, Wg, Wu, Wd, Sg, Su, Sd, expert_bias):
    with ExitStack() as ctx:
        A = Alloc(nc, ctx, "moe")
        wr, wg, wu = A.sb("wr", [P, DH, E]), A.sb("wg", [P, DH, UNITS * P]), A.sb("wu", [P, DH, UNITS * P])
        wd, ebias = A.sb("wd", [P, UNITS, D]), A.sb("ebias", [P, E])
        two = lambda n, shape: [A.sb(f"{n}_{part}", shape, F32R) for part in ("high", "low")]
        gates_, ups, downs = two("gate", wg.shape), two("up", wu.shape), two("down", wd.shape)
        x2, h2 = two("x", [P, DH, GN]), two("h", [P, UNITS, GN])
        xraw, raw = A.sb("xraw", [P, DH, GN]), A.sb("raw", [P, 2, GN])
        xg, xT = A.sb("xg", [P, GT, D]), A.sb("xT", [P, DH, GN])
        silu, prod = A.sb("silu", [P, 2, GN]), A.sb("prod", [P, 2, GN])
        logit, eq, key, first, second = (A.sb(n, [P, GT, E]) for n in ("logit", "eq", "key", "first", "second"))
        rank = A.sb("rank", [P, GT, E])
        m1, m2, km, th, p1, p2 = (A.sb(n, [P, GT]) for n in ("m1", "m2", "km", "th", "p1", "p2"))
        rw = A.sb("rw", [P, GT, E])
        rwT, rwp = A.sb("rwT", [E, GN]), A.sb("rwp", [96, GN], BF16)
        rest, part = A.sb("rest", [E, GN]), A.sb("part", [E, GN], BF16)
        y, stat, mv, rstd = A.sb("y", [P, GT, D]), A.sb("stat", [P, GT, 6]), A.sb("mv", [P, GT, 2]), A.sb("rstd", [P, GT])
        turn = [A.ps(f"turn{n}") for n in range(DH)]
        gate, up = [A.ps(f"gate{n}") for n in range(2)], [A.ps(f"up{n}") for n in range(2)]
        lg, spread = A.ps("lg"), A.ps("spread")
        sems = ("w_in", "ready", "xg_full", "turned", "xT_full", "logits", "routing", "splitting", "norming", "gap", "halves", "weights",
                "rwT_turned", "gated", "upped", "silued", "spreaded", "h_done", "out_done", "var", "rstd_done", "y_done", "tanh", "w_high", "w_split", "x_high", "x_split", "h_full", "h_high", "h_split", "h_rounded", "x_rounded", "w_rounded")
        S = {n: A.sem(n) for n in sems}
        W_DMAS = 10
        SPLITS = 6
        order = list(range(E, UNITS)) + list(range(E))
        flat = lambda a: a[:, :, :].rearrange("p a b -> p (a b)")
        piece = lambda a, k: flat(a)[:, k * GN:(k + 1) * GN]
        PIECES = [(piece(w_, k), piece(h_, k), piece(l_, k)) for w_, (h_, l_) in ((wg, gates_), (wu, ups), (wd, downs))
                  for k in range(UNITS * D // GN)]
        FIRST_PIECES, LAST_PIECES = range(2 * len(PIECES) // 3), range(2 * len(PIECES) // 3, len(PIECES))
        block = ctx.enter_context(nc.Block())

        @block.sync
        def _(sp):
            loads = [(wr[:, :, :], Wr.rearrange("(h p) e -> p h e", p=P)),
                     (wd[:, 0:E, :], Wd.rearrange("e f d -> f e d")),
                     (wd[:, E:UNITS, :], Sd.rearrange("(u f) d -> f u d", f=P)),
                     (ebias[:, :], expert_bias.unsqueeze(0).to_broadcast([P, E]))]
            for dst, routed, shared in ((wg, Wg, Sg), (wu, Wu, Su)):
                loads.append((dst[:, :, E * P:], shared.rearrange("(h p) f -> p h f", p=P)))
                for hh in range(DH):
                    loads.append((dst[:, hh, 0:E * P].rearrange("p (e f) -> p e f", e=E),
                                  routed[:, hh * P:(hh + 1) * P, :].rearrange("e p f -> p e f")))
            assert len(loads) == W_DMAS
            for dst, src in loads:
                sp.dma_start(dst, src).then_inc(S["w_in"], 16)
            sp.wait_ge(S["w_in"], 16 * W_DMAS)

        @block.gpsimd
        def _(pool):
            nc.gpsimd.iota(rank[:, :, :], pattern=[[0, GT], [-1, E]], base=E, channel_multiplier=0,
                           allow_small_or_imprecise_dtypes=True).then_inc(S["ready"], 1)
            nc.gpsimd.memset(rwp[:, :], 0.0).then_inc(S["ready"], 1)

            def fetch(i):
                nc.gpsimd.tensor_copy(xg[:, :, :], X[:, bass.ds(i * GT, GT), :]).then_inc(S["xg_full"], 1)

            def root(i):
                pool.wait_ge(S["var"], i + 1)
                nc.gpsimd.tensor_tensor(out=rstd[:, :], in0=mv[:, :, 1], in1=K["neghalf"][:, 0:GT],
                                        op=ALU.pow).then_inc(S["rstd_done"], 1)

            def lows(i, ns):
                for n in ns:
                    u = order[n]
                    pool.wait_ge(S["h_rounded"], UNITS * i + n + 1)
                    low(nc.gpsimd, h2[1][:, u, :], prod[:, n % 2, :], raw[:, n % 2, :]).then_inc(S["h_split"], 1)

            def body(i, first_, last):
                if not last:
                    pool.wait_ge(S["turned"], DH * (i + 1))
                    fetch(i + 1)
                lows(i, range(2))
                if not first_:
                    root(i - 1)
                lows(i, range(2, UNITS))

            fetch(0)
            body(0, True, False)
            with pool.Fori(1, GROUPS - 1) as i:
                body(i, False, False)
            body(GROUPS - 1, False, True)
            root(GROUPS - 1)

        @block.tensor
        def _(pe):
            def turn_tokens(i):
                pe.wait_ge(S["xg_full"], i + 1)
                pe.wait_ge(S["silued"], UNITS * i)
                for hh in range(DH):
                    for j in range(GT):
                        t = nc.tensor.transpose(gate[hh][:, j * P:(j + 1) * P], xg[:, j, hh * P:(hh + 1) * P], K["ident"][:, :])
                    t.then_inc(S["turned"], 1)

            def logits(i):
                pe.wait_ge(S["xT_full"], DH * (i + 1))
                for j in range(GT):
                    for hh in range(DH):
                        m = nc.tensor.matmul(lg[:, j * E:(j + 1) * E], xT[:, hh, j * P:(j + 1) * P], wr[:, hh, :],
                                             start=(hh == 0), stop=(hh == DH - 1))
                m.then_inc(S["logits"], 1)

            def products(bank, w2, u):
                for hh in range(DH):
                    for q, (w_, x_) in enumerate(passes(w2, x2)):
                        m = nc.tensor.matmul(bank[:, :], w_[:, hh, u * P:(u + 1) * P], x_[:, hh, :],
                                             start=(hh == 0 and q == 0), stop=(hh == DH - 1 and q == 2))
                return m

            def body(i, last):
                pe.wait_ge(S["x_split"], DH * (i + 1))
                for n, u in enumerate(order):
                    if n >= 2:
                        pe.wait_ge(S["silued"], UNITS * i + n - 1)
                    m = products(gate[n % 2], gates_, u)
                    m.then_inc(S["gated"], 1)
                    pe.wait_ge(S["upped"], UNITS * i + max(n - 1, 0))
                    m = products(up[n % 2], ups, u)
                    m.then_inc(S["gated"], 1)
                    if n == 0:
                        pe.wait_ge(S["weights"], i + 1)
                        for j in range(GT):
                            t = nc.tensor.transpose(spread[0:E, j * P:(j + 1) * P], rw[:, j, :], K["ident"][:, :])
                        t.then_inc(S["rwT_turned"], 1)
                    if n >= 2:
                        if n == 2:
                            pe.wait_ge(S["halves"], i + 1)
                        else:
                            pe.wait_ge(S["h_done"], E * i + n - 2)
                        nc.tensor.matmul(spread[:, :], K["sel"][:, u:u + 1].to_broadcast([96, P]), rwp[:, :], start=True,
                                         stop=True).then_inc(S["spreaded"], 1)
                for name in ("w_rounded", "w_split"):
                    pe.wait_ge(S[name], len(PIECES))
                if not last:
                    turn_tokens(i + 1)
                pe.wait_ge(S["y_done"], 2 * i)
                for j in range(GT):
                    if j == 1 and not last:
                        logits(i + 1)
                    for n, u in enumerate(order):
                        if j == 0:
                            pe.wait_ge(S["h_split"], UNITS * i + n + 1)
                        for q, (h_, w_) in enumerate(passes(h2, downs)):
                            m = nc.tensor.matmul(turn[j // 2][:, (j % 2) * D:(j % 2 + 1) * D], h_[:, u, j * P:(j + 1) * P],
                                                 w_[:, u, :], start=(n == 0 and q == 0), stop=(n == UNITS - 1 and q == 2))
                    if j % 2:
                        m.then_inc(S["out_done"], 1)

            pe.wait_ge(S["w_in"], 16 * W_DMAS)
            turn_tokens(0)
            logits(0)
            for name in ("w_rounded", "w_split"):
                pe.wait_ge(S[name], len(FIRST_PIECES))
            with pe.Fori(0, GROUPS - 1) as i:
                body(i, False)
            body(GROUPS - 1, True)

        @block.scalar
        def _(act):
            def turned(i):
                for hh in range(DH):
                    act.wait_ge(S["turned"], DH * i + hh + 1)
                    nc.scalar.activation(xT[:, hh, :], gate[hh][:, :], ACT.Copy).then_inc(S["xT_full"], 1)

            def chances(i):
                act.wait_ge(S["gap"], i + 1)
                nc.scalar.activation(th[:, :], km[:, :], ACT.Tanh, scale=0.5).then_inc(S["tanh"], 1)

            def gates(i):
                for n in range(UNITS):
                    act.wait_ge(S["gated"], 2 * UNITS * i + 2 * n + 1)
                    act.wait_ge(S["upped"], UNITS * i + max(n - 1, 0))
                    nc.scalar.activation(silu[:, n % 2, :], gate[n % 2][:, :], ACT.Silu).then_inc(S["silued"], 1)
                    if n:
                        rounded(i, n - 1)
                rounded(i, UNITS - 1)

            def rounded(i, n):
                act.wait_ge(S["h_high"], UNITS * i + n + 1)
                nc.scalar.activation(h2[0][:, order[n], :], raw[:, n % 2, :], ACT.Copy).then_inc(S["h_rounded"], 1)

            def x_rounded(i):
                for hh in range(DH):
                    act.wait_ge(S["x_high"], DH * i + hh + 1)
                    nc.scalar.activation(x2[0][:, hh, :], xraw[:, hh, :], ACT.Copy).then_inc(S["x_rounded"], 1)

            nc.scalar.preload_act_table_set("silu_and_others")
            def weights_rounded(ks):
                for k in ks:
                    act.wait_ge(S["w_high"], k + 1)
                    nc.scalar.activation(PIECES[k][1], raw[:, k % 2, :], ACT.Copy).then_inc(S["w_rounded"], 1)

            turned(0)
            weights_rounded(FIRST_PIECES)
            x_rounded(0)
            chances(0)
            weights_rounded(LAST_PIECES)
            with act.Fori(0, GROUPS - 1) as i:
                gates(i)
                turned(i + 1)
                x_rounded(i + 1)
                chances(i + 1)
            gates(GROUPS - 1)

        @block.vector
        def _(dve):
            v = nc.vector

            def routing(i):
                st = Steps(dve, S["routing"], 16, i)

                def best(one_hot, m):
                    st.chain(v.tensor_reduce(m[:, :], logit[:, :, :], AXX, ALU.max))
                    st.chain(v.tensor_tensor(out=eq[:, :, :], in0=logit[:, :, :], in1=over(m[:, :], E), op=ALU.is_equal))
                    st.chain(v.tensor_tensor(out=key[:, :, :], in0=eq[:, :, :], in1=rank[:, :, :], op=ALU.mult))
                    st.chain(v.tensor_reduce(km[:, :], key[:, :, :], AXX, ALU.max))
                    st.chain(v.tensor_tensor(out=one_hot[:, :, :], in0=key[:, :, :], in1=over(km[:, :], E), op=ALU.is_equal))

                dve.wait_ge(S["logits"], i + 1)
                st.chain(v.tensor_tensor(out=logit[:, :, :], in0=lg[:, 0:GT * E].rearrange("p (j e) -> p j e", e=E),
                                         in1=each(ebias[:, :], GT), op=ALU.add))
                best(first, m1)
                st.chain(v.scalar_tensor_tensor(out=logit[:, :, :], in0=first[:, :, :], scalar=-3e38, in1=logit[:, :, :],
                                                op0=ALU.mult, op1=ALU.add))
                best(second, m2)
                v.tensor_tensor(out=km[:, :], in0=m1[:, :], in1=m2[:, :], op=ALU.subtract).then_inc(S["gap"], 1)
                dve.wait_ge(S["tanh"], i + 1)
                st.then(v.tensor_scalar(p1[:, :], th[:, :], 0.5, 0.5, ALU.mult, ALU.add))
                st.chain(v.tensor_scalar(p2[:, :], th[:, :], -0.5, 0.5, ALU.mult, ALU.add))
                st.then(v.tensor_tensor(out=first[:, :, :], in0=first[:, :, :], in1=over(p1[:, :], E), op=ALU.mult))
                st.chain(v.tensor_tensor(out=second[:, :, :], in0=second[:, :, :], in1=over(p2[:, :], E), op=ALU.mult))
                v.tensor_tensor(out=rw[:, :, :], in0=first[:, :, :], in1=second[:, :, :], op=ALU.add).then_inc(S["weights"], 1)
                st.close()

            def unit(i, n):
                u = order[n]
                dve.wait_ge(S["silued"], UNITS * i + n + 1)
                dve.wait_ge(S["gated"], 2 * UNITS * i + 2 * n + 2)
                now = prod[:, n % 2, :]
                dve.wait_ge(S["h_split"], UNITS * i + max(n - 1, 0))
                v.tensor_tensor(out=now, in0=silu[:, n % 2, :], in1=up[n % 2][:, :], op=ALU.mult).then_inc(S["upped"], 1)
                dve.wait_ge(S["upped"], UNITS * i + n + 1)
                if u < E:
                    dve.wait_ge(S["spreaded"], E * i + u + 1)
                    v.tensor_tensor(out=now, in0=now, in1=spread[:, :], op=ALU.mult).then_inc(S["h_done"], 1)
                    dve.wait_ge(S["h_done"], E * i + u + 1)
                high(v, raw[:, n % 2, :], now).then_inc(S["h_high"], 1)

            def split_x(i):
                for hh in range(DH):
                    dve.wait_ge(S["xT_full"], DH * i + hh + 1)
                    high(v, xraw[:, hh, :], xT[:, hh, :]).then_inc(S["x_high"], 1)
                for hh in range(DH):
                    dve.wait_ge(S["x_rounded"], DH * i + hh + 1)
                    low(v, x2[1][:, hh, :], xT[:, hh, :], xraw[:, hh, :]).then_inc(S["x_split"], 1)

            def split_weights(ks):
                for k in ks:
                    src, _, low_ = PIECES[k]
                    if k >= 2:
                        dve.wait_ge(S["w_rounded"], k - 1)
                    high(v, raw[:, k % 2, :], src).then_inc(S["w_high"], 1)
                    dve.wait_ge(S["w_high"], k + 1)
                    low(v, low_, src, raw[:, k % 2, :]).then_inc(S["w_split"], 1)

            def variances(st):
                statistics(st, v, lambda j: y[:, j, :], stat, mv, rstd, GT)
                v.tensor_scalar(mv[:, :, 1], mv[:, :, 1], LN_EPS, None, ALU.add).then_inc(S["var"], 1)

            def writes(st, i):
                dve.wait_ge(S["rstd_done"], i + 1)
                for j in range(GT):
                    st.then(v.tensor_scalar(X[:, bass.ds(i * GT + j, 1), :].rearrange("p a d -> p (a d)"), y[:, j, :], mv[:, j, 0:1],
                                            rstd[:, j:j + 1], ALU.subtract, ALU.mult))

            def body(i, first_, last):
                st = Steps(dve, S["norming"], 3 * GT + 1, i - 1)
                unit(i, 0)
                sp = Steps(dve, S["splitting"], SPLITS, i)
                dve.wait_ge(S["rwT_turned"], i + 1)
                sp.chain(v.tensor_copy(rwT[:, :], spread[0:E, :]))
                split3(sp, v, rwT[:, :], rest[:, :], part[:, :], rwp, E).then_inc(S["halves"], 1)
                sp.close()
                unit(i, 1)
                if not first_:
                    variances(st)
                unit(i, 2)
                if not first_:
                    writes(st, i - 1)
                for n in range(3, UNITS):
                    unit(i, n)
                if not last:
                    split_x(i + 1)
                    routing(i + 1)
                for b in range(2):
                    if b == 0 and not first_:
                        st.wait()
                    dve.wait_ge(S["out_done"], 2 * i + b + 1)
                    v.tensor_tensor(out=y[:, 2 * b:2 * b + 2, :], in0=turn[b][:, :].rearrange("p (j d) -> p j d", d=D),
                                    in1=X[:, bass.ds(i * GT + 2 * b, 2), :], op=ALU.add).then_inc(S["y_done"], 1)
                dve.wait_ge(S["y_done"], 2 * (i + 1))
                if not first_:
                    st.close()

            dve.wait_ge(S["ready"], 2)
            dve.wait_ge(S["w_in"], 16 * W_DMAS)
            split_weights(FIRST_PIECES)
            split_x(0)
            routing(0)
            split_weights(LAST_PIECES)
            dve.wait_ge(S["w_rounded"], len(PIECES))
            body(0, True, False)
            with dve.Fori(1, GROUPS - 1) as i:
                body(i, False, False)
            body(GROUPS - 1, False, True)
            st = Steps(dve, S["norming"], 3 * GT + 1, GROUPS - 1)
            variances(st)
            writes(st, GROUPS - 1)
            st.wait()


HW = 512
HT = HW // P
CHUNKS = SEQ // P
KEYS = 2 * P
VT = CHUNKS + 1


def banded_phase(nc, X, K, tag, W, heads, scale, shift, valid, norm=None, add=None, out=None):
    twin = W["q"].shape[1] == HW // 2
    width = W["q"].shape[1] // heads
    rows = HW // heads
    per = P // rows
    pairs = heads // 2
    KB, VW = (HT // 2, HW // 2) if twin else (HT, HW)
    block_of = lambda p, a: p // per * 2 + a
    key_block = lambda p, a: p // per if twin else block_of(p, a)
    base_of = lambda p: p % per * rows
    head = lambda p, a: 2 * p + a if twin else block_of(p, a) * per + p % per
    HR = P // 2
    high_at = lambda blk: blk % 2 * HR
    halo = P - shift
    with ExitStack() as ctx:
        A = Alloc(nc, ctx, tag)
        wq, wk, wv = A.sb("wq", [P, DH, VW]), A.sb("wk", [P, DH, VW]), A.sb("wv", [P, DH, VW])
        wo = A.sb("wo", [P, KB, D])
        gain, bias = A.sb("gain", [P, DH]), A.sb("bias", [P, DH])
        xs = A.sb("xs", [P, GT, D])
        xT = A.sb("xT", [P, DH, halo + GN + halo])
        if twin:
            QT, QL, KT = A.sb("QT", [P, 2 * KB, SEQ]), A.sb("QL", [P, KB, SEQ]), A.sb("KT", [P, 2 * KB, P + SEQ], F32R)
            own2 = A.sb("own2", [P, P // width // 2])
            ql = [A.sb(f"ql{k}", [P, heads, P], F32R) for k in range(2)]
        else:
            QT, KT = A.sb("QT", [P, KB, SEQ]), A.sb("KT", [P, KB, P + SEQ])
        V = A.sb("V", [P, VT, VW])
        band, edge = A.sb("band", [P, KEYS], BF16), A.sb("edge", [P, P + SEQ], BF16)
        identb = A.sb("identb", [P, P], BF16)
        OWN = P // width
        own, keep = A.sb("own", [P, OWN]), A.sb("keep", [P, 2])
        qs = [A.sb(f"qs{k}", [P, heads, P], F32R if twin else F32) for k in range(2)]
        vs = [A.sb(f"vs{k}", [P, 2, VW]) for k in range(2)]
        mask = [A.sb(f"mask{k}", [P, KEYS], BF16) for k in range(2)]
        prob = [A.sb(f"prob{k}", [P, 2, KEYS]) for k in range(4)]
        raw, khigh = ([a[:, :, :].rearrange("p a j -> p (a j)") for a in some] for some in (prob, vs))
        probT = [A.sb(f"probT{k}", [P, 4, P]) for k in range(2)]
        nmax, sums, inv = ([A.sb(f"{n}{k}", [P, heads]) for k in range(2)] for n in ("nmax", "sums", "inv"))
        mixed, other = A.sb("mixed", [P, KB, P]), A.sb("other", [P, KB, P])
        stat, mv, rstd = A.sb("stat", [P, GT, 6]), A.sb("mv", [P, GT, 2]), A.sb("rstd", [P, GT])
        stat1, mv1, rstd1 = A.sb("stat1", [P, 1, 6]), A.sb("mv1", [P, 1, 2]), A.sb("rstd1", [P, 1])
        y = A.sb("y", [P, D])
        if add:
            pick, picked = [A.sb(f"pick{k}", [P, 1], U32) for k in range(2)], [A.sb(f"picked{k}", [P, D]) for k in range(2)]
        bank = [A.ps(f"bank{k}") for k in range(8)]
        score, turned, outT = bank[0:4], bank[4:6], bank[6:8]
        S = {n: A.sem(n) for n in (
            "w_in", "made", "xs_full", "turned", "xT_full", "proj", "proj_out", "v_done", "v_out", "halo", "var", "rstd_done",
            "q_copied", "v_copied", "masked", "scored", "maxed", "exped", "inverted", "scaled", "scaled2", "prob_turned", "probT_full", "outT_done",
            "mixed_full", "out_done", "y_done", "x_done", "picks", "picked0", "picked1",
            "var1", "rstd1_done", "last", "kept", "stored", "started", "groups", "q_high", "q_low", "k_high", "k_rounded", "k_low")}
        block = ctx.enter_context(nc.Block())
        vec = lambda a: a.rearrange("(h p) -> p h", p=P)
        loads = [(dst[:, :, :], src.rearrange("(h p) e -> p h e", p=P))
                 for dst, src in ((wq, W["q"]), (wk, W["k"]), (wv, W["v"]), (wo, W["o"]))]
        if norm:
            loads += [(gain[:, :], vec(norm[0])), (bias[:, :], vec(norm[1]))]
        LOADED = 16 * len(loads)
        VB = GN // VW
        VTILES = CHUNKS + (1 if halo else 0)
        VOUT = CHUNKS // VB + (1 if halo else 0)
        VGROUP = GT // VB
        BODIES = CHUNKS // 2
        AHEAD = 3 if twin else 2
        MIX, PROJECT, ADD, WRITE = (1, 3, 4, 6) if twin else (1, 2, 2, 3)
        SHARE = 4
        shared = lambda p: p % SHARE == SHARE - 1
        made_steps = []

        @block.sync
        def _(sp):
            with nc.allow_non_contiguous_dma(reason="vectors onto partitions, once"):
                for dst, src in loads:
                    sp.dma_start(dst, src).then_inc(S["w_in"], 16)
            sp.wait_ge(S["w_in"], LOADED)
            if out is not None:
                rows_of = out.rearrange("b (t p) d -> p (b t) d", p=P)
                for g in range(GROUPS):
                    tiles = slice(g * GT, (g + 1) * GT)
                    sp.wait_ge(S["x_done"], (g + 1) * GT)
                    sp.dma_start(rows_of[:, tiles, :], X[:, tiles, :]).then_inc(S["stored"], 16)
                sp.wait_ge(S["stored"], 16 * GROUPS)

        @block.gpsimd
        def _(pool):
            g = nc.gpsimd
            made = Steps(pool, S["made"])
            made.chain(g.memset(identb[:, :], 0.0))
            made.chain(g.affine_select(out=identb[:, :], in_=identb[:, :], compare_op=ALU.not_equal, fill=1.0, base=0,
                                       pattern=[[-1, P]], channel_multiplier=1))
            made.chain(g.memset(own[:, :], scale))
            made.chain(g.affine_select(out=own[:, :], in_=own[:, :], compare_op=ALU.is_ge, fill=0.0, base=0,
                                       pattern=[[-width, OWN]], channel_multiplier=1))
            made.chain(g.affine_select(out=own[:, :], in_=own[:, :], compare_op=ALU.is_ge, fill=0.0, base=width - 1,
                                       pattern=[[width, OWN]], channel_multiplier=-1))
            if twin:
                made.chain(g.tensor_tensor(out=own2[:, :], in0=own[:, 0:OWN // 2], in1=own[:, OWN // 2:], op=ALU.add))
            made.chain(g.memset(band[:, :], 0.0))
            valid(g, made, band)
            made.chain(g.memset(edge[:, :], 0.0))
            made.chain(g.memset(edge[:, 0:shift], -BIG))
            if twin:
                made.chain(g.memset(raw[0], 0.0))
                made.chain(g.tensor_copy(KT[:, :, 0:shift], raw[0].rearrange("p (m j) -> p m j", j=shift)))
            else:
                made.chain(g.memset(KT[:, :, 0:shift], 0.0))
            if halo:
                made.chain(g.memset(edge[:, shift + SEQ:], -BIG))
                made.chain(g.memset(KT[:, :, shift + SEQ:], 0.0))
                made.chain(g.memset(xT[:, :, halo + GN:], 0.0))
            else:
                made.chain(g.memset(V[:, 0, :], 0.0))
            made_steps.append(made.n)
            pool.wait_ge(S["w_in"], LOADED)

            def alone_in(alone, now, heads_rows):
                n = heads_rows.shape[1]
                shape = [P, now.shape[1], n, P]
                return g.tensor_tensor(out=alone[:, :, :].rearrange("p (m h) q -> p m h q", h=n), in0=now.unsqueeze(2).to_broadcast(shape),
                                       in1=heads_rows[:, :].unsqueeze(1).unsqueeze(3).to_broadcast(shape), op=ALU.mult)

            def prepare(b, cc, k, half=0):
                c = b * CHUNKS + cc
                if add:
                    pool.wait_ge(S[f"picked{k}"], 16 * (b * BODIES + (0 if isinstance(cc, int) else half)))
                pool.wait_ge(S["scored"], used(b, cc, k))
                if add:
                    g.tensor_copy(pick[k][:, :], add[1][:, bass.ds(c, 1)]).then_inc(S["picks"], 1)
                ins = alone_in(qs[k], QT[:, :, bass.ds(cc * P, P)], own2 if twin else own)
                if twin:
                    if isinstance(cc, int):
                        pool.wait_ge(S["q_low"], KB * SGROUPS * (b + 1))
                        pool.wait_ge(S["k_low"], KB * SGROUPS * (b + 1))
                        pool.wait_ge(S["k_rounded"], KB * SGROUPS * (b + 1))
                    ins = alone_in(ql[k], QL[:, :, bass.ds(cc * P, P)], own)
                ins.then_inc(S["q_copied"], 1)
                if add and isinstance(cc, int):
                    pool.wait_ge(S["picks"], c + 1)
                pool.wait_ge(S["outT_done"], used(b, cc, k))
                g.tensor_tensor(out=mask[k][:, :], in0=band[:, :], in1=edge[:, bass.ds(cc * P, KEYS)],
                                op=ALU.add).then_inc(S["masked"], 1)
                if isinstance(cc, int):
                    gather(k)
                g.tensor_copy(vs[k][:, :, :], V[:, bass.ds(cc, 2), :]).then_inc(S["v_copied"], 1)

            def gather(k):
                if add:
                    g.indirect_dma_start(out=picked[k][:, :], out_offset=None, in_=add[0],
                                         in_offset=bass.IndirectOffsetOnAxis(ap=pick[k][:, 0:1], axis=0)).then_inc(S[f"picked{k}"], 16)

            def used(b, cc, k):
                return pairs * (b * CHUNKS + (cc - 1 if k or not isinstance(cc, int) else 0))

            def root(n, k=None):
                if k is not None and add:
                    pool.wait_ge(S["picks"], n + 3)
                pool.wait_ge(S["var1"], n + 1)
                g.tensor_tensor(out=rstd1[:, :], in0=mv1[:, 0, 1:2], in1=K["neghalf"][:, 0:1], op=ALU.pow).then_inc(S["rstd1_done"], 1)
                if k is not None:
                    gather(k)

            with pool.Fori(0, BATCH) as b:
                if norm:
                    with pool.Fori(0, SGROUPS) as s:
                        pool.wait_ge(S["var"], b * SGROUPS + s + 1)
                        g.tensor_tensor(out=rstd[:, :], in0=mv[:, :, 1], in1=K["neghalf"][:, :], op=ALU.pow).then_inc(S["rstd_done"], 1)
                else:
                    with pool.Fori(0, SGROUPS) as s:
                        i = b * SGROUPS + s
                        pool.wait_ge(S["turned"], DH * i)
                        g.tensor_copy(xs[:, :, :], X[:, bass.ds(i * GT, GT), :]).then_inc(S["xs_full"], 1)
                if twin:
                    pool.wait_ge(S["q_high"], KB * SGROUPS * (b + 1))
                else:
                    pool.wait_ge(S["proj_out"], 2 * KB * SGROUPS * (b + 1))
                pool.wait_ge(S["v_out"], VOUT * (b + 1))
                prepare(b, 0, 0)
                prepare(b, 1, 1)
                with pool.Fori(1, BODIES) as c2:
                    for k in range(2):
                        prepare(b, c2 * 2 + k, k, c2)
                        root(b * CHUNKS + c2 * 2 + k - 2, k)
                root(b * CHUNKS + CHUNKS - 2)
                root(b * CHUNKS + CHUNKS - 1)

        @block.tensor
        def _(pe):
            t = nc.tensor
            pe.wait_ge(S["w_in"], LOADED)
            pe.wait_ge(S["made"], made_steps[0])

            def values(n, nb, j, first):
                if j % VB == 0 and not first:
                    pe.wait_ge(S["v_out"], nb - 1)
                for hh in range(DH):
                    ins = t.matmul(bank[4 + j // VB % 2][:, j % VB * VW:(j % VB + 1) * VW], xT[:, hh, j * P:(j + 1) * P], wv[:, hh, :],
                                   start=(hh == 0), stop=(hh == DH - 1))
                if j % VB == VB - 1 or j == GT:
                    ins.then_inc(S["v_done"], 1)

            def scores(b, c, k, p, first=False):
                j = k * pairs + p
                n = b * CHUNKS + c
                pe.wait_ge(S["exped"], n * pairs + (0 if first else p - 3))
                if p == 0:
                    pe.wait_ge(S["q_copied"], n + 1)
                    pe.wait_ge(S["masked"], n + 1)
                t.matmul(score[j % 4][:, :], identb[:, :], mask[k][:, :].unsqueeze(1).to_broadcast([P, 2, KEYS]),
                         start=True, stop=False)
                for a in range(2):
                    out_ = score[j % 4][:, a * KEYS:(a + 1) * KEYS]
                    h = head(p, a)
                    if twin:
                        keys = KT[:, h * 2 // OWN, bass.ds(c * P, KEYS)]
                        t.matmul(out_, qs[k][:, h, :], keys, start=False, stop=False)
                        ins = t.matmul(out_, ql[k][:, h, :], keys, start=False, stop=(a == 1))
                    else:
                        ins = t.matmul(out_, qs[k][:, h, :], KT[:, key_block(p, a), bass.ds(c * P, KEYS)], start=False, stop=(a == 1))
                ins.then_inc(S["scored"], 1)

            def turns(b, c, k, p):
                j = k * pairs + p
                n = b * CHUNKS + c
                pe.wait_ge(S["scaled"], n * pairs + p + 1)
                if twin and shared(p):
                    pe.wait_ge(S["scaled2"], n * (pairs // SHARE) + p // SHARE + 1)
                if p >= 2 or k:
                    pe.wait_ge(S["probT_full"], n * pairs + p - 1)
                else:
                    pe.wait_ge(S["probT_full"], n * pairs)
                for kt in range(2):
                    for a in range(2):
                        ins = t.transpose(turned[j % 2][:, (2 * kt + a) * P:(2 * kt + a + 1) * P],
                                          prob[j % 4][:, a, kt * P:(kt + 1) * P], K["ident"][:, :])
                ins.then_inc(S["prob_turned"], 1)

            def mixes(b, c, k, p):
                j = k * pairs + p
                n = b * CHUNKS + c
                pe.wait_ge(S["probT_full"], n * pairs + p + 1)
                if p == 0:
                    pe.wait_ge(S["y_done"], n - 1) if k else pe.wait_ge(S["y_done"], b * CHUNKS + before(c))
                    pe.wait_ge(S["v_copied"], n + 1)
                base, m = base_of(p), block_of(p, 0)
                for a in range(1 if twin else 2):
                    for kt in range(2):
                        h = p if twin else head(p, a)
                        ins = t.matmul(outT[k][base:base + rows, (m + a) * P:(m + a + (2 if twin else 1)) * P], vs[k][:, kt, h * rows:(h + 1) * rows],
                                       probT[j % 2][:, 2 * kt:2 * kt + 2, :].rearrange("p a q -> p (a q)") if twin else probT[j % 2][:, 2 * kt + a, :],
                                       start=(kt == 0), stop=(kt == 1), tile_position=(0, base))
                ins.then_inc(S["outT_done"], 1)

            before = lambda c: c - 1 if not isinstance(c, int) or c else 0

            def project(n, k):
                pe.wait_ge(S["mixed_full"], n + 1)
                for m in range(KB):
                    ins = t.matmul(outT[k][:, 0:D], mixed[:, m, :], wo[:, m, :], start=(m == 0), stop=(m == KB - 1))
                ins.then_inc(S["out_done"], 1)

            def body(b, c2, first, last):
                for k in range(2):
                    c = c2 * 2 + k
                    n = b * CHUNKS + c
                    for p in range(pairs):
                        if p + AHEAD < pairs:
                            scores(b, c, k, p + AHEAD, first and not k and p + AHEAD < 4)
                        elif not (k and last):
                            scores(b, c + 1, 1 - k, p + AHEAD - pairs)
                        turns(b, c, k, p)
                        if p:
                            mixes(b, c, k, p - 1)
                        elif k or not first:
                            mixes(b, c - 1, 1 - k, pairs - 1)
                        if p == PROJECT and (k or not first):
                            project(n - 1, 1 - k)

            with pe.Fori(0, BATCH) as b:
                with pe.Fori(0, SGROUPS) as s:
                    i = b * SGROUPS + s
                    pe.wait_ge(S["xs_full"], i + 1)
                    for hh in range(DH):
                        for j in range(GT):
                            ins = t.transpose(bank[hh][:, j * P:(j + 1) * P], xs[:, j, hh * P:(hh + 1) * P], K["ident"][:, :])
                        ins.then_inc(S["turned"], 1)
                    pe.wait_ge(S["xT_full"], DH * (i + 1))
                    pe.wait_ge(S["v_out"], b * VOUT + s * VGROUP)
                    for j in range(GT):
                        values(0, b * VOUT + s * VGROUP + j // VB, j, j // VB < 2)
                    for m in range(2 * KB):
                        w = wq if m < KB else wk
                        pe.wait_ge(S["proj_out"], 2 * KB * i + max(m - 1, 0))
                        for hh in range(DH):
                            ins = t.matmul(bank[2 + m % 2][:, :], w[:, hh, (m % KB) * P:(m % KB + 1) * P], xT[:, hh, halo:halo + GN],
                                           start=(hh == 0), stop=(hh == DH - 1))
                        ins.then_inc(S["proj"], 1)
                if halo:
                    values(0, b * VOUT + CHUNKS // VB, GT, False)
                for p in range(AHEAD):
                    scores(b, 0, 0, p, True)
                body(b, 0, True, False)
                with pe.Fori(1, BODIES - 1) as c2:
                    body(b, c2, False, False)
                body(b, BODIES - 1, False, True)
                mixes(b, CHUNKS - 1, 1, pairs - 1)
                project(b * CHUNKS + CHUNKS - 1, 1)

        @block.scalar
        def _(act):
            a_ = nc.scalar
            act.wait_ge(S["w_in"], LOADED)
            act.wait_ge(S["made"], made_steps[0])
            def exps(n, k, p, first):
                j = k * pairs + p
                act.wait_ge(S["maxed"], n * pairs + p + 1)
                if j >= 4 or not first:
                    act.wait_ge(S["prob_turned"], n * pairs + p - 3)
                else:
                    act.wait_ge(S["prob_turned"], n * pairs)
                for a in range(2):
                    h = head(p, a)
                    ins = a_.activation(prob[j % 4][:, a, :], score[j % 4][:, a * KEYS:(a + 1) * KEYS], ACT.Exp,
                                        bias=nmax[k][:, h:h + 1], accum_out=sums[k][:, h:h + 1])
                ins.then_inc(S["exped"], 1)

            def scales(n, k, p):
                act.wait_ge(S["inverted"], n * pairs + p + 1)
                for a in range(1 if shared(p) else 2):
                    h = head(p, a)
                    now = prob[(k * pairs + p) % 4][:, a, :]
                    ins = a_.activation(now, now, ACT.Copy, scale=inv[k][:, h:h + 1])
                ins.then_inc(S["scaled"], 1)

            def body(b, c2, first, last):
                for k in range(2):
                    n = b * CHUNKS + c2 * 2 + k
                    for p in range(pairs):
                        exps(n, k, p, first)
                        if twin and p:
                            scales(n, k, p - 1)
                        elif twin and (k or not first):
                            scales(n - 1, 1 - k, pairs - 1)

            with act.Fori(0, BATCH) as b:
                with act.Fori(0, SGROUPS) as s:
                    i = b * SGROUPS + s
                    if halo:
                        act.wait_ge(S["halo"], i + b + 1)
                    for hh in range(DH):
                        act.wait_ge(S["turned"], DH * i + hh + 1)
                        dst = xT[:, hh, halo:halo + GN]
                        if norm:
                            ins = a_.activation(dst, bank[hh][:, :], ACT.Identity, scale=gain[:, hh:hh + 1], bias=bias[:, hh:hh + 1])
                        else:
                            ins = a_.activation(dst, bank[hh][:, :], ACT.Copy)
                        ins.then_inc(S["xT_full"], 1)
                    for m in range(2 * KB):
                        act.wait_ge(S["proj"], 2 * KB * i + m + 1)
                        if twin:
                            act.wait_ge(S["q_low" if m < KB else "k_low"], KB * i)
                            a_.activation(raw[m], bank[2 + m % 2][:, :], ACT.Copy).then_inc(S["proj_out"], 1)
                        elif m >= KB:
                            a_.activation(KT[:, m - KB, bass.ds(s * GN + shift, GN)], bank[2 + m % 2][:, :], ACT.Copy).then_inc(S["proj_out"], 1)
                        else:
                            a_.activation(QT[:, m, bass.ds(s * GN, GN)], bank[2 + m % 2][:, :], ACT.Copy).then_inc(S["proj_out"], 1)
                body(b, 0, True, False)
                with act.Fori(1, BODIES - 1) as c2:
                    body(b, c2, False, False)
                body(b, BODIES - 1, False, True)
                if twin:
                    scales(b * CHUNKS + CHUNKS - 1, 1, pairs - 1)

        @block.vector
        def _(dve):
            v = nc.vector
            dve.wait_ge(S["made"], made_steps[0])
            if twin:
                v.tensor_reduce(keep[:, :], own[:, :].rearrange("p (h a) -> p a h", a=2), AXX, ALU.max).then_inc(S["kept"], 1)
                dve.wait_ge(S["kept"], 1)
                v.tensor_scalar(keep[:, :], keep[:, :], 1 / scale, None, ALU.mult).then_inc(S["kept"], 1)
                dve.wait_ge(S["kept"], 2)

            both = lambda p: slice(head(p, 0), head(p, 1) + 1, head(p, 1) - head(p, 0))

            def maxes(n, k, p, first=False):
                j = k * pairs + p
                dve.wait_ge(S["scored"], n * pairs + p + 1)
                if p == 0:
                    dve.wait_ge(S["exped"], n * pairs if first else (n - 1) * pairs)
                hs = both(p)
                v.tensor_reduce(nmax[k][:, hs], score[j % 4][:, :].rearrange("p (a j) -> p a j", j=KEYS), AXX, ALU.max,
                                negate=True).then_inc(S["maxed"], 1)

            def copies(n, k, p, first):
                j = k * pairs + p
                dve.wait_ge(S["prob_turned"], n * pairs + p + 1)
                if p >= 2 or k:
                    dve.wait_ge(S["outT_done"], n * pairs + p - 1)
                else:
                    dve.wait_ge(S["outT_done"], n * pairs if first else n * pairs + p - 1)
                v.tensor_copy(probT[j % 2][:, :, :], turned[j % 2][:, :].rearrange("p (n q) -> p n q", q=P))\
                 .then_inc(S["probT_full"], 1)

            def invert(n, k, p):
                dve.wait_ge(S["exped"], n * pairs + p + 1)
                v.reciprocal(inv[k][:, both(p)], sums[k][:, both(p)]).then_inc(S["inverted"], 1)
                if twin and not shared(p):
                    return
                dve.wait_ge(S["inverted"], n * pairs + p + 1)
                for a in range(1 if twin else 0, 2):
                    h = head(p, a)
                    now = prob[(k * pairs + p) % 4][:, a, :]
                    ins = v.tensor_scalar(now, now, inv[k][:, h:h + 1], None, ALU.mult)
                ins.then_inc(S["scaled2" if twin else "scaled"], 1)

            def mix(n, k):
                dve.wait_ge(S["outT_done"], (n + 1) * pairs)
                blocks = outT[k][:, :].rearrange("p (m q) -> p m q", q=P)
                if not twin:
                    v.tensor_copy(mixed[:, :, :], blocks).then_inc(S["mixed_full"], 1)
                    return
                v.tensor_scalar(other[:, :, :], blocks[:, 1::2, :], keep[:, 1:2], None, ALU.mult).then_inc(S["last"], 1)
                dve.wait_ge(S["last"], n + 1)
                v.scalar_tensor_tensor(out=mixed[:, :, :], in0=blocks[:, 0::2, :], scalar=keep[:, 0:1], in1=other[:, :, :],
                                       op0=ALU.mult, op1=ALU.add).then_inc(S["mixed_full"], 1)

            ENDS = 4 if add else 3

            def adds(b, c, n, k):
                st = Steps(dve, S["started"], ENDS, n)
                xc = X[:, bass.ds(n, 1), :].rearrange("p a d -> p (a d)")
                dve.wait_ge(S["out_done"], n + 1)
                v.tensor_tensor(out=y[:, :], in0=outT[k][:, 0:D], in1=xc, op=ALU.add).then_inc(S["y_done"], 1)
                dve.wait_ge(S["y_done"], n + 1)
                if add:
                    dve.wait_ge(S[f"picked{k}"], 16 * (b * BODIES + pair_of(c) + 1))
                    st.chain(v.tensor_tensor(out=y[:, :], in0=y[:, :], in1=picked[k][:, :], op=ALU.add))
                statistics(st, v, lambda j: y[:, :], stat1, mv1, rstd1, 1)
                v.tensor_scalar(mv1[:, 0, 1:2], mv1[:, 0, 1:2], LN_EPS, None, ALU.add).then_inc(S["var1"], 1)
                st.close()

            def writes(n):
                xc = X[:, bass.ds(n, 1), :].rearrange("p a d -> p (a d)")
                dve.wait_ge(S["rstd1_done"], n + 1)
                v.tensor_scalar(xc, y[:, :], mv1[:, 0, 0:1], rstd1[:, 0:1], ALU.subtract, ALU.mult).then_inc(S["x_done"], 1)

            pair_of = lambda c: c[0] + c[1]

            def body(b, c2, first, last):
                for k in range(2):
                    n = b * CHUNKS + c2 * 2 + k
                    for p in range(pairs):
                        if p + AHEAD < pairs:
                            maxes(n, k, p + AHEAD)
                        elif not (k and last):
                            maxes(n + 1, 1 - k, p + AHEAD - pairs)
                        if p + 1 < pairs:
                            invert(n, k, p + 1)
                        elif not (k and last):
                            invert(n + 1, 1 - k, 0)
                        copies(n, k, p, first and not k)
                        if k or not first:
                            if p == MIX:
                                mix(n - 1, 1 - k)
                            if p == ADD:
                                adds(b, (c2, 0 if k else -1), n - 1, 1 - k)
                            if p == WRITE:
                                writes(n - 1)

            with dve.Fori(0, BATCH) as b:
                if halo:
                    v.memset(xT[:, :, 0:halo], 0.0).then_inc(S["halo"], 1)
                with dve.Fori(0, SGROUPS) as s:
                    i = b * SGROUPS + s
                    st = Steps(dve, S["groups"], (1 + 2 * GT) if norm else 0, i)
                    if norm:
                        dve.wait_ge(S["turned"], DH * i)
                        xj = lambda j: X[:, bass.ds(i * GT + j, 1), :].rearrange("p a d -> p (a d)")
                        statistics(st, v, xj, stat, mv, rstd, GT)
                        v.tensor_scalar(mv[:, :, 1], mv[:, :, 1], LN_EPS, None, ALU.add).then_inc(S["var"], 1)
                        dve.wait_ge(S["rstd_done"], i + 1)
                        for j in range(GT):
                            ins = v.tensor_scalar(xs[:, j, :], xj(j), mv[:, j, 0:1], rstd[:, j:j + 1], ALU.subtract, ALU.mult)
                        ins.then_inc(S["xs_full"], 1)
                    for j in range(VGROUP):
                        dve.wait_ge(S["v_done"], b * VOUT + s * VGROUP + j + 1)
                        v.tensor_copy(V[:, bass.ds(s * GT + j * VB + (0 if halo else 1), VB), :],
                                      bank[4 + j % 2][:, :].rearrange("p (n e) -> p n e", e=VW)).then_inc(S["v_out"], 1)
                    if twin:
                        for m in range(KB):
                            dve.wait_ge(S["proj_out"], 2 * KB * i + m + 1)
                            for blk in (2 * m, 2 * m + 1):
                                at = slice(high_at(blk), high_at(blk) + HR)
                                for to in (0, HR):
                                    ins = high(v, QT[to:to + HR, blk, bass.ds(s * GN, GN)], raw[m][at, :])
                            ins.then_inc(S["q_high"], 1)
                        dve.wait_ge(S["k_rounded"], KB * i)
                        for m in range(KB):
                            dve.wait_ge(S["proj_out"], 2 * KB * i + KB + m + 1)
                            high(v, khigh[m], raw[KB + m]).then_inc(S["k_high"], 1)
                        for m in range(KB):
                            dve.wait_ge(S["k_high"], KB * i + m + 1)
                            for blk in (2 * m, 2 * m + 1):
                                at = slice(high_at(blk), high_at(blk) + HR)
                                ins = v.tensor_copy(KT[at, blk, bass.ds(s * GN + shift, GN)], khigh[m][at, :])
                            ins.then_inc(S["k_rounded"], 1)
                        for m in range(KB):
                            dve.wait_ge(S["q_high"], KB * i + m + 1)
                            for blk in (2 * m, 2 * m + 1):
                                at = slice(high_at(blk), high_at(blk) + HR)
                                ins = low(v, QL[at, m, bass.ds(s * GN, GN)], raw[m][at, :], QT[at, blk, bass.ds(s * GN, GN)])
                            ins.then_inc(S["q_low"], 1)
                        for m in range(KB):
                            dve.wait_ge(S["k_high"], KB * i + m + 1)
                            for blk in (2 * m, 2 * m + 1):
                                at, to = (slice(r, r + HR) for r in (high_at(blk), HR - high_at(blk)))
                                ins = low(v, KT[to, blk, bass.ds(s * GN + shift, GN)], raw[KB + m][at, :], khigh[m][at, :])
                            ins.then_inc(S["k_low"], 1)
                    if halo:
                        v.tensor_copy(xT[:, :, 0:halo], xT[:, :, GN:GN + halo]).then_inc(S["halo"], 1)
                    st.close()
                if halo:
                    dve.wait_ge(S["v_done"], VOUT * (b + 1))
                    v.tensor_copy(V[:, CHUNKS, :], bank[4 + GT // VB % 2][:, :]).then_inc(S["v_out"], 1)
                for p in range(AHEAD):
                    maxes(b * CHUNKS, 0, p, True)
                invert(b * CHUNKS, 0, 0)
                body(b, 0, True, False)
                with dve.Fori(1, BODIES - 1) as c2:
                    body(b, c2, False, False)
                body(b, BODIES - 1, False, True)
                n = b * CHUNKS + CHUNKS - 1
                mix(n, 1)
                adds(b, (BODIES - 1, 0), n, 1)
                writes(n)


def sliding_phase(nc, X, K, I):
    def valid(g, made, band):
        made.chain(g.affine_select(out=band[:, :], in_=band[:, :], compare_op=ALU.is_ge, fill=-BIG, base=-1,
                                   pattern=[[1, KEYS]], channel_multiplier=-1))
        made.chain(g.affine_select(out=band[:, :], in_=band[:, :], compare_op=ALU.is_ge, fill=-BIG, base=P,
                                   pattern=[[-1, KEYS]], channel_multiplier=1))

    W = {n: I["L1_attn_W" + n] for n in "qkvo"}
    banded_phase(nc, X, K, "sw", W, heads=16, scale=0.25, shift=P, valid=valid)


LH, DHD = 8, 64
NQ, NKV = 256, 512
QT_, KVT = NQ // P, NKV // P
K_EFF = [min(n * 9 / 8, SEQ) for n in (NQ, NKV)]
ITERS = 50
UNROLL = 7
DT = 8
BT = SEQ // P
PROBLEMS = 2 * BATCH
ROUTES = ((0, QT_), (1, QT_), (2, KVT), (3, KVT))
RANKED = BATCH * (QT_ + KVT)
SLOT = lambda q, blk: q % BATCH * (QT_ + KVT) + (QT_ if q >= BATCH else 0) + blk
KEY_SCALE, KEY_LOW = 2.0 ** -38, 2.0 ** -63
KEY_HIGH = 2.0 ** -31 * (1 - 2.0 ** -24)
HOT, ROWS = 4, 8
DIGITS = 14


def route_block(nc, X, K, I, R):
    T = BT
    with ExitStack() as ctx:
        A = Alloc(nc, ctx, "ro")
        rt = A.sb("rt", [P, 2, D])
        prod = [A.sb(f"prod{k}", [P, DT, D]) for k in range(3)]
        s, d, ex = A.sb("s", [P, PROBLEMS, T]), A.sb("d", [P, PROBLEMS, T]), A.sb("ex", [P, PROBLEMS, T])
        part, na, m, mk, lnt = (A.sb(n, [P, PROBLEMS]) for n in ("part", "na", "m", "mk", "lnt"))
        top, diag = A.sb("top", [PROBLEMS, 1]), A.sb("diag", [PROBLEMS, PROBLEMS])
        logk, first = A.sb("logk", [P, PROBLEMS]), A.sb("first", [P, PROBLEMS])
        ones, before = A.sb("ones", [P, P]), A.sb("before", [P, P])
        kneg = A.sb("kneg", [P, PROBLEMS, 4])
        base = A.sb("base", [P, PROBLEMS, T])
        go_on = A.sb("go_on", [P, PROBLEMS, T])
        iota, ptok = A.sb("iota", [P, NKV]), A.sb("ptok", [P, 1])
        score, key = A.sb("score", [P, PROBLEMS, T]), A.sb("key", [P, PROBLEMS, T])
        digit = A.sb("digit", [P, 4], U32)
        cand, kept, cut = A.sb("cand", [P, PROBLEMS, 4]), A.sb("kept", [P, PROBLEMS, 4]), A.sb("cut", [P, PROBLEMS])
        less = A.sb("less", [P, PROBLEMS * 4, T])
        lt, eq, sel, incl, rank = (A.sb(n, [P, PROBLEMS, T]) for n in ("lt", "eq", "sel", "incl", "rank"))
        count = A.sb("count", [P, PROBLEMS * 4])
        vals = A.sb("vals", [P, PROBLEMS, T, 5], BF16)
        zeros = A.sb("zeros", [P, P], BF16)
        hot = [A.sb(f"hot{k}", [P, NKV], BF16) for k in range(HOT)]
        rows = A.sb("rows", [P, RANKED], U32)
        small, totals, tri, tot = (A.ps(n) for n in ("small", "totals", "tri", "tot"))
        acc = [A.ps(f"acc{k}") for k in range(KVT)]
        lists = (acc[0:QT_], acc[QT_:2 * QT_], (totals, tri, tot, small), acc)
        H = R["heavy"]
        loads = heavy_loads(I, H)
        S = {n: A.sem(n) for n in ("loaded", "zeroed", "heavy_in", "weighed", "summed_up", "spilled", "made", "dve", "maxed", "max_turned", "max_diag", "max_spread", "shifted", "exped",
                                   "summed", "totalled", "logged", "low", "scored", "counted", "tallied", "flagged", "placed", "ties",
                                   "chosen", "vals_full", "hot_full", "hot_used", "listed", "rows_full", "gathered")}
        xd = R["xd"]
        block = ctx.enter_context(nc.Block())

        @block.sync
        def _(sp):
            for r, n in enumerate(("rt_q", "rt_kv")):
                sp.dma_start(rt[:, r, :], I["L1_ffn_" + n].to_broadcast([P, D])).then_inc(S["loaded"], 16)
            sp.dma_start(xd.rearrange("(t p) d -> p t d", p=P), X[:, :, :]).then_inc(S["spilled"], 16)
            sp.dma_start(R["out"][BATCH * NQ:, :], I["L1_ffn_null_q"].unsqueeze(0)).then_inc(S["spilled"], 16)
            sp.wait_ge(S["zeroed"], 2)
            with nc.allow_non_contiguous_dma(reason="vectors onto partitions, once"):
                for dst, src in loads:
                    sp.dma_start(dst, src).then_inc(S["heavy_in"], 16)
            sp.wait_ge(S["loaded"], 32)
            sp.wait_ge(S["spilled"], 32)
            sp.wait_ge(S["heavy_in"], 16 * len(loads))

        made_steps = []

        @block.gpsimd
        def _(pool):
            g = nc.gpsimd
            g.memset(H["nkey"][:, :, :], 0.0).then_inc(S["zeroed"], 1)
            g.memset(H["nval"][:, :], 0.0).then_inc(S["zeroed"], 1)
            pool.wait_ge(S["loaded"], 32)
            for i in range(TILES // DT):
                if i >= 2:
                    pool.wait_ge(S["summed_up"], i - 1)
                g.tensor_tensor(out=prod[1 + i % 2][:, :, :], in0=X[:, i * DT:(i + 1) * DT, :], in1=each(rt[:, 1, :], DT),
                                op=ALU.mult).then_inc(S["weighed"], 1)
            made = Steps(pool, S["made"])
            made.then(g.memset(ones[:, :], 1.0))
            made.then(g.memset(zeros[:, :], 0.0))
            made.chain(g.memset(before[:, :], 1.0))
            made.chain(g.affine_select(out=before[:, :], in_=before[:, :], compare_op=ALU.is_gt, fill=0.0, base=0,
                                       pattern=[[1, P]], channel_multiplier=-1))
            for r in range(2):
                half = slice(r * BATCH, (r + 1) * BATCH)
                made.then(g.memset(kneg[:, half, :], -(NQ, NKV)[r] / P))
                made.then(g.memset(logk[:, half], math.log(K_EFF[r])))
                made.then(g.memset(first[:, half], math.log(SEQ / K_EFF[r])))
            for b in range(BATCH):
                made.then(g.memset(base[:, b, :], float(b * NQ - BATCH * NQ)))
            made.chain(g.memset(go_on[:, :, :], 1.0))
            made.chain(g.memset(go_on[:, :, 0:1], 0.0))
            for c in range(4):
                made.then(g.memset(digit[:, c:c + 1], c << 2 * (DIGITS - 1)))
            made.chain(g.iota(iota[:, :], pattern=[[1, NKV]], base=0, channel_multiplier=0, allow_small_or_imprecise_dtypes=True))
            made.chain(g.iota(ptok[:, :], pattern=[[0, 1]], base=0, channel_multiplier=1, allow_small_or_imprecise_dtypes=True))
            for q in range(PROBLEMS):
                made.chain(g.tensor_copy(vals[:, q, :, 3], ptok[:, :].to_broadcast([P, T])))
                made.chain(g.iota(vals[:, q, :, 4], pattern=[[P, T]], base=q % BATCH * SEQ, channel_multiplier=0,
                                  allow_small_or_imprecise_dtypes=True))
            made_steps.append(made.n)
            pool.wait_ge(S["spilled"], 32)
            for q, blocks in ROUTES:
                for blk in range(blocks):
                    n = SLOT(q, blk)
                    pool.wait_ge(S["rows_full"], q + 1)
                    g.indirect_dma_start(out=R["x"][:, n, :], out_offset=None, in_=xd,
                                         in_offset=bass.IndirectOffsetOnAxis(ap=rows[:, n:n + 1], axis=0)).then_inc(S["gathered"], 16)
            pool.wait_ge(S["gathered"], 16 * RANKED)

        @block.tensor
        def _(pe):
            t = nc.tensor
            pe.wait_ge(S["made"], made_steps[0])
            pe.wait_ge(S["maxed"], 1)
            t.transpose(small[0:PROBLEMS, 0:P], part[:, :], K["ident"][:, :]).then_inc(S["max_turned"], 1)
            pe.wait_ge(S["max_diag"], 1)
            t.matmul(small[:, 0:PROBLEMS], ones[0:PROBLEMS, :], diag[:, :], start=True, stop=True).then_inc(S["max_spread"], 1)
            with pe.Fori(0, (ITERS - 1) // UNROLL) as i7:
                for u in range(UNROLL):
                    pe.wait_ge(S["summed"], i7 * UNROLL + u + 1)
                    t.matmul(totals[:, 0:PROBLEMS], ones[:, :], part[:, :], start=True, stop=True).then_inc(S["totalled"], 1)
            flat = lambda a: a[:, :, :].rearrange("p q t -> p (q t)")
            with pe.Fori(0, DIGITS // UNROLL) as i7:
                for u in range(UNROLL):
                    pe.wait_ge(S["counted"], i7 * UNROLL + u + 1)
                    t.matmul(small[:, 0:4 * PROBLEMS], ones[:, :], count[:, :], start=True, stop=False)
                    t.matmul(small[:, 0:4 * PROBLEMS], ones[:, :], flat(kneg), start=False, stop=True).then_inc(S["tallied"], 1)
            pe.wait_ge(S["flagged"], 1)
            t.matmul(small[:, 0:PROBLEMS], ones[:, :], part[:, :], start=True, stop=False)
            t.matmul(small[:, 0:PROBLEMS], ones[:, :], kneg[:, :, 0], start=False, stop=True)
            for k, flags in ((1, eq), (2, sel)):
                pe.wait_ge(S["flagged"], k)
                t.matmul(tri[:, 0:PROBLEMS * T], before[:, :], flat(flags), start=True, stop=True)
                t.matmul(tot[:, 0:PROBLEMS * T], ones[:, :], flat(flags), start=True, stop=True).then_inc(S["placed"], 1)
            pe.wait_ge(S["vals_full"], 1)
            for q, blocks in ROUTES:
                if q == PROBLEMS - 1:
                    pe.wait_ge(S["rows_full"], 2)
                for blk in range(blocks):
                    t.matmul(lists[q][blk][:, 0:5], zeros[:, :], vals[:, q, 0, :], start=True, stop=False)
                if q == 0:
                    ins = t.matmul(acc[KVT - 1][:, 0:5], zeros[:, :], vals[:, 0, 0, :], start=True, stop=True)
                    ins.then_inc(S["hot_used"], HOT)
                with pe.Fori(0, T // ROWS) as t8:
                    for t_ in range(ROWS):
                        k = t_ % HOT
                        pe.wait_ge(S["hot_full"], q * T + t8 * ROWS + t_ + 1)
                        for blk in range(blocks):
                            ins = t.matmul(lists[q][blk][:, 0:5], hot[k][:, blk * P:(blk + 1) * P],
                                           vals[:, q, bass.ds(t8 * ROWS + t_, 1), :].rearrange("p a c -> p (a c)"), start=False, stop=False)
                        ins.then_inc(S["hot_used"], 1)
                for blk in range(blocks):
                    ins = t.matmul(lists[q][blk][:, 0:5], zeros[:, :], vals[:, q, 0, :], start=False, stop=True)
                ins.then_inc(S["listed"], 1)

        @block.scalar
        def _(act):
            a_ = nc.scalar
            a_.preload_act_table_set("natural_log_exp_and_others")
            tiles = s[:, :, :].rearrange("p (r b) t -> p r (b t)", r=2)
            with act.Fori(0, TILES // DT // 2) as i2:
                for k in range(2):
                    i = i2 * 2 + k
                    act.wait_ge(S["weighed"], i + 1)
                    for j in range(DT):
                        ins = a_.activation(prod[1 + k][:, j, :], prod[1 + k][:, j, :], ACT.Copy, accum_out=tiles[:, 1, bass.ds(i * DT + j, 1)])
                    ins.then_inc(S["summed_up"], 1)
            with act.Fori(0, (ITERS - 1) // UNROLL) as i7:
                for u in range(UNROLL):
                    i = i7 * UNROLL + u
                    act.wait_ge(S["shifted"], i + 1)
                    a_.activation(ex[:, :, :], d[:, :, :], ACT.Exp).then_inc(S["exped"], 1)
                    act.wait_ge(S["totalled"], i + 1)
                    a_.activation(lnt[:, :], totals[:, 0:PROBLEMS], ACT.Ln).then_inc(S["logged"], 1)
            act.wait_ge(S["low"], 1)
            a_.activation(score[:, :, :], d[:, :, :], ACT.Exp).then_inc(S["scored"], 1)

        @block.vector
        def _(dve):
            v = nc.vector
            tt = v.tensor_tensor
            wide = lambda a: over(a[:, :], T)
            flat = lambda a: a[:, :, :].rearrange("p q t -> p (q t)")
            dve.wait_ge(S["loaded"], 32)
            tiles = s[:, :, :].rearrange("p (r b) t -> p r (b t)", r=2)
            with dve.Fori(0, TILES // DT) as i:
                st = Steps(dve, S["dve"], 2, i)
                xg = X[:, bass.ds(i * DT, DT), :]
                st.chain(tt(out=prod[0][:, :, :], in0=xg, in1=each(rt[:, 0, :], DT), op=ALU.mult))
                st.chain(v.tensor_reduce(tiles[:, 0, bass.ds(i * DT, DT)], prod[0][:, :, :], AXX, ALU.add))
                st.close()
            dve.wait_ge(S["summed_up"], TILES // DT)
            dve.wait_ge(S["made"], made_steps[0])
            v.tensor_reduce(part[:, :], s[:, :, :], AXX, ALU.max).then_inc(S["maxed"], 1)
            dve.wait_ge(S["max_turned"], 1)
            st = Steps(dve, S["dve"], 0, 0)
            st.base = 2 * (TILES // DT)
            st.chain(v.tensor_reduce(top[:, :], small[0:PROBLEMS, 0:P], AXX, ALU.max))
            v.tensor_scalar(diag[:, :], K["ident"][0:PROBLEMS, 0:PROBLEMS], top[:, 0:1], None, ALU.mult).then_inc(S["max_diag"], 1)
            dve.wait_ge(S["max_spread"], 1)
            st.then(tt(out=s[:, :, :], in0=s[:, :, :], in1=over(small[:, 0:PROBLEMS], T), op=ALU.subtract))
            st.chain(tt(out=na[:, :], in0=first[:, :], in1=small[:, 0:PROBLEMS], op=ALU.subtract))
            start = st.base + st.n
            with dve.Fori(0, (ITERS - 1) // UNROLL) as i7:
                for u in range(UNROLL):
                    i = i7 * UNROLL + u
                    st = Steps(dve, S["dve"], 4, i)
                    st.base = start + i * 4
                    st.then(tt(out=d[:, :, :], in0=s[:, :, :], in1=wide(na), op=ALU.min))
                    st.chain(v.tensor_scalar(m[:, :], na[:, :], 0.0, None, ALU.min))
                    tt(out=d[:, :, :], in0=d[:, :, :], in1=wide(m), op=ALU.subtract).then_inc(S["shifted"], 1)
                    st.then(tt(out=mk[:, :], in0=m[:, :], in1=logk[:, :], op=ALU.subtract))
                    dve.wait_ge(S["exped"], i + 1)
                    v.tensor_reduce(part[:, :], ex[:, :, :], AXX, ALU.add).then_inc(S["summed"], 1)
                    st.wait()
                    dve.wait_ge(S["logged"], i + 1)
                    st.chain(tt(out=na[:, :], in0=lnt[:, :], in1=mk[:, :], op=ALU.add))
                    st.close()
            st = Steps(dve, S["dve"])
            st.base = start + 4 * (ITERS - 1)
            st.chain(tt(out=s[:, :, :], in0=s[:, :, :], in1=wide(na), op=ALU.subtract))
            v.tensor_scalar(d[:, :, :], s[:, :, :], 0.0, None, ALU.min).then_inc(S["low"], 1)
            st.chain(v.tensor_scalar(key[:, :, :], s[:, :, :], -KEY_SCALE, KEY_LOW, ALU.mult, ALU.max))
            st.chain(v.tensor_scalar(key[:, :, :], key[:, :, :], KEY_HIGH, None, ALU.min))
            st.chain(v.memset(cut[:, :], KEY_LOW))
            start = st.base + st.n
            with dve.Fori(0, DIGITS // UNROLL) as i7:
                for u in range(UNROLL):
                    i = i7 * UNROLL + u
                    st = Steps(dve, S["dve"], 5)
                    st.base = start + i * 5
                    st.chain(tt(out=cand[:, :, :].bitcast(U32), in0=over(cut[:, :].bitcast(U32), 4), in1=each(digit[:, :], PROBLEMS),
                                op=ALU.bitwise_or))
                    for c in range(4):
                        ins = tt(out=less[:, c * PROBLEMS:(c + 1) * PROBLEMS, :], in0=key[:, :, :], in1=over(cand[:, :, c], T), op=ALU.is_lt)
                    st.chain(ins)
                    v.tensor_reduce(count[:, :].rearrange("p (q c) -> p c q", c=4), less[:, :, :].rearrange("p (c q) t -> p c q t", c=4),
                                    AXX, ALU.add).then_inc(S["counted"], 1)
                    st.then(v.tensor_scalar(digit[:, :], digit[:, :], 2, None, ALU.logical_shift_right))
                    dve.wait_ge(S["tallied"], i + 1)
                    st.chain(v.scalar_tensor_tensor(out=kept[:, :, :], in0=small[:, 0:4 * PROBLEMS].rearrange("p (q c) -> p q c", c=4),
                                                    scalar=0.0, in1=cand[:, :, :], op0=ALU.is_lt, op1=ALU.mult))
                    st.chain(v.tensor_reduce(cut[:, :], kept[:, :, :], AXX, ALU.max))
                    st.close()
            st = Steps(dve, S["dve"])
            st.base = start + 5 * DIGITS
            st.chain(tt(out=lt[:, :, :], in0=key[:, :, :], in1=wide(cut), op=ALU.is_lt))
            st.chain(v.tensor_reduce(part[:, :], lt[:, :, :], AXX, ALU.add))
            tt(out=eq[:, :, :], in0=key[:, :, :], in1=wide(cut), op=ALU.is_equal).then_inc(S["flagged"], 1)

            def places():
                st.chain(v.tensor_tensor_scan(flat(incl), flat(go_on), tot[:, 0:PROBLEMS * T], 0.0, ALU.mult, ALU.add))
                st.chain(tt(out=flat(rank), in0=flat(incl), in1=tot[:, 0:PROBLEMS * T], op=ALU.subtract))
                st.chain(tt(out=flat(rank), in0=flat(rank), in1=tri[:, 0:PROBLEMS * T], op=ALU.add))

            dve.wait_ge(S["placed"], 1)
            places()
            st.chain(tt(out=rank[:, :, :], in0=rank[:, :, :], in1=over(small[:, 0:PROBLEMS], T), op=ALU.add))
            st.chain(v.scalar_tensor_tensor(out=sel[:, :, :], in0=rank[:, :, :], scalar=0.0, in1=eq[:, :, :], op0=ALU.is_lt, op1=ALU.mult))
            tt(out=sel[:, :, :], in0=sel[:, :, :], in1=lt[:, :, :], op=ALU.add).then_inc(S["flagged"], 1)
            dve.wait_ge(S["scored"], 1)
            st.chain(v.tensor_scalar(d[:, :, :], score[:, :, :], -1.0, 1.0, ALU.mult, ALU.add))
            st.chain(tt(out=d[:, :, :], in0=d[:, :, :], in1=score[:, :, :], op=ALU.add))
            for k in range(3):
                ins = v.tensor_copy(vals[:, :, :, k], d[:, :, :])
                if k < 2:
                    st.chain(ins)
                    st.chain(tt(out=d[:, :, :], in0=d[:, :, :], in1=vals[:, :, :, k], op=ALU.subtract))
            ins.then_inc(S["vals_full"], 1)
            dve.wait_ge(S["flagged"], 2)
            dve.wait_ge(S["placed"], 2)
            places()
            nq = slice(0, BATCH)
            st.chain(tt(out=incl[:, nq, :], in0=rank[:, nq, :], in1=base[:, nq, :], op=ALU.add))
            st.chain(tt(out=incl[:, nq, :], in0=incl[:, nq, :], in1=sel[:, nq, :], op=ALU.mult))
            st.then(v.tensor_scalar(R["pick"][:, :], incl[:, nq, :].rearrange("p b t -> p (b t)"), float(BATCH * NQ), None, ALU.add))
            st.chain(v.scalar_tensor_tensor(out=rank[:, :, :], in0=rank[:, :, :], scalar=1.0, in1=sel[:, :, :], op0=ALU.add, op1=ALU.mult))
            st.chain(v.tensor_scalar(rank[:, :, :], rank[:, :, :], -1.0, None, ALU.add))

            def listed(q, blocks):
                dve.wait_ge(S["listed"], q + 1)
                for blk in range(blocks):
                    n = SLOT(q, blk)
                    st.then(v.tensor_reduce(R["score"][:, n:n + 1], lists[q][blk][:, 0:3], AXX, ALU.add))
                    with nc.allow_low_precision(reason="whole numbers"):
                        ins = v.tensor_reduce(rows[:, n:n + 1], lists[q][blk][:, 3:5], AXX, ALU.add)
                ins.then_inc(S["rows_full"], 1)

            for q, blocks in ROUTES:
                with dve.Fori(0, T // ROWS) as t8:
                    for t_ in range(ROWS):
                        k = t_ % HOT
                        n = q * T + t8 * ROWS + t_
                        dve.wait_ge(S["hot_used"], n + 1)
                        v.tensor_scalar(hot[k][:, 0:blocks * P], iota[:, 0:blocks * P], rank[:, q, bass.ds(t8 * ROWS + t_, 1)], None,
                                        ALU.is_equal).then_inc(S["hot_full"], 1)
                if q:
                    listed(*ROUTES[q - 1])
            listed(*ROUTES[-1])


def heavy_loads(I, H):
    w = lambda n: I["L1_ffn_" + n]
    w_kv = w("w_kv_h").rearrange("(h p) e c -> p h e c", p=P)
    heads_of = lambda a: a[:, :, :].rearrange("p h (e c) -> p h e c", c=DHD)
    loads = [(H["wq"][:, :, :], w("w_q_h").rearrange("(h p) e -> p h e", p=P))]
    loads += [(heads_of(H["wk"])[:, hh], w_kv[:, hh, :, 0:DHD]) for hh in range(DH)]
    loads += [(heads_of(H["wv"])[:, hh], w_kv[:, hh, :, DHD:]) for hh in range(DH)]
    loads += [(H["wo"][:, :, :], w("w_out_h").rearrange("(h p) e -> p h e", p=P)),
              (H["gain"][:, :], w("rms_g").rearrange("(h p) -> p h", p=P))]
    loads += [(H["nkey"][DHD * a:DHD * (a + 1), :, a], w("null_kv")[0].rearrange("(m a) d -> a d m", a=2)[a]) for a in range(2)]
    loads += [(H["nval"][h:h + 1, h * DHD:(h + 1) * DHD], w("null_kv")[1, h:h + 1, :]) for h in range(LH)]
    return loads


def heavy_block(nc, X, K, I, R):
    RT = QT_ + KVT
    with ExitStack() as ctx:
        A = Alloc(nc, ctx, "he")
        wq, wk, wv, wo, gain, nkey, nval = (R["heavy"][n] for n in ("wq", "wk", "wv", "wo", "gain", "nkey", "nval"))
        expand = A.sb("expand", [LH, HT, P])
        stat, mv, rstd = A.sb("stat", [P, RT, 6]), A.sb("mv", [P, RT, 2]), A.sb("rstd", [P, RT])
        half = A.sb("half", [P, RT])
        xs = A.sb("xs", [P, RT, D])
        qT, kvT = A.sb("qT", [P, DH, NQ]), A.sb("kvT", [P, DH, NKV])
        Q, KK, V = A.sb("Q", [P, HT, NQ]), A.sb("K", [P, HT, NKV]), A.sb("V", [P, KVT, HW])
        prob = [A.sb(f"prob{k}", [P, NKV]) for k in range(3)]
        probT = [A.sb(f"probT{k}", [P, KVT, P]) for k in range(2)]
        nsim, nmax, sums, nprob, inv = (A.sb(n, [P, LH]) for n in ("nsim", "nmax", "sums", "nprob", "inv"))
        nprobT, invT = A.sb("nprobT", [LH, P]), A.sb("invT", [LH, P])
        invs, mixed = A.sb("invs", [P, HT, P]), A.sb("mixed", [P, HT, P])
        y = [A.sb(f"y{k}", [P, D]) for k in range(QT_)]
        bank = [A.ps(f"bank{k}") for k in range(8)]
        score, turned, outT, nullT, small = bank[0:3], bank[3:5], bank[5], bank[6], bank[7]
        S = {n: A.sem(n) for n in (
            "made", "dve", "var", "rstd_done", "xs_full", "turned", "xT_full", "q_done", "q_out", "k_done", "k_out", "v_done",
            "v_out", "null_scored", "null_out", "scored", "maxed", "exped", "prob_turned", "probT_full", "outT_done", "null_shift",
            "null_exped", "inv_done", "nprobT_full", "inv_turned", "invT_full", "null_mixed", "invs_used", "spread", "invs_full",
            "mixed_full", "out_done", "y_full", "stored")}
        block = ctx.enter_context(nc.Block())
        made_steps = []

        @block.sync
        def _(sp):
            with sp.Fori(0, BATCH) as b:
                for k in range(QT_):
                    sp.wait_ge(S["y_full"], b * QT_ + k + 1)
                    sp.dma_start(R["out"][bass.ds(b * NQ + k * P, P), :], y[k][:, :]).then_inc(S["stored"], 16)
            sp.wait_ge(S["stored"], 16 * BATCH * QT_)

        @block.gpsimd
        def _(pool):
            g = nc.gpsimd
            made = Steps(pool, S["made"])
            made.chain(g.memset(half[:, :], -0.5))
            made.chain(g.memset(expand[:, :, :], 1.0))
            flat = expand[:, :, :].rearrange("h m p -> h (m p)")
            made.chain(g.affine_select(out=flat, in_=flat, compare_op=ALU.is_ge, fill=0.0, base=0,
                                       pattern=[[1, HW]], channel_multiplier=-DHD))
            made.chain(g.affine_select(out=flat, in_=flat, compare_op=ALU.is_ge, fill=0.0, base=DHD - 1,
                                       pattern=[[-1, HW]], channel_multiplier=DHD))
            made_steps.append(made.n)
            with pool.Fori(0, BATCH) as b:
                pool.wait_ge(S["var"], b + 1)
                g.tensor_tensor(out=rstd[:, :], in0=mv[:, :, 1], in1=half[:, :], op=ALU.pow).then_inc(S["rstd_done"], 1)

        @block.tensor
        def _(pe):
            t = nc.tensor
            pe.wait_ge(S["made"], made_steps[0])
            with pe.Fori(0, BATCH) as b:
                pe.wait_ge(S["xs_full"], b + 1)
                for hh in range(DH):
                    for j in range(QT_):
                        t.transpose(bank[2][:, hh * NQ + j * P:hh * NQ + (j + 1) * P], xs[:, j, hh * P:(hh + 1) * P], K["ident"][:, :])
                    for j in range(KVT):
                        ins = t.transpose(bank[hh][:, j * P:(j + 1) * P], xs[:, QT_ + j, hh * P:(hh + 1) * P], K["ident"][:, :])
                    ins.then_inc(S["turned"], 1)
                pe.wait_ge(S["xT_full"], 2 * DH * (b + 1))
                for m in range(HT):
                    for hh in range(DH):
                        ins = t.matmul(bank[3 + m // 2][:, m % 2 * NQ:(m % 2 + 1) * NQ], wq[:, hh, m * P:(m + 1) * P], qT[:, hh, :],
                                       start=(hh == 0), stop=(hh == DH - 1))
                    if m % 2:
                        ins.then_inc(S["q_done"], 1)
                for m in range(HT):
                    if m >= 2:
                        pe.wait_ge(S["k_out"], HT * b + m - 1)
                    for hh in range(DH):
                        ins = t.matmul(bank[5 + m % 2][:, :], wk[:, hh, m * P:(m + 1) * P], kvT[:, hh, :], start=(hh == 0), stop=(hh == DH - 1))
                    ins.then_inc(S["k_done"], 1)
                for j in range(KVT):
                    if j >= 2:
                        pe.wait_ge(S["v_out"], KVT * b + j - 1)
                    for hh in range(DH):
                        ins = t.matmul(bank[j % 2][:, :], kvT[:, hh, j * P:(j + 1) * P], wv[:, hh, :], start=(hh == 0), stop=(hh == DH - 1))
                    ins.then_inc(S["v_done"], 1)
                pe.wait_ge(S["q_out"], QT_ * (b + 1))
                pe.wait_ge(S["k_out"], HT * (b + 1))
                pe.wait_ge(S["v_out"], KVT * (b + 1))
                for k in range(QT_):
                    c = b * QT_ + k
                    tokens = slice(k * P, (k + 1) * P)

                    def scores(h, ahead=0):
                        tokens = slice((k + ahead) * P, (k + ahead + 1) * P)
                        if h >= 3:
                            pe.wait_ge(S["exped"], c * LH + h - 2)
                        m, base = h // 2, h % 2 * DHD
                        t.matmul(score[h % 3][:, :], Q[base:base + DHD, m, tokens], KK[base:base + DHD, m, :], start=True, stop=True,
                                 tile_position=(base, 0)).then_inc(S["scored"], 1)

                    def turns(h):
                        pe.wait_ge(S["exped"], c * LH + h + 1)
                        if h >= 2:
                            pe.wait_ge(S["probT_full"], c * LH + h - 1)
                        for kt in range(KVT):
                            ins = t.transpose(turned[h % 2][:, kt * P:(kt + 1) * P], prob[h % 3][:, kt * P:(kt + 1) * P], K["ident"][:, :])
                        ins.then_inc(S["prob_turned"], 1)

                    def mixes(h):
                        pe.wait_ge(S["probT_full"], c * LH + h + 1)
                        m, base = h // 2, h % 2 * DHD
                        for kt in range(KVT):
                            ins = t.matmul(outT[base:base + DHD, m * P:(m + 1) * P], V[:, kt, h * DHD:(h + 1) * DHD], probT[h % 2][:, kt, :],
                                           start=(kt == 0), stop=(kt == KVT - 1), tile_position=(0, base))
                        ins.then_inc(S["outT_done"], 1)

                    if k == 0:
                        scores(0)
                        scores(1)
                    else:
                        pe.wait_ge(S["y_full"], c)
                    for m in range(HT):
                        ins = t.matmul(small[:, 2 * m:2 * m + 2], Q[:, m, tokens], nkey[:, m, :], start=True, stop=True)
                    ins.then_inc(S["null_scored"], 1)
                    for h in range(LH):
                        if h + 2 < LH:
                            scores(h + 2)
                        turns(h)
                        if h >= 1:
                            mixes(h - 1)
                    pe.wait_ge(S["null_exped"], c + 1)
                    t.transpose(small[0:LH, 0:P], nprob[:, :], K["ident"][:, :])
                    pe.wait_ge(S["inv_done"], c + 1)
                    t.transpose(small[0:LH, P:2 * P], inv[:, :], K["ident"][:, :]).then_inc(S["inv_turned"], 1)
                    mixes(LH - 1)
                    pe.wait_ge(S["nprobT_full"], c + 1)
                    pe.wait_ge(S["invT_full"], c + 1)
                    for m in range(HT):
                        ins = t.matmul(small[:, m * P:(m + 1) * P], expand[:, m, :], invT[:, :], start=True, stop=True)
                    ins.then_inc(S["spread"], 1)
                    for m in range(HT):
                        ins = t.matmul(nullT[:, m * P:(m + 1) * P], nval[:, m * P:(m + 1) * P], nprobT[:, :], start=True, stop=True)
                    ins.then_inc(S["null_mixed"], 1)
                    if k + 1 < QT_:
                        scores(0, 1)
                        scores(1, 1)
                    pe.wait_ge(S["mixed_full"], c + 1)
                    for m in range(HT):
                        ins = t.matmul(small[:, 0:D], mixed[:, m, :], wo[:, m, :], start=(m == 0), stop=(m == HT - 1))
                    ins.then_inc(S["out_done"], 1)

        @block.scalar
        def _(act):
            a_ = nc.scalar
            with act.Fori(0, BATCH) as b:
                for hh in range(DH):
                    act.wait_ge(S["turned"], DH * b + hh + 1)
                    a_.activation(kvT[:, hh, :], bank[hh][:, :], ACT.Copy, scale=gain[:, hh:hh + 1]).then_inc(S["xT_full"], 1)
                for hh in range(DH):
                    a_.activation(qT[:, hh, :], bank[2][:, hh * NQ:(hh + 1) * NQ], ACT.Copy, scale=gain[:, hh:hh + 1]).then_inc(S["xT_full"], 1)
                for n in range(2):
                    act.wait_ge(S["q_done"], 2 * b + n + 1)
                    a_.activation(Q[:, 2 * n:2 * n + 2, :], bank[3 + n][:, :].rearrange("p (m q) -> p m q", m=2), ACT.Copy,
                                  scale=DHD ** -0.5).then_inc(S["q_out"], 1)
                for m in range(HT):
                    act.wait_ge(S["k_done"], HT * b + m + 1)
                    a_.activation(KK[:, m, :], bank[5 + m % 2][:, :], ACT.Copy).then_inc(S["k_out"], 1)
                for k in range(QT_):
                    c = b * QT_ + k
                    for h in range(LH):
                        act.wait_ge(S["maxed"], c * LH + h + 1)
                        if h >= 3:
                            act.wait_ge(S["prob_turned"], c * LH + h - 2)
                        a_.activation(prob[h % 3][:, :], score[h % 3][:, :], ACT.Exp, bias=nmax[:, h:h + 1],
                                      accum_out=sums[:, h:h + 1]).then_inc(S["exped"], 1)
                    act.wait_ge(S["null_shift"], c + 1)
                    a_.activation(nprob[:, :], nprob[:, :], ACT.Exp).then_inc(S["null_exped"], 1)
                    act.wait_ge(S["inv_turned"], c + 1)
                    a_.activation(nprobT[:, :], small[0:LH, 0:P], ACT.Copy).then_inc(S["nprobT_full"], 1)
                    a_.activation(invT[:, :], small[0:LH, P:2 * P], ACT.Copy).then_inc(S["invT_full"], 1)
                    act.wait_ge(S["spread"], c + 1)
                    a_.activation(invs[:, :, :], small[:, :].rearrange("p (m q) -> p m q", q=P), ACT.Copy).then_inc(S["invs_full"], 1)

        @block.vector
        def _(dve):
            v = nc.vector
            with dve.Fori(0, BATCH) as b:
                st = Steps(dve, S["dve"], 2 * RT + 3 + QT_ * (LH + 2), b)
                row = lambda j: R["x"][:, bass.ds(b * RT + j, 1), :].rearrange("p a d -> p (a d)")
                statistics(st, v, row, stat, mv, rstd, RT)
                st.chain(v.tensor_tensor(out=mv[:, :, 0], in0=mv[:, :, 0], in1=mv[:, :, 0], op=ALU.mult))
                st.chain(v.tensor_tensor(out=mv[:, :, 0], in0=mv[:, :, 0], in1=mv[:, :, 1], op=ALU.add))
                v.tensor_scalar(mv[:, :, 1], mv[:, :, 0], 1e-24 / D, None, ALU.max).then_inc(S["var"], 1)
                dve.wait_ge(S["rstd_done"], b + 1)
                for j in range(RT):
                    ins = v.tensor_scalar(xs[:, j, :], row(j), rstd[:, j:j + 1], None, ALU.mult)
                ins.then_inc(S["xs_full"], 1)
                for j in range(KVT):
                    dve.wait_ge(S["v_done"], KVT * b + j + 1)
                    v.tensor_scalar(V[:, j, :], bank[j % 2][:, :], R["score"][:, bass.ds(b * RT + QT_ + j, 1)], None,
                                    ALU.mult).then_inc(S["v_out"], 1)
                for k in range(QT_):
                    c = b * QT_ + k
                    dve.wait_ge(S["null_scored"], c + 1)
                    v.tensor_scalar(nsim[:, :], small[:, 0:LH], -1.0, None, ALU.mult).then_inc(S["null_out"], 1)

                    def maxes(h):
                        dve.wait_ge(S["scored"], c * LH + h + 1)
                        st.chain(v.tensor_reduce(nmax[:, h:h + 1], score[h % 3][:, :], AXX, ALU.max, negate=True))
                        if h == 0:
                            dve.wait_ge(S["null_out"], c + 1)
                        v.tensor_tensor(out=nmax[:, h:h + 1], in0=nmax[:, h:h + 1], in1=nsim[:, h:h + 1], op=ALU.min).then_inc(S["maxed"], 1)

                    maxes(0)
                    maxes(1)
                    for h in range(LH):
                        if h + 2 < LH:
                            maxes(h + 2)
                        if h == LH - 2:
                            dve.wait_ge(S["maxed"], (c + 1) * LH)
                            v.tensor_tensor(out=nprob[:, :], in0=nmax[:, :], in1=nsim[:, :], op=ALU.subtract).then_inc(S["null_shift"], 1)
                        if h == LH - 1:
                            dve.wait_ge(S["null_exped"], c + 1)
                            st.chain(v.tensor_tensor(out=sums[:, :], in0=sums[:, :], in1=nprob[:, :], op=ALU.add))
                            v.reciprocal(inv[:, :], sums[:, :]).then_inc(S["inv_done"], 1)
                        dve.wait_ge(S["prob_turned"], c * LH + h + 1)
                        if h >= 2:
                            dve.wait_ge(S["outT_done"], c * LH + h - 1)
                        v.tensor_copy(probT[h % 2][:, :, :], turned[h % 2][:, :].rearrange("p (n q) -> p n q", q=P)).then_inc(S["probT_full"], 1)
                    dve.wait_ge(S["outT_done"], (c + 1) * LH)
                    dve.wait_ge(S["invs_full"], c + 1)
                    both = lambda a: a[:, :].rearrange("p (m q) -> p m q", q=P)
                    st.chain(v.tensor_tensor(out=mixed[:, :, :], in0=both(outT), in1=invs[:, :, :], op=ALU.mult))
                    dve.wait_ge(S["null_mixed"], c + 1)
                    v.tensor_tensor(out=invs[:, :, :], in0=both(nullT), in1=invs[:, :, :], op=ALU.mult).then_inc(S["invs_used"], 1)
                    dve.wait_ge(S["invs_used"], c + 1)
                    v.tensor_tensor(out=mixed[:, :, :], in0=mixed[:, :, :], in1=invs[:, :, :], op=ALU.add).then_inc(S["mixed_full"], 1)
                    dve.wait_ge(S["stored"], 16 * QT_ * b)
                    dve.wait_ge(S["out_done"], c + 1)
                    v.tensor_scalar(y[k][:, :], small[:, 0:D], R["score"][:, bass.ds(b * RT + k, 1)], None, ALU.mult).then_inc(S["y_full"], 1)
                st.close()


def routed_phase(nc, X, K, I, out):
    w = lambda n: I["L1_ffn_" + n]

    def valid(g, made, band):
        half = P // 2
        made.chain(g.memset(band[0:half, KEYS - half:], -BIG))
        made.chain(g.memset(band[half:P, 0:half], -BIG))

    with ExitStack() as ctx:
        R = {"xd": nc.dram_tensor("x_rows", (TOK, D), F32).ap(), "out": nc.dram_tensor("heavy_rows", (BATCH * NQ + 1, D), F32).ap(),
             "pick": ctx.enter_context(nc.sbuf_tensor("pick", [P, TILES], U32))}
        with ExitStack() as inner:
            R["x"] = inner.enter_context(nc.sbuf_tensor("routed_x", [P, RANKED, D], F32))
            R["score"] = inner.enter_context(nc.sbuf_tensor("routed_score", [P, RANKED], F32))
            shapes = {"wq": [P, DH, HW], "wk": [P, DH, HW], "wv": [P, DH, HW], "wo": [P, HT, D], "gain": [P, DH],
                      "nkey": [P, HT, 2], "nval": [LH, HW]}
            R["heavy"] = {n: inner.enter_context(nc.sbuf_tensor("heavy_" + n, shape, F32)) for n, shape in shapes.items()}
            route_block(nc, X, K, I, R)
            heavy_block(nc, X, K, I, R)
        qkv = w("w_qkv_l")
        W = {"q": qkv[:, 0:HW], "k": qkv[:, HW:2 * HW], "v": qkv[:, 2 * HW:], "o": w("w_out_l")}
        banded_phase(nc, X, K, "li", W, heads=LH, scale=DHD ** -0.5, shift=P // 2, valid=valid, norm=(w("ln_g"), w("ln_b")),
                     add=(R["out"], R["pick"]), out=out)


def lay_out(inputs, np):
    a = {k: np.asarray(v) for k, v in inputs.items()}
    for name in ("L0_attn_in_proj_w", "L0_attn_x_proj_w", "L0_attn_dt_proj_w", "L0_attn_out_proj_w", "L0_attn_fc1_w",
                 "L0_attn_fc2_w", "L0_attn_fc3_w", "L1_attn_Wq", "L1_attn_Wk", "L1_attn_Wv", "L1_attn_Wo"):
        a[name] = a[name].T
    a["L0_attn_x_proj_w"] = np.concatenate([a["L0_attn_x_proj_w"][:, RANK:], a["L0_attn_x_proj_w"][:, :RANK]], axis=1)
    return a


def program(nc, A, out):
    with ExitStack() as ctx:
        X = ctx.enter_context(nc.sbuf_tensor("X", [P, TILES, D], F32))
        K = {"ident": ctx.enter_context(nc.sbuf_tensor("ident", [P, P], F32)),
             "neghalf": ctx.enter_context(nc.sbuf_tensor("neghalf", [P, GT], F32))}
        with nc.sbuf_tensor("sel", [96, 32], BF16) as K["sel"]:
            constants_phase(nc, K)
            mamba_phase(nc, X, K, A)
            moe_phase(nc, X, K, *(A["L0_ffn_" + n] for n in ("Wr", "Wg", "Wu", "Wd", "Sg", "Su", "Sd", "expert_bias")))
        sliding_phase(nc, X, K, A)
        routed_phase(nc, X, K, A, out)


def kernel(**inputs):
    import numpy as _np
    import concourse.bacc as _bacc
    from concourse import mybir as _mybir
    from concourse.bass_utils import run_bass_kernel_spmd as _run

    nc = _bacc.Bacc("TRN2", target_bir_lowering=False, num_devices=1)
    arrays, args = {}, {}
    for name, a in lay_out(inputs, _np).items():
        arrays[f"in_{name}_dram"] = _np.ascontiguousarray(a)
        args[name] = nc.dram_tensor(f"in_{name}_dram", a.shape, _mybir.dt.from_np(a.dtype), kind="ExternalInput").ap()
    out = nc.dram_tensor("out_0_dram", (BATCH, SEQ, D), F32, kind="ExternalOutput").ap()
    program(nc, args, out)
    r = _run(nc, [arrays], core_ids=[0])
    return r.results[0]["out_0_dram"]
```
